# Optimizing a Trainium2 kernel written in Bass

```python
import numpy as np
import jax
import jax.numpy as jnp

def _softmax(x, axis=-1):
    return jax.nn.softmax(x, axis=axis)

def _gelu(x):
    return jax.nn.gelu(x, approximate=True)

def _silu(x):
    return jax.nn.silu(x)

def _sigmoid(x):
    return jax.nn.sigmoid(x)

def _layernorm(x, axis=-1, eps=1e-05):
    m = jnp.mean(x, axis=axis, keepdims=True)
    v = jnp.var(x, axis=axis, keepdims=True)
    return (x - m) / jnp.sqrt(v + eps)

def _scatter_add(tgt, idx, src, axis=0):
    return tgt.at[idx].add(src)

def _segment_sum(src, seg, n):
    return jax.ops.segment_sum(src, seg, n)
kernel_name = 'mk_cond_seq_d2_seqx_r2_47a4c6'

def setup_inputs(seed: int=0):
    np.random.seed(seed)
    _w = jnp.asarray

    def _rec_inputs():
        import jax
        import jax.numpy as jnp
        _rk = jax.random.key(seed)
        x = -0.0003929 + 0.9999 * jax.random.normal(jax.random.fold_in(_rk, 1), (8, 512, 512), jnp.float32)
        _lenS = 512 - jax.random.randint(jax.random.fold_in(_rk, 7), (8,), 0, max(1, 512 // 4) + 1, jnp.int32)
        _lenS2 = 512 - jax.random.randint(jax.random.fold_in(_rk, 8), (8,), 0, max(1, 512 // 4) + 1, jnp.int32)
        cond_2048 = 0.00782532 + 1.00527 * jax.random.normal(jax.random.fold_in(_rk, 11), (8, 1024), jnp.float32)
        _validS = jnp.arange(512)[None, :] < _lenS[:, None]
        _validS2 = jnp.arange(512)[None, :] < _lenS2[:, None]
        _causal = jnp.tril(jnp.ones((512, 512), dtype=bool))
        mask_BxS_ik0 = jnp.where(jnp.broadcast_to(_validS[:, :], (8, 512)), 0, 1).astype(jnp.int32)
        return (x, cond_2048, mask_BxS_ik0)
    x, cond_2048, mask_BxS_ik0 = _rec_inputs()

    def _L0_cond_setup():
        import jax, jax.numpy as jnp
        import numpy as np
        H = 16
        LN_EPS = 1e-05

        def _layernorm(x, scale, bias):
            mu = jnp.mean(x, axis=-1, keepdims=True)
            var = jnp.var(x, axis=-1, keepdims=True)
            return (x - mu) * jax.lax.rsqrt(var + LN_EPS) * scale + bias
        key = jax.random.key(seed)
        ks = jax.random.split(key, 8)
        B, T, D, E = (4, 2048, 512, 1024)
        s = 0.02
        return {'x': jax.random.normal(ks[0], (B, T, D), jnp.float32), 'emb': jax.random.normal(ks[1], (B, E), jnp.float32), 'src_mask': jax.random.randint(ks[2], (B, T), 0, 2).astype(jnp.int32), 'norm_scale': jnp.ones((D,), jnp.float32), 'norm_bias': jnp.zeros((D,), jnp.float32), 'Wq': jax.random.normal(ks[3], (D, D), jnp.float32) * s, 'bq': jnp.zeros((D,), jnp.float32), 'Wk': jax.random.normal(ks[4], (D, D), jnp.float32) * s, 'bk': jnp.zeros((D,), jnp.float32), 'Wv': jax.random.normal(ks[5], (D, D), jnp.float32) * s, 'bv': jnp.zeros((D,), jnp.float32), 'film_emb_W': jax.random.normal(ks[6], (E, 2 * D), jnp.float32) * s, 'film_emb_b': jnp.zeros((2 * D,), jnp.float32), 'film_norm_scale': jnp.ones((D,), jnp.float32), 'film_norm_bias': jnp.zeros((D,), jnp.float32), 'film_out_W': jax.random.normal(ks[7], (D, D), jnp.float32) * s, 'film_out_b': jnp.zeros((D,), jnp.float32)}
    _L0_cond_all = _L0_cond_setup()
    _L0_cond_in = {k: v for k, v in _L0_cond_all.items() if k in ('norm_scale', 'norm_bias', 'Wq', 'bq', 'Wk', 'bk', 'Wv', 'bv', 'film_emb_W', 'film_emb_b', 'film_norm_scale', 'film_norm_bias', 'film_out_W', 'film_out_b')}
    del _L0_cond_all

    def _L1_cond_setup():
        import jax, jax.numpy as jnp
        import numpy as np
        D = 512
        H = 8
        DI = 1024
        DT_RANK = 64
        N = 16
        K = 4
        EPS = 1e-05

        def _ln(x, g, b):
            mu = jnp.mean(x, axis=-1, keepdims=True)
            var = jnp.mean(jnp.square(x - mu), axis=-1, keepdims=True)
            return (x - mu) * jax.lax.rsqrt(var + EPS) * g + b

        def _attention(xm, Wqkv, bqkv, Wproj, bproj):
            b, s, d = xm.shape
            hd = d // H
            qkv = (xm @ Wqkv + bqkv).reshape(b, s, 3, H, hd)
            q = jnp.transpose(qkv[:, :, 0], (0, 2, 1, 3))
            k = jnp.transpose(qkv[:, :, 1], (0, 2, 1, 3))
            v = jnp.transpose(qkv[:, :, 2], (0, 2, 1, 3))
            att = jax.nn.softmax(jnp.einsum('bhqd,bhkd->bhqk', q * hd ** (-0.5), k), axis=-1)
            out = jnp.einsum('bhqk,bhkd->bhqd', att, v)
            out = jnp.transpose(out, (0, 2, 1, 3)).reshape(b, s, d)
            return out @ Wproj + bproj

        def _mamba(xm, W_in, W_conv, b_conv, W_x, W_dt, b_dt, A_log, D_param, W_out):
            b, s, _ = xm.shape
            xz = xm @ W_in
            xr, z = jnp.split(xz, 2, axis=-1)
            xt = jnp.transpose(xr, (0, 2, 1))
            xt = jax.lax.conv_general_dilated(xt, W_conv, window_strides=(1,), padding=[(K - 1, 0)], dimension_numbers=('NCH', 'OIH', 'NCH'), feature_group_count=DI)
            xt = xt + b_conv[None, :, None]
            u = jax.nn.silu(jnp.transpose(xt, (0, 2, 1)))
            x_dbl = u @ W_x
            dt, Bm, Cm = jnp.split(x_dbl, [DT_RANK, DT_RANK + N], axis=-1)
            delta = jax.nn.softplus(dt @ W_dt + b_dt)
            A = -jnp.exp(A_log)

            def step(h, inp):
                d_t, B_t, C_t, u_t = inp
                dA = jnp.exp(d_t[:, :, None] * A[None])
                h = dA * h + (d_t * u_t)[:, :, None] * B_t[:, None, :]
                y = jnp.sum(h * C_t[:, None, :], axis=-1)
                return (h, y)
            xs = (jnp.transpose(delta, (1, 0, 2)), jnp.transpose(Bm, (1, 0, 2)), jnp.transpose(Cm, (1, 0, 2)), jnp.transpose(u, (1, 0, 2)))
            h0 = jnp.zeros((b, DI, N), xm.dtype)
            _, ys = jax.lax.scan(step, h0, xs)
            y = jnp.transpose(ys, (1, 0, 2)) + u * D_param
            y = y * jax.nn.silu(z)
            return y @ W_out
        key = jax.random.key(seed)
        ks = jax.random.split(key, 20)
        w = lambda k, shp, s=0.02: jax.random.normal(k, shp, dtype=jnp.float32) * s
        inp = {'x': jax.random.normal(ks[0], (4, 512, D), dtype=jnp.float32), 'c': jax.random.normal(ks[1], (4, 2 * D), dtype=jnp.float32), 'ln1_g': jnp.ones((D,), jnp.float32), 'ln1_b': jnp.zeros((D,), jnp.float32), 'Wqkv': w(ks[2], (D, 3 * D)), 'bqkv': jnp.zeros((3 * D,), jnp.float32), 'Wproj': w(ks[3], (D, D)), 'bproj': jnp.zeros((D,), jnp.float32), 'W_ada': w(ks[4], (2 * D, 3 * D)), 'b_ada': jnp.zeros((3 * D,), jnp.float32), 'W_in': w(ks[5], (D, 2 * DI)), 'W_conv': w(ks[6], (DI, 1, K), 0.2), 'b_conv': jnp.zeros((DI,), jnp.float32), 'W_x': w(ks[7], (DI, DT_RANK + 2 * N)), 'W_dt': w(ks[8], (DT_RANK, DI), 0.1), 'b_dt': jnp.full((DI,), -4.0, jnp.float32), 'A_log': jnp.broadcast_to(jnp.log(jnp.arange(1, N + 1, dtype=jnp.float32)), (DI, N)).copy(), 'D_param': jnp.ones((DI,), jnp.float32), 'W_out': w(ks[9], (DI, D)), 'ln2_g': jnp.ones((2 * D,), jnp.float32), 'ln2_b': jnp.zeros((2 * D,), jnp.float32), 'W_full': w(ks[10], (2 * D, D)), 'b_full': jnp.zeros((D,), jnp.float32)}
        return inp
    _L1_cond_all = _L1_cond_setup()
    _L1_cond_in = {k: v for k, v in _L1_cond_all.items() if k in ('ln1_g', 'ln1_b', 'Wqkv', 'bqkv', 'Wproj', 'bproj', 'W_ada', 'b_ada', 'W_in', 'W_conv', 'b_conv', 'W_x', 'W_dt', 'b_dt', 'A_log', 'D_param', 'W_out', 'ln2_g', 'ln2_b', 'W_full', 'b_full')}
    del _L1_cond_all
    return {'x': x, 'cond_2048': cond_2048, 'mask_BxS_ik0': mask_BxS_ik0, 'L0_cond_norm_scale': _L0_cond_in['norm_scale'], 'L0_cond_norm_bias': _L0_cond_in['norm_bias'], 'L0_cond_Wq': _L0_cond_in['Wq'], 'L0_cond_bq': _L0_cond_in['bq'], 'L0_cond_Wk': _L0_cond_in['Wk'], 'L0_cond_bk': _L0_cond_in['bk'], 'L0_cond_Wv': _L0_cond_in['Wv'], 'L0_cond_bv': _L0_cond_in['bv'], 'L0_cond_film_emb_W': _L0_cond_in['film_emb_W'], 'L0_cond_film_emb_b': _L0_cond_in['film_emb_b'], 'L0_cond_film_norm_scale': _L0_cond_in['film_norm_scale'], 'L0_cond_film_norm_bias': _L0_cond_in['film_norm_bias'], 'L0_cond_film_out_W': _L0_cond_in['film_out_W'], 'L0_cond_film_out_b': _L0_cond_in['film_out_b'], 'L1_cond_ln1_g': _L1_cond_in['ln1_g'], 'L1_cond_ln1_b': _L1_cond_in['ln1_b'], 'L1_cond_Wqkv': _L1_cond_in['Wqkv'], 'L1_cond_bqkv': _L1_cond_in['bqkv'], 'L1_cond_Wproj': _L1_cond_in['Wproj'], 'L1_cond_bproj': _L1_cond_in['bproj'], 'L1_cond_W_ada': _L1_cond_in['W_ada'], 'L1_cond_b_ada': _L1_cond_in['b_ada'], 'L1_cond_W_in': _L1_cond_in['W_in'], 'L1_cond_W_conv': _L1_cond_in['W_conv'], 'L1_cond_b_conv': _L1_cond_in['b_conv'], 'L1_cond_W_x': _L1_cond_in['W_x'], 'L1_cond_W_dt': _L1_cond_in['W_dt'], 'L1_cond_b_dt': _L1_cond_in['b_dt'], 'L1_cond_A_log': _L1_cond_in['A_log'], 'L1_cond_D_param': _L1_cond_in['D_param'], 'L1_cond_W_out': _L1_cond_in['W_out'], 'L1_cond_ln2_g': _L1_cond_in['ln2_g'], 'L1_cond_ln2_b': _L1_cond_in['ln2_b'], 'L1_cond_W_full': _L1_cond_in['W_full'], 'L1_cond_b_full': _L1_cond_in['b_full']}

def reference(x, cond_2048, mask_BxS_ik0, L0_cond_norm_scale, L0_cond_norm_bias, L0_cond_Wq, L0_cond_bq, L0_cond_Wk, L0_cond_bk, L0_cond_Wv, L0_cond_bv, L0_cond_film_emb_W, L0_cond_film_emb_b, L0_cond_film_norm_scale, L0_cond_film_norm_bias, L0_cond_film_out_W, L0_cond_film_out_b, L1_cond_ln1_g, L1_cond_ln1_b, L1_cond_Wqkv, L1_cond_bqkv, L1_cond_Wproj, L1_cond_bproj, L1_cond_W_ada, L1_cond_b_ada, L1_cond_W_in, L1_cond_W_conv, L1_cond_b_conv, L1_cond_W_x, L1_cond_W_dt, L1_cond_b_dt, L1_cond_A_log, L1_cond_D_param, L1_cond_W_out, L1_cond_ln2_g, L1_cond_ln2_b, L1_cond_W_full, L1_cond_b_full):
    import jax
    import jax.numpy as jnp

    def _L0_cond_ref(x, emb, src_mask, norm_scale, norm_bias, Wq, bq, Wk, bk, Wv, bv, film_emb_W, film_emb_b, film_norm_scale, film_norm_bias, film_out_W, film_out_b):
        import jax, jax.numpy as jnp
        import numpy as np
        H = 16
        LN_EPS = 1e-05

        def _layernorm(x, scale, bias):
            mu = jnp.mean(x, axis=-1, keepdims=True)
            var = jnp.var(x, axis=-1, keepdims=True)
            return (x - mu) * jax.lax.rsqrt(var + LN_EPS) * scale + bias
        B, T, D = x.shape
        dh = D // H
        xn = _layernorm(x, norm_scale, norm_bias)
        q = xn @ Wq + bq
        k = xn @ Wk + bk
        v = xn @ Wv + bv
        mask = (src_mask == 1)[:, :, None]
        k = jnp.where(mask, -jnp.inf, k)
        v = jnp.where(mask, 0.0, v)
        q = q.reshape(B, T, H, dh).transpose(0, 2, 1, 3)
        k = k.reshape(B, T, H, dh).transpose(0, 2, 1, 3)
        v = v.reshape(B, T, H, dh).transpose(0, 2, 1, 3)
        q = jax.nn.softmax(q, axis=-1)
        k = jax.nn.softmax(k, axis=2)
        attn = jnp.einsum('bhse,bhsd->bhed', k, v)
        y = jnp.einsum('bhtd,bhed->bhte', q, attn)
        y = y.transpose(0, 2, 1, 3).reshape(B, T, D)
        emb_out = jax.nn.silu(emb) @ film_emb_W + film_emb_b
        scale, shift = jnp.split(emb_out, 2, axis=-1)
        h = _layernorm(y, film_norm_scale, film_norm_bias) * (1.0 + scale[:, None, :]) + shift[:, None, :]
        h = jax.nn.silu(h) @ film_out_W + film_out_b
        return x + h

    def _L1_cond_ref(x, c, ln1_g, ln1_b, Wqkv, bqkv, Wproj, bproj, W_ada, b_ada, W_in, W_conv, b_conv, W_x, W_dt, b_dt, A_log, D_param, W_out, ln2_g, ln2_b, W_full, b_full):
        import jax, jax.numpy as jnp
        import numpy as np
        D = 512
        H = 8
        DI = 1024
        DT_RANK = 64
        N = 16
        K = 4
        EPS = 1e-05

        def _ln(x, g, b):
            mu = jnp.mean(x, axis=-1, keepdims=True)
            var = jnp.mean(jnp.square(x - mu), axis=-1, keepdims=True)
            return (x - mu) * jax.lax.rsqrt(var + EPS) * g + b

        def _attention(xm, Wqkv, bqkv, Wproj, bproj):
            b, s, d = xm.shape
            hd = d // H
            qkv = (xm @ Wqkv + bqkv).reshape(b, s, 3, H, hd)
            q = jnp.transpose(qkv[:, :, 0], (0, 2, 1, 3))
            k = jnp.transpose(qkv[:, :, 1], (0, 2, 1, 3))
            v = jnp.transpose(qkv[:, :, 2], (0, 2, 1, 3))
            att = jax.nn.softmax(jnp.einsum('bhqd,bhkd->bhqk', q * hd ** (-0.5), k), axis=-1)
            out = jnp.einsum('bhqk,bhkd->bhqd', att, v)
            out = jnp.transpose(out, (0, 2, 1, 3)).reshape(b, s, d)
            return out @ Wproj + bproj

        def _mamba(xm, W_in, W_conv, b_conv, W_x, W_dt, b_dt, A_log, D_param, W_out):
            b, s, _ = xm.shape
            xz = xm @ W_in
            xr, z = jnp.split(xz, 2, axis=-1)
            xt = jnp.transpose(xr, (0, 2, 1))
            xt = jax.lax.conv_general_dilated(xt, W_conv, window_strides=(1,), padding=[(K - 1, 0)], dimension_numbers=('NCH', 'OIH', 'NCH'), feature_group_count=DI)
            xt = xt + b_conv[None, :, None]
            u = jax.nn.silu(jnp.transpose(xt, (0, 2, 1)))
            x_dbl = u @ W_x
            dt, Bm, Cm = jnp.split(x_dbl, [DT_RANK, DT_RANK + N], axis=-1)
            delta = jax.nn.softplus(dt @ W_dt + b_dt)
            A = -jnp.exp(A_log)

            def step(h, inp):
                d_t, B_t, C_t, u_t = inp
                dA = jnp.exp(d_t[:, :, None] * A[None])
                h = dA * h + (d_t * u_t)[:, :, None] * B_t[:, None, :]
                y = jnp.sum(h * C_t[:, None, :], axis=-1)
                return (h, y)
            xs = (jnp.transpose(delta, (1, 0, 2)), jnp.transpose(Bm, (1, 0, 2)), jnp.transpose(Cm, (1, 0, 2)), jnp.transpose(u, (1, 0, 2)))
            h0 = jnp.zeros((b, DI, N), xm.dtype)
            _, ys = jax.lax.scan(step, h0, xs)
            y = jnp.transpose(ys, (1, 0, 2)) + u * D_param
            y = y * jax.nn.silu(z)
            return y @ W_out
        ada = jax.nn.silu(c) @ W_ada + b_ada
        shift, scale, gate = jnp.split(ada, 3, axis=1)
        xn = _ln(x, ln1_g, ln1_b)
        xm = xn * (1.0 + scale[:, None, :]) + shift[:, None, :]
        attn_out = _attention(xm, Wqkv, bqkv, Wproj, bproj)
        ssm_out = _mamba(xm, W_in, W_conv, b_conv, W_x, W_dt, b_dt, A_log, D_param, W_out)
        combined = jnp.concatenate([ssm_out, attn_out], axis=-1)
        full = jax.nn.silu(_ln(combined, ln2_g, ln2_b) @ W_full + b_full)
        return x + gate[:, None, :] * full
    x = _L0_cond_ref(x, cond_2048, mask_BxS_ik0, L0_cond_norm_scale, L0_cond_norm_bias, L0_cond_Wq, L0_cond_bq, L0_cond_Wk, L0_cond_bk, L0_cond_Wv, L0_cond_bv, L0_cond_film_emb_W, L0_cond_film_emb_b, L0_cond_film_norm_scale, L0_cond_film_norm_bias, L0_cond_film_out_W, L0_cond_film_out_b)
    x = _L1_cond_ref(x, cond_2048, L1_cond_ln1_g, L1_cond_ln1_b, L1_cond_Wqkv, L1_cond_bqkv, L1_cond_Wproj, L1_cond_bproj, L1_cond_W_ada, L1_cond_b_ada, L1_cond_W_in, L1_cond_W_conv, L1_cond_b_conv, L1_cond_W_x, L1_cond_W_dt, L1_cond_b_dt, L1_cond_A_log, L1_cond_D_param, L1_cond_W_out, L1_cond_ln2_g, L1_cond_ln2_b, L1_cond_W_full, L1_cond_b_full)
    return x

_drawn_inputs = setup_inputs


def setup_inputs(seed=0):
    import zlib

    import numpy as np

    out = dict(_drawn_inputs(seed))
    spreads = {'L0_cond_norm_scale': (1.0, 0.2),
     'L0_cond_norm_bias': (0.0, 0.1),
     'L0_cond_bq': (0.0, 0.268),
     'L0_cond_bk': (0.0, 2.0),
     'L0_cond_bv': (0.0, 0.1),
     'L0_cond_film_emb_b': (0.0, 0.1),
     'L0_cond_film_norm_scale': (1.0, 0.2),
     'L0_cond_film_norm_bias': (0.0, 0.273),
     'L0_cond_film_out_b': (0.0, 0.1),
     'L1_cond_ln1_g': (1.0, 0.6),
     'L1_cond_ln1_b': (0.0, 0.379),
     'L1_cond_bqkv': (0.0, 2.0),
     'L1_cond_bproj': (0.0, 2.0),
     'L1_cond_b_ada': (0.0, 0.1),
     'L1_cond_b_conv': (0.0, 0.8),
     'L1_cond_b_dt': (-4.0, 0.6),
     'L1_cond_D_param': (1.0, 0.6),
     'L1_cond_ln2_g': (1.0, 0.578),
     'L1_cond_ln2_b': (0.0, 0.636),
     'L1_cond_b_full': (0.0, 0.36)}
    factors = {'L1_cond_W_conv': 2.846,
     'L1_cond_W_x': 8.0,
     'L1_cond_W_dt': 8.0,
     'L1_cond_A_log': 8.0,
     'L1_cond_Wqkv': 8.0,
     'L1_cond_Wproj': 8.0}
    for name, (base, spread) in spreads.items():
        noise = np.random.default_rng([zlib.crc32(name.encode()), seed]).standard_normal(out[name].shape)
        drawn = base * np.exp(spread * noise) if base else spread * noise
        out[name] = jnp.asarray(drawn.astype(out[name].dtype))
    for name, factor in factors.items():
        out[name] = (out[name] * factor).astype(out[name].dtype)
    return out
```

```python
from contextlib import ExitStack

import numpy as np

import concourse.bass as bass
from concourse import mybir

ALU = mybir.AluOpType
ACT = mybir.ActivationFunctionType
F32 = mybir.dt.float32
I32 = mybir.dt.int32
AX = mybir.AxisListType.X

P = 128
B, T, D, E = 8, 512, 512, 1024
TT, DC, EC = T // P, D // P, E // P
H0, DH0 = 16, 32
H1, DH1 = 8, 64
DI, N, RANK, TAPS = 1024, 16, 64, 4
IC = DI // P
QUAD = 4
XD = RANK + 2 * N
EPS = 1e-5
MASKED = -float(2 ** 100)

VECTORS = [
    ("L0_cond_norm_scale", 0, DC), ("L0_cond_norm_bias", 0, DC), ("L0_cond_bk", 0, DC),
    ("L0_cond_film_norm_scale", 0, DC), ("L0_cond_film_norm_bias", 0, DC),
    ("L1_cond_ln1_g", 0, DC), ("L1_cond_ln1_b", 0, DC), ("L1_cond_bqkv", 0, 2 * DC),
    ("L1_cond_b_conv", 0, IC), ("L1_cond_b_dt", 0, IC), ("L1_cond_D_param", 0, IC),
    ("L1_cond_ln2_g", 0, 2 * DC), ("L1_cond_ln2_b", 0, 2 * DC),
]
COL, NCOL = {}, 0
for _name, _, _n in VECTORS:
    COL[_name] = NCOL
    NCOL += _n
FILM_A, FILM_B, LN1_A, LN1_B, VALID = (DC * i for i in range(5))
NCUR = VALID + TT


class Link:

    def __init__(self, eng, sem, per):
        self.eng, self.sem, self.per = eng, sem, per

    def begin(self, b):
        self.base, self.n = b * self.per, 0

    def __call__(self, ins):
        ins.then_inc(self.sem, 1)
        self.n += 1
        self.eng.wait_ge(self.sem, self.base + self.n)

    def end(self):
        assert self.n == self.per, (self.n, self.per)


def build(nc, a, out):
    ctx = ExitStack()
    with ctx:
        def sem(name, c=ctx):
            return c.enter_context(nc.semaphore(name))

        def sb(name, shape, dt=F32, c=ctx):
            return c.enter_context(nc.sbuf_tensor(name, shape, dt))

        x1_d = nc.dram_tensor("x1_d", (B, T, D), F32, kind="Internal").ap()
        xm_d = nc.dram_tensor("xm_d", (B, P, DC, T), F32, kind="Internal").ap()
        attn_d = nc.dram_tensor("attn_d", (B, T, D), F32, kind="Internal").ap()
        gate_d = nc.dram_tensor("gate_d", (B, D), F32, kind="Internal").ap()
        b_d = nc.dram_tensor("b_d", (B, N, T), F32, kind="Internal").ap()

        bank = [ctx.enter_context(nc.psum_tensor(f"bank{i}", [P, 512], F32)) for i in range(8)]

        ident = sb("ident", [P, P])
        cols = sb("cols", [P, NCOL])
        bq8 = sb("bq8", [P, DC])
        aneg = sb("aneg", [P, IC, N])
        convw = sb("convw", [P, IC, TAPS])
        per_batch = sb("per_batch", [P, B, NCUR])

        def col(name, c):
            return cols[:, COL[name] + c:COL[name] + c + 1]

        setup(nc, a, bank, ident, cols, bq8, aneg, convw, per_batch, gate_d)
        attend(nc, a, bank, ident, cols, col, bq8, per_batch, x1_d, xm_d, attn_d)
        mix(nc, a, out, bank, ident, col, aneg, convw, x1_d, xm_d, attn_d, gate_d, b_d)


def setup(nc, a, bank, ident, cols, bq8, aneg, convw, per_batch, gate_d):
    ctx = ExitStack()
    with ctx:
        def sem(name):
            return ctx.enter_context(nc.semaphore(name))

        def sb(name, shape, dt=F32):
            return ctx.enter_context(nc.sbuf_tensor(name, shape, dt))

        vecrows = sb("vecrows", [P, P])
        maskrows = sb("maskrows", [B * TT, P], I32)
        validrows = sb("validrows", [B * TT, P])
        cond = sb("cond", [B, E])
        scond = sb("scond", [B, E])
        condT = sb("condT", [P, EC, B])
        wfilm = sb("wfilm", [P, EC, 2 * D])
        wada = sb("wada", [P, EC, 3 * D])
        film_bias = sb("film_bias", [B, 2 * D])
        ada_bias = sb("ada_bias", [B, 3 * D])
        film = sb("film", [B, 2 * D])
        ada = sb("ada", [B, 3 * D])
        scale1 = sb("scale1", [P, 2, DC, B])
        zeros = sb("zeros", [P, P])

        vec_in, mask_in, cond_in = sem("vec_in"), sem("mask_in"), sem("cond_in")
        par_in, film_in, ada_in = sem("par_in"), sem("film_in"), sem("ada_in")
        zeroed, ident_done, silu_done = sem("zeroed"), sem("ident_done"), sem("silu_done")
        a_exp, valid_done = sem("a_exp"), sem("valid_done")
        turned, condT_done, cond_mm, rows_done = sem("turned"), sem("condT_done"), sem("cond_mm"), sem("rows_done")
        rows_turned, own = sem("rows_turned"), sem("setup_dve")
        gate_out = sem("gate_out")

        with nc.Block() as block:

            @block.sync
            def _(sp):
                sp.dma_start(cond[:], a["cond_2048"]).then_inc(cond_in, 16)
                for name, first, n in VECTORS:
                    src = a[name][first:first + n * P].rearrange("(c p) -> c p", p=P)
                    sp.dma_start(vecrows[COL[name]:COL[name] + n, :], src).then_inc(vec_in, 16)
                sp.dma_start(maskrows[:], a["mask_BxS_ik0"].rearrange("b (t p) -> (b t) p", p=P)).then_inc(mask_in, 16)
                sp.dma_start(wfilm[:], a["L0_cond_film_emb_W"].rearrange("(c p) n -> p c n", p=P)).then_inc(film_in, 16)
                sp.dma_start(film_bias[:], a["L0_cond_film_emb_b"].rearrange("(o n) -> o n", o=1).to_broadcast([B, 2 * D])).then_inc(film_in, 16)
                sp.wait_ge(rows_done, 5)
                sp.dma_start(gate_d, ada[:, 2 * D:3 * D]).then_inc(gate_out, 16)
                sp.wait_ge(gate_out, 16)

            @block.gpsimd
            def _(pool):
                nc.gpsimd.memset(zeros[:], 0.0).then_inc(zeroed, 1)
                pool.wait_ge(zeroed, 1)
                nc.gpsimd.affine_select(out=ident[:], in_=zeros[:], compare_op=ALU.not_equal, fill=1.0, base=0,
                                        pattern=[[-1, P]], channel_multiplier=1).then_inc(ident_done, 1)

            @block.scalar
            def _(act):
                act.dma_start(aneg[:], a["L1_cond_A_log"].rearrange("(c p) n -> p c n", p=P)).then_inc(par_in, 16)
                act.dma_start(convw[:], a["L1_cond_W_conv"].rearrange("(c p) o k -> p c (o k)", p=P)).then_inc(par_in, 16)
                act.dma_start(wada[:], a["L1_cond_W_ada"].rearrange("(c p) n -> p c n", p=P)).then_inc(ada_in, 16)
                act.dma_start(ada_bias[:], a["L1_cond_b_ada"].rearrange("(o n) -> o n", o=1).to_broadcast([B, 3 * D])).then_inc(ada_in, 16)
                act.wait_ge(cond_in, 16)
                nc.scalar.activation(scond[:], cond[:], ACT.Silu).then_inc(silu_done, 1)
                act.wait_ge(par_in, 32)
                nc.scalar.activation(aneg[:], aneg[:], ACT.Exp).then_inc(a_exp, 1)

            @block.tensor
            def _(pe):
                pe.wait_ge(ident_done, 1)
                pe.wait_ge(vec_in, 16 * len(VECTORS))
                nc.tensor.transpose(bank[0][:, 0:NCOL], vecrows[0:NCOL, :], ident[0:NCOL, 0:NCOL]).then_inc(turned, 1)
                pe.wait_ge(valid_done, 1)
                nc.tensor.transpose(bank[1][:, 0:B * TT], validrows[:], ident[0:B * TT, 0:B * TT]).then_inc(turned, 1)
                pe.wait_ge(silu_done, 1)
                for c in range(EC):
                    last = nc.tensor.transpose(bank[2][:, c * B:(c + 1) * B], scond[:, c * P:(c + 1) * P], ident[0:B, 0:B])
                last.then_inc(turned, 1)
                pe.wait_ge(condT_done, 1)
                for w, arrived, first, n in ((wfilm, film_in, 3, 2), (wada, ada_in, 5, 3)):
                    pe.wait_ge(arrived, 32)
                    for j in range(n):
                        for c in range(EC):
                            last = nc.tensor.matmul(bank[first + j][0:B, :], condT[:, c, :], w[:, c, j * D:(j + 1) * D],
                                                    start=(c == 0), stop=(c == EC - 1))
                        last.then_inc(cond_mm, 1)
                pe.wait_ge(rows_done, 5)
                for i in range(4 * DC):
                    src = film if i < 2 * DC else ada
                    j = i % (2 * DC)
                    last = nc.tensor.transpose(bank[0][:, i * B:(i + 1) * B], src[:, j * P:(j + 1) * P], ident[0:B, 0:B])
                last.then_inc(rows_turned, 1)

            @block.vector
            def _(dve):
                link = Link(dve, own, 100)
                link.begin(0)
                dve.wait_ge(mask_in, 16)
                nc.vector.tensor_scalar(validrows[:], maskrows[:], 1.0, None, ALU.not_equal).then_inc(valid_done, 1)
                dve.wait_ge(turned, 1)
                link(nc.vector.tensor_copy(cols[:], bank[0][:, 0:NCOL]))
                i = COL["L1_cond_bqkv"]
                nc.vector.tensor_scalar(bq8[:], cols[:, i:i + DC], DH1 ** -0.5, None, ALU.mult)
                dve.wait_ge(turned, 2)
                nc.vector.tensor_copy(per_batch[:, :, VALID:VALID + TT], bank[1][:, 0:B * TT].rearrange("p (b t) -> p b t", t=TT))
                dve.wait_ge(turned, 3)
                nc.vector.tensor_copy(condT[:], bank[2][:, 0:EC * B].rearrange("p (c b) -> p c b", b=B)).then_inc(condT_done, 1)
                dve.wait_ge(a_exp, 1)
                nc.vector.tensor_scalar(aneg[:], aneg[:], -1.0, None, ALU.mult)
                for j in range(5):
                    rows, bias, k = (film, film_bias, j) if j < 2 else (ada, ada_bias, j - 2)
                    dve.wait_ge(film_in if j < 2 else ada_in, 32)
                    dve.wait_ge(cond_mm, j + 1)
                    nc.vector.tensor_tensor(rows[:, k * D:(k + 1) * D], bank[3 + j][0:B, :], bias[:, k * D:(k + 1) * D],
                                            ALU.add).then_inc(rows_done, 1)
                dve.wait_ge(rows_turned, 1)
                t = bank[0][:, 0:4 * DC * B].rearrange("p (k c b) -> p k c b", k=4, b=B)
                for i, (g, bb, sc, sh, at_a, at_b) in enumerate((
                        ("L0_cond_film_norm_scale", "L0_cond_film_norm_bias", 0, 1, FILM_A, FILM_B),
                        ("L1_cond_ln1_g", "L1_cond_ln1_b", 3, 2, LN1_A, LN1_B))):
                    link(nc.vector.tensor_scalar(scale1[:, i], t[:, sc], 1.0, None, ALU.add))
                    for at, v in ((at_a, g), (at_b, bb)):
                        for c in range(DC):
                            last = nc.vector.tensor_scalar(per_batch[:, :, at + c], scale1[:, i, c, :],
                                                           cols[:, COL[v] + c:COL[v] + c + 1], None, ALU.mult)
                    link(last)
                    dst = per_batch[:, :, at_b:at_b + DC].rearrange("p b c -> p c b")
                    link(nc.vector.tensor_tensor(dst, dst, t[:, sh], ALU.add))


def attend(nc, a, bank, ident, cols, col, bq8, per_batch, x1_d, xm_d, attn_d):
    ctx = ExitStack()
    with ctx:
        def sem(name):
            return ctx.enter_context(nc.semaphore(name))

        def sb(name, shape, dt=F32):
            return ctx.enter_context(nc.sbuf_tensor(name, shape, dt))

        W = {}
        for name in ("Wk", "Wq", "Wv", "film_out_W"):
            W[name] = sb(name, [P, DC, D])
        wqkv = sb("wqkv", [P, DC, 3 * D])
        wproj = sb("wproj", [P, DC, D])
        bias = {k: sb(f"bias_{k}", [P, D]) for k in ("q", "v", "film", "v1", "proj")}
        X = sb("X", [P, TT, D])
        H = sb("H", [P, TT, D])
        NT = sb("NT", [P, DC, T])
        KT = sb("KT", [P, DC, T])
        Q = sb("Q", [P, TT, D])
        QT = sb("QT", [P, DC, T])
        V = sb("V", [P, TT, D])
        ATT = sb("ATT", [P, DC, P])
        blocks = sb("blocks", [P, DC, P])
        mask = sb("mask", [P, T], I32)
        mbias = sb("mbias", [P, T])
        nkmax, kden, kr = sb("nkmax", [P, DC]), sb("kden", [P, DC]), sb("kr", [P, DC])
        qmax, qr = sb("qmax", [P, TT, H0]), sb("qr", [P, TT, H0])
        cur = sb("cur", [P, NCUR])
        H2 = sb("H2", [P, TT, D])
        XM = sb("XM", [P, DC, T])
        Q2, K2 = sb("Q2", [P, DC, T]), sb("K2", [P, DC, T])
        V2 = sb("V2", [P, TT, D])
        PR = sb("PR", [P, 2, TT, T])
        PT = sb("PT", [P, TT, T])
        nsmax, rsum = sb("nsmax", [P, 2, TT]), sb("rsum", [P, H1, TT])
        rrec = sb("rrec", [P, H1, TT])
        stats = sb("stats", [P, TT, 6])
        mv, rs, rt = sb("mv", [P, TT, 2]), sb("rs", [P, TT]), sb("rt", [P, TT])
        veps, spare = sb("veps", [P, TT]), sb("spare", [P, 1])

        w_in = sem("w_in"); bias_in = sem("bias_in")
        x_in, mask_in = sem("x_in"), sem("mk_in")
        blocks_zero, blocks_done = sem("blocks_zero"), sem("blocks_done")
        cur_done, xb_done = sem("cur_done"), sem("xb_done")
        ln_var, ln_ln, ln_r0 = sem("ln_var"), sem("ln_ln"), sem("ln_r0")
        xhat, yhat, x1hat = sem("xhat"), sem("yhat"), sem("x1hat")
        t1_full, t1_done = sem("t1_full"), sem("t1_done")
        m1_full, m1_done = sem("m1_full"), sem("m1_done")
        kmax, kexp, knorm = sem("kmax"), sem("kexp"), sem("knorm")
        mbias_done, qsub = sem("mbias_done"), sem("qsub")
        t2_full, t2_done = sem("t2_full"), sem("t2_done")
        sc_full, smax, pexp = sem("sc_full"), sem("smax"), sem("pexp")
        pt_full, pt_done = sem("pt_full"), sem("pt_done")
        o_full, o_done = sem("o_full"), sem("o_done")
        x1_out, xm_out, attn_out = sem("x1_out"), sem("xm_out"), sem("attn_out")
        own0, own1 = sem("l0_dve"), sem("l1_dve")
        T1, M1, T2, SC, PTN, O = 20, 22, 12, H1 * TT, H1 * TT, 16
        T1_X, T1_E, T1_Q, T1_Y, T1_X1 = 0, 4, 8, 12, 16
        M1_K, M1_Q, M1_V, M1_ATT, M1_SUM, M1_Y, M1_F = 0, 4, 8, 12, 13, 14, 18
        T2_QK, T2_O = 0, 8
        O_V, O_PV, O_P = 0, 4, 12
        t1_bank, m1_bank, t2_bank, sc_bank, pt_bank, o_bank = bank[0], bank[1:3], bank[3], bank[4:6], bank[6], bank[7]
        qk_bank, vp_bank = (t2_bank, pt_bank), (o_bank, pt_bank)

        S_TURN_X, S_K, S_E, S_Q, S_V, S_TURN_Q, S_ATT, S_Y, S_NORM_Y, S_TURN_Y, S_F, S_NORM_X1, S_TURN_X1 = (
            0, 4, 9, 8, 12, 12, 16, 17, 19, 22, 23, 27, 29)
        SLOTS = H1 * TT

        def l0_alone(l0, n):
            for g in range(SLOTS):
                l0(n, g)

        with nc.Block() as block:

            @block.sync
            def _(sp):
                for name in ("Wk", "Wq", "Wv", "film_out_W"):
                    sp.dma_start(W[name][:], a["L0_cond_" + name].rearrange("(c p) n -> p c n", p=P)).then_inc(w_in, 16)
                sp.dma_start(wqkv[:], a["L1_cond_Wqkv"].rearrange("(c p) n -> p c n", p=P)).then_inc(w_in, 16)
                sp.dma_start(wproj[:], a["L1_cond_Wproj"].rearrange("(c p) n -> p c n", p=P)).then_inc(w_in, 16)
                def load(n, x1_stored, x1_normed, masked):
                    sp.wait_ge(x1_out, x1_stored)
                    sp.wait_ge(x1hat, x1_normed)
                    sp.dma_start(X[:], a["x"][n].rearrange("(t p) d -> p t d", p=P)).then_inc(x_in, 16)
                    sp.wait_ge(mbias_done, masked)
                    sp.dma_start(mask[:], a["mask_BxS_ik0"][bass.ds(n, 1), :].to_broadcast([P, T])).then_inc(mask_in, 16)

                def store_l0(n):
                    sp.wait_ge(m1_done, n * M1 + M1)
                    sp.dma_start(x1_d[n].rearrange("(t p) d -> p t d", p=P), X[:]).then_inc(x1_out, 16)
                    sp.wait_ge(t1_done, n * T1 + T1)
                    sp.dma_start(xm_d[n], XM[:]).then_inc(xm_out, 16)

                def store_l1(b):
                    sp.wait_ge(o_done, b * O + O)
                    sp.dma_start(attn_d[b].rearrange("(t p) d -> p t d", p=P), H2[:]).then_inc(attn_out, 16)

                load(0, 0, 0, 0)
                store_l0(0)
                with sp.Fori(0, B - 1) as b:
                    load(b + 1, sp.to_reg((b + 1) * 16), sp.to_reg((b + 1) * TT), b + 1)
                    store_l0(b + 1)
                    store_l1(b)
                store_l1(B - 1)
                sp.wait_ge(x1_out, B * 16)
                sp.wait_ge(xm_out, B * 16)
                sp.wait_ge(attn_out, B * 16)

            @block.gpsimd
            def _(pool):
                nc.gpsimd.memset(blocks[:], 0.0).then_inc(blocks_zero, 1)
                pool.wait_ge(blocks_zero, 1)
                for g in range(P // DH0):
                    s = slice(g * DH0, (g + 1) * DH0)
                    nc.gpsimd.memset(blocks[s, :, s], 1.0).then_inc(blocks_done, 1)
                pool.wait_ge(blocks_done, P // DH0)
                pool.wait_ge(bias_in, 5 * 16)
                with pool.Fori(0, B) as n:
                    pool.wait_ge(t1_done, n * T1)
                    nc.gpsimd.tensor_copy(cur[:], per_batch[:, n, :]).then_inc(cur_done, 1)
                    for t in range(TT):
                        pool.wait_ge(xhat, n * TT + t + 1)
                        nc.gpsimd.tensor_tensor(X[:, t, :], X[:, t, :], bias["film"][:], ALU.add).then_inc(xb_done, 1)

            @block.scalar
            def _(act):
                for k, (name, first) in {"q": ("L0_cond_bq", 0), "v": ("L0_cond_bv", 0), "film": ("L0_cond_film_out_b", 0),
                                         "v1": ("L1_cond_bqkv", 2 * D), "proj": ("L1_cond_bproj", 0)}.items():
                    src = a[name][first:first + D].rearrange("(o n) -> o n", o=1).to_broadcast([P, D])
                    act.dma_start(bias[k][:], src).then_inc(bias_in, 16)

                def inv_std(n, i):
                    act.wait_ge(ln_var, n * 3 + i + 1)
                    nc.scalar.activation(rt[:], veps[:], ACT.Ln).then_inc(ln_ln, 1)
                    act.wait_ge(ln_ln, n * 3 + i + 1)
                    nc.scalar.activation(rs[:], rt[:], ACT.Exp, scale=-0.5).then_inc(ln_r0, 1)

                def l0(n, g):
                    if S_TURN_X <= g < S_TURN_X + DC:
                        c = g - S_TURN_X
                        act.wait_ge(t1_full, n * T1 + T1_X + c + 1)
                        nc.scalar.activation(NT[:, c, :], t1_bank[:], ACT.Identity, scale=col("L0_cond_norm_scale", c),
                                             bias=col("L0_cond_norm_bias", c)).then_inc(t1_done, 1)
                    if S_K + 1 <= g < S_K + 1 + DC:
                        c = g - (S_K + 1)
                        act.wait_ge(kmax, n * DC + c + 1)
                        nc.scalar.activation(KT[:, c, :], KT[:, c, :], ACT.Exp, bias=nkmax[:, c:c + 1],
                                             accum_out=kden[:, c:c + 1]).then_inc(kexp, 1)
                    if S_E <= g < S_E + TT:
                        t = g - S_E
                        if t == 0:
                            act.wait_ge(cur_done, n + 1)
                        act.wait_ge(t1_full, n * T1 + T1_E + t + 1)
                        nc.scalar.activation(H[:, t, :], t1_bank[:], ACT.Identity,
                                             scale=cur[:, VALID + t:VALID + t + 1]).then_inc(t1_done, 1)
                    if S_TURN_Q <= g < S_TURN_Q + DC:
                        c = g - S_TURN_Q
                        act.wait_ge(t1_full, n * T1 + T1_Q + c + 1)
                        nc.scalar.activation(QT[:, c, :], t1_bank[:], ACT.Exp).then_inc(t1_done, 1)
                    if g == S_NORM_Y + 1:
                        inv_std(n, 1)
                    if g == S_TURN_Y:
                        for c in range(DC):
                            act.wait_ge(t1_full, n * T1 + T1_Y + c + 1)
                            nc.scalar.activation(NT[:, c, :], t1_bank[:], ACT.Silu, scale=cur[:, FILM_A + c:FILM_A + c + 1],
                                                 bias=cur[:, FILM_B + c:FILM_B + c + 1]).then_inc(t1_done, 1)
                    if g == S_NORM_X1 + 1:
                        inv_std(n, 2)
                    if S_TURN_X1 <= g < S_TURN_X1 + DC // 2:
                        if g == S_TURN_X1:
                            act.wait_ge(xm_out, n * 16)
                        for c in range(2 * (g - S_TURN_X1), 2 * (g - S_TURN_X1) + 2):
                            act.wait_ge(t1_full, n * T1 + T1_X1 + c + 1)
                            nc.scalar.activation(XM[:, c, :], t1_bank[:], ACT.Identity, scale=cur[:, LN1_A + c:LN1_A + c + 1],
                                                 bias=cur[:, LN1_B + c:LN1_B + c + 1]).then_inc(t1_done, 1)

                def l1(b, n):
                    for i in range(2 * DC):
                        if i == DC and n is not None:
                            inv_std(n, 0)
                        act.wait_ge(t2_full, b * T2 + T2_QK + i + 1)
                        if i < DC:
                            nc.scalar.activation(Q2[:, i, :], qk_bank[i % 2][:], ACT.Identity, scale=DH1 ** -0.5,
                                                 bias=bq8[:, i:i + 1]).then_inc(t2_done, 1)
                        else:
                            nc.scalar.activation(K2[:, i - DC, :], qk_bank[i % 2][:], ACT.Identity,
                                                 bias=col("L1_cond_bqkv", i)).then_inc(t2_done, 1)

                    def probabilities(h, t):
                        act.wait_ge(smax, b * SC + h * TT + t + 1)
                        if h >= 2 and t == 0:
                            act.wait_ge(pt_full, b * PTN + (h - 1) * TT)
                        nc.scalar.activation(PR[:, h % 2, t, :], sc_bank[t % 2][:], ACT.Exp, bias=nsmax[:, h % 2, t:t + 1],
                                             accum_out=rsum[:, h, t:t + 1]).then_inc(pexp, 1)

                    for t in range(TT):
                        probabilities(0, t)
                    for h in range(H1):
                        for k in range(TT):
                            if h + 1 < H1:
                                probabilities(h + 1, k)
                            if n is not None:
                                l0(n, h * TT + k)
                    for c in range(DC):
                        act.wait_ge(t2_full, b * T2 + T2_O + c + 1)
                        nc.scalar.activation(Q2[:, c, :], t2_bank[:], ACT.Identity).then_inc(t2_done, 1)

                inv_std(0, 0)
                l0_alone(l0, 0)
                with act.Fori(0, B - 1) as b:
                    l1(b, b + 1)
                l1(B - 1, None)

            @block.vector
            def _(dve):
                link0, link1 = Link(dve, own0, 3 * 5 + TT + 2), Link(dve, own1, H1)

                def variance(src):
                    for t in range(TT):
                        last = nc.vector.bn_stats(stats[:, t, :], src[:, t, :])
                    link0(last)
                    nc.vector.memset(spare[:], 0.0)
                    for t in range(TT):
                        last = nc.vector.bn_aggr(mv[:, t, :], stats[:, t, :])
                    link0(last)
                    nc.vector.tensor_scalar(veps[:], mv[:, :, 1], EPS, None, ALU.add).then_inc(ln_var, 1)

                def norm(n, i, src, dst, ready):
                    dve.wait_ge(ln_r0, n * 3 + i + 1)
                    link0(nc.vector.tensor_tensor(rt[:], rs[:], rs[:], ALU.mult))
                    link0(nc.vector.scalar_tensor_tensor(out=rt[:], in0=rt[:], scalar=-0.5, in1=veps[:], op0=ALU.mult, op1=ALU.mult))
                    link0(nc.vector.scalar_tensor_tensor(out=rs[:], in0=rt[:], scalar=1.5, in1=rs[:], op0=ALU.add, op1=ALU.mult))
                    for t in range(TT):
                        nc.vector.tensor_scalar(dst[:, t, :], src[:, t, :], mv[:, t, 0:1], rs[:, t:t + 1],
                                                ALU.subtract, ALU.mult).then_inc(ready, 1)

                def l0_begin(n):
                    link0.begin(n)
                    dve.wait_ge(x_in, n * 16 + 16)
                    variance(X)
                    dve.wait_ge(t1_full, n * T1)
                    norm(n, 0, X, H, xhat)

                def l0(n, g):
                    if g == S_TURN_X:
                        dve.wait_ge(mask_in, n * 16 + 16)
                        nc.vector.tensor_scalar(mbias[:], mask[:], 1.0, MASKED, ALU.is_equal, ALU.mult).then_inc(mbias_done, 1)
                    if S_K <= g < S_K + DC:
                        c = g - S_K
                        if c == 0:
                            dve.wait_ge(mbias_done, n + 1)
                        dve.wait_ge(m1_full, n * M1 + M1_K + c + 1)
                        nc.vector.scalar_tensor_tensor(out=KT[:, c, :], in0=m1_bank[c % 2][:], scalar=col("L0_cond_bk", c),
                                                       in1=mbias[:], op0=ALU.add, op1=ALU.add).then_inc(m1_done, 1)
                        dve.wait_ge(m1_done, n * M1 + M1_K + c + 1)
                        nc.vector.tensor_reduce(nkmax[:, c:c + 1], KT[:, c, :], AX, ALU.max, negate=True).then_inc(kmax, 1)
                    if S_Q <= g < S_Q + TT:
                        t = g - S_Q
                        dve.wait_ge(m1_full, n * M1 + M1_Q + t + 1)
                        nc.vector.tensor_tensor(Q[:, t, :], m1_bank[t % 2][:], bias["q"][:], ALU.add).then_inc(m1_done, 1)
                        dve.wait_ge(m1_done, n * M1 + M1_Q + t + 1)
                        heads = Q[:, t, :].rearrange("p (h d) -> p h d", d=DH0)
                        link0(nc.vector.tensor_reduce(qmax[:, t, :], heads, AX, ALU.max))
                        nc.vector.tensor_tensor(heads, heads, qmax[:, t, :].unsqueeze(2).to_broadcast([P, H0, DH0]),
                                                ALU.subtract).then_inc(qsub, 1)
                    if g == S_E - 1:
                        dve.wait_ge(kexp, n * DC + DC)
                        link0(nc.vector.scalar_tensor_tensor(out=kden[:], in0=nkmax[:], scalar=-MASKED / 2, in1=kden[:],
                                                             op0=ALU.is_lt, op1=ALU.mult))
                        link0(nc.vector.reciprocal(kr[:], kden[:]))
                        for c in range(DC):
                            nc.vector.tensor_scalar(KT[:, c, :], KT[:, c, :], kr[:, c:c + 1], None, ALU.mult).then_inc(knorm, 1)
                    if S_V <= g < S_V + TT:
                        t = g - S_V
                        dve.wait_ge(m1_full, n * M1 + M1_V + t + 1)
                        nc.vector.tensor_tensor(V[:, t, :], m1_bank[t % 2][:], bias["v"][:], ALU.add).then_inc(m1_done, 1)
                    if g == S_ATT:
                        dve.wait_ge(m1_full, n * M1 + M1_ATT + 1)
                        nc.vector.tensor_tensor(ATT[:], m1_bank[0][:].rearrange("p (c e) -> p c e", e=P), blocks[:],
                                                ALU.mult).then_inc(m1_done, 1)
                        dve.wait_ge(m1_full, n * M1 + M1_SUM + 1)
                        nc.vector.reciprocal(qr[:].rearrange("p t h -> p (t h)"), m1_bank[1][:, 0:TT * H0]).then_inc(m1_done, 1)
                    if S_Y <= g < S_Y + TT // 2:
                        if g == S_Y:
                            dve.wait_ge(m1_done, n * M1 + M1_SUM + 1)
                        for t in range(2 * (g - S_Y), 2 * (g - S_Y) + 2):
                            dve.wait_ge(m1_full, n * M1 + M1_Y + t + 1)
                            nc.vector.tensor_tensor(Q[:, t, :].rearrange("p (h d) -> p h d", d=DH0),
                                                    m1_bank[t % 2][:].rearrange("p (h d) -> p h d", d=DH0),
                                                    qr[:, t, :].unsqueeze(2).to_broadcast([P, H0, DH0]), ALU.mult).then_inc(m1_done, 1)
                    if g == S_NORM_Y:
                        dve.wait_ge(m1_done, n * M1 + M1_Y + TT)
                        variance(Q)
                    if g == S_NORM_Y + 1:
                        norm(n, 1, Q, H, yhat)
                    if S_F <= g < S_F + TT:
                        t = g - S_F
                        if t == 0:
                            dve.wait_ge(xb_done, n * TT + TT)
                        dve.wait_ge(m1_full, n * M1 + M1_F + t + 1)
                        nc.vector.tensor_tensor(X[:, t, :], m1_bank[t % 2][:], X[:, t, :], ALU.add).then_inc(m1_done, 1)
                    if g == S_NORM_X1:
                        dve.wait_ge(m1_done, n * M1 + M1)
                        variance(X)
                    if g == S_NORM_X1 + 1:
                        norm(n, 2, X, H, x1hat)
                        link0.end()

                def l1(b, n):
                    link1.begin(b)
                    if n is not None:
                        l0_begin(n)
                    for t in range(TT):
                        dve.wait_ge(o_full, b * O + O_V + t + 1)
                        nc.vector.tensor_tensor(V2[:, t, :], vp_bank[t % 2][:], bias["v1"][:], ALU.add).then_inc(o_done, 1)

                    def score_max(h, t):
                        dve.wait_ge(sc_full, b * SC + h * TT + t + 1)
                        nc.vector.tensor_reduce(nsmax[:, h % 2, t:t + 1], sc_bank[t % 2][:], AX, ALU.max, negate=True).then_inc(smax, 1)

                    def head_out(h):
                        dve.wait_ge(pexp, b * SC + (h + 1) * TT)
                        link1(nc.vector.reciprocal(rrec[:, h, :], rsum[:, h, :]))
                        dve.wait_ge(o_full, b * O + O_PV + h + 1)
                        nc.vector.tensor_tensor(H2[:, :, h * DH1:(h + 1) * DH1],
                                                o_bank[:, 0:TT * DH1].rearrange("p (t d) -> p t d", d=DH1),
                                                rrec[:, h, :].unsqueeze(2).to_broadcast([P, TT, DH1]), ALU.mult).then_inc(o_done, 1)

                    for t in range(TT):
                        score_max(0, t)
                    dve.wait_ge(attn_out, b * 16)
                    for h in range(H1):
                        for k in range(TT):
                            if h + 1 < H1:
                                score_max(h + 1, k)
                            if h >= 1 and k == 0:
                                dve.wait_ge(o_full, b * O + O_PV + h)
                            dve.wait_ge(pt_full, b * PTN + h * TT + k + 1)
                            nc.vector.tensor_copy(PT[:, k, :], pt_bank[:]).then_inc(pt_done, 1)
                            if h >= 1 and k == 0:
                                head_out(h - 1)
                            if n is not None:
                                l0(n, h * TT + k)
                    head_out(H1 - 1)
                    dve.wait_ge(t2_full, b * T2 + T2)
                    for t in range(TT):
                        dve.wait_ge(o_full, b * O + O_P + t + 1)
                        nc.vector.tensor_tensor(H2[:, t, :], vp_bank[t % 2][:], bias["proj"][:], ALU.add).then_inc(o_done, 1)
                    link1.end()

                dve.wait_ge(bias_in, 5 * 16)
                dve.wait_ge(blocks_done, P // DH0)
                l0_begin(0)
                l0_alone(l0, 0)
                with dve.Fori(0, B - 1) as b:
                    l1(b, b + 1)
                l1(B - 1, None)

            @block.tensor
            def _(pe):
                def turn(dst, src, c):
                    for t in range(TT):
                        last = nc.tensor.transpose(dst[:, t * P:(t + 1) * P], src[:, t, c * P:(c + 1) * P], ident[:])
                    return last

                def product(dst, lhs, rhs):
                    for c in range(DC):
                        last = nc.tensor.matmul(dst[:], lhs(c), rhs(c), start=(c == 0), stop=(c == DC - 1))
                    return last

                def l0(n, g):
                    def m1_free(i):
                        pe.wait_ge(m1_done, n * M1 + max(i - 1, 0))

                    def t1_free(i):
                        pe.wait_ge(t1_done, n * T1 + i)

                    if S_TURN_X <= g < S_TURN_X + DC:
                        if g == S_TURN_X:
                            pe.wait_ge(xhat, n * TT + TT)
                        t1_free(T1_X + g - S_TURN_X)
                        turn(t1_bank, H, g - S_TURN_X).then_inc(t1_full, 1)
                    if S_E <= g < S_E + TT:
                        t = g - S_E
                        if t == 0:
                            pe.wait_ge(knorm, n * DC + DC)
                        t1_free(T1_E + t)
                        for c in range(DC):
                            last = nc.tensor.transpose(t1_bank[:, c * P:(c + 1) * P], KT[:, c, t * P:(t + 1) * P], ident[:])
                        last.then_inc(t1_full, 1)
                    if S_K <= g < S_K + DC:
                        c = g - S_K
                        if c == 0:
                            t1_free(T1_X + DC)
                        m1_free(M1_K + c)
                        product(m1_bank[c % 2], lambda k: W["Wk"][:, k, c * P:(c + 1) * P], lambda k: NT[:, k, :]).then_inc(m1_full, 1)
                    for s, i, w in ((S_Q, M1_Q, "Wq"), (S_V, M1_V, "Wv")):
                        if s <= g < s + TT:
                            t = g - s
                            m1_free(i + t)
                            product(m1_bank[t % 2], lambda k: NT[:, k, t * P:(t + 1) * P], lambda k: W[w][:, k, :]).then_inc(m1_full, 1)
                    if S_TURN_Q <= g < S_TURN_Q + DC:
                        c = g - S_TURN_Q
                        if c == 0:
                            pe.wait_ge(qsub, n * TT + TT)
                        t1_free(T1_Q + c)
                        turn(t1_bank, Q, c).then_inc(t1_full, 1)
                    if g == S_ATT:
                        t1_free(T1_Q + DC)
                        pe.wait_ge(m1_done, n * M1 + M1_ATT)
                        for c in range(DC):
                            f = slice(c * P, (c + 1) * P)
                            for s in range(TT):
                                last = nc.tensor.matmul(m1_bank[0][:, f], V[:, s, f], H[:, s, f], start=(s == 0), stop=(s == TT - 1))
                        last.then_inc(m1_full, 1)
                        m1_free(M1_SUM)
                        for t in range(TT):
                            for c in range(DC):
                                i = t * H0 + c * (H0 // DC)
                                last = nc.tensor.matmul(m1_bank[1][:, i:i + H0 // DC], QT[:, c, t * P:(t + 1) * P],
                                                        blocks[:, 0, 0:P:DH0], start=True, stop=True)
                        last.then_inc(m1_full, 1)
                    if S_Y <= g < S_Y + TT // 2:
                        if g == S_Y:
                            pe.wait_ge(m1_done, n * M1 + M1_ATT + 1)
                        for t in range(2 * (g - S_Y), 2 * (g - S_Y) + 2):
                            m1_free(M1_Y + t)
                            for c in range(DC):
                                last = nc.tensor.matmul(m1_bank[t % 2][:, c * P:(c + 1) * P], QT[:, c, t * P:(t + 1) * P],
                                                        ATT[:, c, :], start=True, stop=True)
                            last.then_inc(m1_full, 1)
                    if g == S_TURN_Y:
                        pe.wait_ge(yhat, n * TT + TT)
                        for c in range(DC):
                            t1_free(T1_Y + c)
                            turn(t1_bank, H, c).then_inc(t1_full, 1)
                    if S_F <= g < S_F + TT:
                        t = g - S_F
                        if t == 0:
                            t1_free(T1_Y + DC)
                        m1_free(M1_F + t)
                        product(m1_bank[t % 2], lambda k: NT[:, k, t * P:(t + 1) * P], lambda k: W["film_out_W"][:, k, :]).then_inc(m1_full, 1)
                    if S_TURN_X1 <= g < S_TURN_X1 + DC // 2:
                        if g == S_TURN_X1:
                            pe.wait_ge(x1hat, n * TT + TT)
                        for c in range(2 * (g - S_TURN_X1), 2 * (g - S_TURN_X1) + 2):
                            t1_free(T1_X1 + c)
                            turn(t1_bank, H, c).then_inc(t1_full, 1)

                def l1(b, n):
                    pe.wait_ge(t1_done, (b + 1) * T1)
                    pe.wait_ge(o_done, b * O)
                    for i in range(2 * DC):
                        pe.wait_ge(t2_done, b * T2 + T2_QK + max(i - 1, 0))
                        product(qk_bank[i % 2], lambda k: wqkv[:, k, i * P:(i + 1) * P], lambda k: XM[:, k, :]).then_inc(t2_full, 1)
                    for t in range(TT):
                        if t == 1:
                            pe.wait_ge(t2_done, b * T2 + T2_QK + 2 * DC)
                        pe.wait_ge(o_done, b * O + O_V + max(t - 1, 0))
                        product(vp_bank[t % 2], lambda k: XM[:, k, t * P:(t + 1) * P], lambda k: wqkv[:, k, 2 * D:3 * D]).then_inc(o_full, 1)

                    def scores(h, t):
                        pe.wait_ge(pexp, b * SC + max(h * TT + t - 1, 0))
                        s = slice(h % 2 * DH1, h % 2 * DH1 + DH1)
                        nc.tensor.matmul(sc_bank[t % 2][:], Q2[s, h // 2, t * P:(t + 1) * P], K2[s, h // 2, :],
                                         start=True, stop=True).then_inc(sc_full, 1)

                    for t in range(TT):
                        scores(0, t)
                    pe.wait_ge(o_done, b * O + O_V + TT)
                    for h in range(H1):
                        for k in range(TT):
                            if h + 1 < H1:
                                scores(h + 1, k)
                            pe.wait_ge(pexp, b * SC + (h + 1) * TT)
                            pe.wait_ge(pt_done, b * PTN + h * TT + k)
                            for t in range(TT):
                                last = nc.tensor.transpose(pt_bank[:, t * P:(t + 1) * P], PR[:, h % 2, t, k * P:(k + 1) * P], ident[:])
                            last.then_inc(pt_full, 1)
                            if n is not None:
                                l0(n, h * TT + k)
                        pe.wait_ge(pt_done, b * PTN + (h + 1) * TT)
                        pe.wait_ge(o_done, b * O + O_PV + h)
                        for t in range(TT):
                            for k in range(TT):
                                last = nc.tensor.matmul(o_bank[:, t * DH1:(t + 1) * DH1], PT[:, k, t * P:(t + 1) * P],
                                                        V2[:, k, h * DH1:(h + 1) * DH1], start=(k == 0), stop=(k == TT - 1))
                        last.then_inc(o_full, 1)
                    pe.wait_ge(o_done, b * O + O_PV + H1)
                    for c in range(DC):
                        pe.wait_ge(t2_done, b * T2 + T2_O + c)
                        turn(t2_bank, H2, c).then_inc(t2_full, 1)
                    pe.wait_ge(t2_done, b * T2 + T2)
                    for t in range(TT):
                        pe.wait_ge(o_done, b * O + O_P + max(t - 1, 0))
                        product(vp_bank[t % 2], lambda k: Q2[:, k, t * P:(t + 1) * P], lambda k: wproj[:, k, :]).then_inc(o_full, 1)

                pe.wait_ge(w_in, 6 * 16)
                pe.wait_ge(blocks_done, P // DH0)
                l0_alone(l0, 0)
                with pe.Fori(0, B - 1) as b:
                    l1(b, b + 1)
                l1(B - 1, None)


def mix(nc, a, out, bank, ident, col, aneg, convw, x1_d, xm_d, attn_d, gate_d, b_d):
    ctx = ExitStack()
    with ctx:
        def sem(name):
            return ctx.enter_context(nc.semaphore(name))

        def sb(name, shape, dt=F32):
            return ctx.enter_context(nc.sbuf_tensor(name, shape, dt))

        w_io = sb("w_io", [P, DC, 2 * DI])
        w_x = sb("w_x", [P, IC, XD])
        w_dt = sb("w_dt", [RANK, DI])
        w_out = sb("w_out", [P, IC, D])
        w_full = sb("w_full", [P, 2 * DC, D])
        bias_full = sb("bias_full", [P, D])
        gate = sb("gate", [P, D])
        XM = sb("XM2", [P, DC * T])
        U = sb("U", [P, IC, T])
        DEL = sb("DEL", [P, IC * T])
        DU = sb("DU", [P, IC, T])
        brep = sb("brep", [P, 2, T])
        dA = sb("dA", [P, 2, QUAD, T])
        HS = sb("HS", [P, 2, QUAD, T])
        acc = sb("acc", [P, TT, DI])
        conv = sb("conv", [P, 2, T])
        tmp = sb("tmp", [P, 2, T])
        w1, lnw = sb("w1", [P, 2, T]), sb("lnw", [P, 2, T])
        xdbl = sb("xdbl", [XD, T])
        C = sb("C", [P, TT, N])
        stats = sb("stats2", [P, TT, 2, 6])
        mv, rs, rt, veps = sb("mv2", [P, TT, 2]), sb("rs2", [P, TT]), sb("rt2", [P, TT]), sb("veps2", [P, TT])
        spare = sb("spare2", [P, 1])
        xm = XM[:].rearrange("p (c t) -> p c t", t=T)
        x1 = XM[:].rearrange("p (t d) -> p t d", d=D)
        delta = DEL[:].rearrange("p (c t) -> p c t", t=T)
        comb = DEL[:].rearrange("p (t d) -> p t d", d=2 * D)

        win_in, w_in, gate_in = sem("win_in"), sem("w2_in"), sem("gate_in")
        xm_in, x1_in, attn_in = sem("xm_in"), sem("x1_in"), sem("attn_in")
        brep_in = [sem("brep_in0"), sem("brep_in1")]
        b_out, out_done = sem("b_out"), sem("out_done")
        fv_full, fv_done = sem("fv_full"), sem("fv_done")
        fa_full, fa_done = sem("fa_full"), sem("fa_done")
        conv0, u_done = sem("conv0"), sem("u_done")
        sp_abs, sp_exp, sp_w, sp_ln, du_done = sem("sp_abs"), sem("sp_exp"), sem("sp_w"), sem("sp_ln"), sem("du_done")
        acc_zero = sem("acc_zero")
        dA_done, dA_free, dbu_done = sem("dA_done"), sem("dA_free"), sem("dbu_done")
        yt_full, acc_done = sem("yt_full"), sem("acc_done")
        g_done = sem("g_done")
        ln_var, ln_ln, ln_r0, chat = sem("ln2_var"), sem("ln2_ln"), sem("ln2_r0"), sem("chat")
        silu_done, out_ready = sem("silu2_done"), sem("out_ready")
        own = sem("mix_dve")
        FV, FA = 34, 16
        FV_XR, FV_XD, FV_C, FV_DT, FV_Y, FV_O, FV_F = 0, 8, 9, 10, 18, 26, 30
        FA_Z, FA_C = 0, 8
        UNITS = N * IC // QUAD
        BODY = 4
        TURNS = UNITS // BODY
        y_bank, fv_bank, fa_bank = bank[0:4], bank[4:6], bank[6:8]

        with nc.Block() as block:

            @block.sync
            def _(sp):
                sp.dma_start(w_io[:], a["L1_cond_W_in"].rearrange("(c p) n -> p c n", p=P)).then_inc(win_in, 16)
                sp.dma_start(w_x[:], a["L1_cond_W_x"].rearrange("(c p) n -> p c n", p=P)).then_inc(w_in, 16)
                sp.dma_start(w_dt[:], a["L1_cond_W_dt"]).then_inc(w_in, 16)
                with sp.Fori(0, B) as b:
                    sp.wait_ge(out_ready, b * TT)
                    sp.dma_start(XM[:], xm_d[b].rearrange("p c t -> p (c t)")).then_inc(xm_in, 16)
                    sp.dma_start(gate[:], gate_d[bass.ds(b, 1), :].to_broadcast([P, D])).then_inc(gate_in, 16)
                    sp.wait_ge(fv_done, b * FV + FV_XD + 1)
                    sp.dma_start(b_d[b], xdbl[RANK:RANK + N, :]).then_inc(b_out, 16)

                    def load_b(n, slot, turn):
                        sp.dma_start(brep[:, slot, :], b_d[b, bass.ds(n, 1), :].to_broadcast([P, T])).then_inc(brep_in[slot], 16)

                    stored, used = sp.to_reg(b * 16 + 16), sp.to_reg(b * UNITS)
                    sp.wait_ge(b_out, stored)
                    sp.wait_ge(dbu_done, used)
                    for slot in range(2):
                        load_b(slot, slot, 0)
                    with sp.Fori(0, TURNS - 1) as m:
                        for slot in range(2):
                            sp.wait_ge(dbu_done, b * UNITS + m * BODY + 2 * slot + 2)
                            load_b(m * 2 + (2 + slot), slot, m + 1)
                    sp.wait_ge(fa_full, b * FA + FA_Z + IC)
                    sp.dma_start(x1, x1_d[b].rearrange("(t p) d -> p t d", p=P)).then_inc(x1_in, 16)
                    scaled, products = sp.to_reg((b + 1) * UNITS), sp.to_reg((b + 1) * IC)
                    sp.wait_ge(dA_done, scaled)
                    sp.wait_ge(du_done, products)
                    sp.dma_start(comb[:, :, D:2 * D], attn_d[b].rearrange("(t p) d -> p t d", p=P)).then_inc(attn_in, 16)
                    sp.wait_ge(out_ready, (b + 1) * TT)
                    sp.dma_start(out[b].rearrange("(t p) d -> p t d", p=P), acc[:, :, 0:D]).then_inc(out_done, 16)
                sp.wait_ge(out_done, B * 16)

            @block.gpsimd
            def _(pool):
                with pool.Fori(0, B) as b:
                    with pool.Fori(0, TURNS) as m:
                        for i in range(BODY):
                            slot, q = i // 2, i % 2
                            u = b * UNITS + m * BODY + i
                            pool.wait_ge(yt_full, u * TT)
                            if i < 2:
                                pool.wait_ge(du_done, (b + 1) * IC)
                            if q == 0:
                                pool.wait_ge(brep_in[slot], (b * TURNS + m) * 16 + 16)
                            nc.gpsimd.tensor_tensor(HS[:, q], DU[:, q * QUAD:(q + 1) * QUAD, :],
                                                    brep[:, slot, :].unsqueeze(1).to_broadcast([P, QUAD, T]),
                                                    ALU.mult).then_inc(dbu_done, 1)

            @block.scalar
            def _(act):
                act.dma_start(w_out[:], a["L1_cond_W_out"].rearrange("(c p) n -> p c n", p=P)).then_inc(w_in, 16)
                act.dma_start(w_full[:], a["L1_cond_W_full"].rearrange("(c p) n -> p c n", p=P)).then_inc(w_in, 16)
                act.dma_start(bias_full[:], a["L1_cond_b_full"].rearrange("(o n) -> o n", o=1).to_broadcast([P, D])).then_inc(w_in, 16)
                with act.Fori(0, B) as b:
                    for c in range(IC):
                        act.wait_ge(fv_full, b * FV + FV_XR + c + 1)
                        act.wait_ge(u_done, b * IC + max(c - 1, 0))
                        nc.scalar.activation(conv[:, c % 2, :], fv_bank[c % 2][:], ACT.Identity, scale=convw[:, c, TAPS - 1:TAPS],
                                             bias=col("L1_cond_b_conv", c)).then_inc(conv0, 1)
                        if c >= 1:
                            act.wait_ge(fv_done, b * FV + FV_XR + c)
                            nc.scalar.activation(U[:, c - 1, :], conv[:, (c - 1) % 2, :], ACT.Silu).then_inc(u_done, 1)
                    act.wait_ge(fv_done, b * FV + FV_XR + IC)
                    nc.scalar.activation(U[:, IC - 1, :], conv[:, (IC - 1) % 2, :], ACT.Silu).then_inc(u_done, 1)
                    for c in range(IC):
                        s = c % 2
                        act.wait_ge(fv_full, b * FV + FV_DT + c + 1)
                        act.wait_ge(du_done, b * IC + max(c - 1, 0))
                        nc.scalar.activation(tmp[:, s, :], fv_bank[s][:], ACT.Abs, bias=col("L1_cond_b_dt", c)).then_inc(sp_abs, 1)
                        nc.scalar.activation(conv[:, s, :], fv_bank[s][:], ACT.Relu, bias=col("L1_cond_b_dt", c)).then_inc(fv_done, 1)
                        act.wait_ge(sp_abs, b * IC + c + 1)
                        nc.scalar.activation(tmp[:, s, :], tmp[:, s, :], ACT.Exp, scale=-1.0).then_inc(sp_exp, 1)
                        act.wait_ge(sp_exp, b * IC + c + 1)
                        nc.scalar.activation(w1[:, s, :], tmp[:, s, :], ACT.Identity, bias=1.0).then_inc(sp_w, 1)
                        nc.scalar.activation(lnw[:, s, :], tmp[:, s, :], ACT.Ln, bias=1.0).then_inc(sp_ln, 1)
                    act.wait_ge(du_done, (b + 1) * IC)
                    with act.Fori(0, TURNS) as m:
                        for i in range(BODY):
                            q, n = i % 2, m * 2 + i // 2
                            act.wait_ge(dA_free, b * UNITS + m * BODY + i + 1)
                            for j in range(QUAD):
                                c = q * QUAD + j
                                last = nc.scalar.activation(dA[:, q, j, 1:T], delta[:, c, 1:T], ACT.Exp,
                                                            scale=aneg[:, c, bass.ds(n, 1)])
                            last.then_inc(dA_done, 1)
                    for c in range(IC):
                        act.wait_ge(fa_full, b * FA + FA_Z + c + 1)
                        act.wait_ge(g_done, b * IC + max(c - 1, 0))
                        nc.scalar.activation(tmp[:, c % 2, :], fa_bank[c % 2][:], ACT.Silu).then_inc(fa_done, 1)
                    act.wait_ge(ln_var, b + 1)
                    nc.scalar.activation(rt[:], veps[:], ACT.Ln).then_inc(ln_ln, 1)
                    act.wait_ge(ln_ln, b + 1)
                    nc.scalar.activation(rs[:], rt[:], ACT.Exp, scale=-0.5).then_inc(ln_r0, 1)
                    for c in range(2 * DC):
                        act.wait_ge(fa_full, b * FA + FA_C + c + 1)
                        nc.scalar.activation(DU[:, c, :], fa_bank[c % 2][:], ACT.Identity, scale=col("L1_cond_ln2_g", c),
                                             bias=col("L1_cond_ln2_b", c)).then_inc(fa_done, 1)
                    for t in range(TT):
                        act.wait_ge(fv_done, b * FV + FV_F + t + 1)
                        nc.scalar.activation(acc[:, t, 0:D], acc[:, t, 0:D], ACT.Silu).then_inc(silu_done, 1)

            @block.vector
            def _(dve):
                link = Link(dve, own, 5 * IC + 5 + TT)
                for q in range(2):
                    nc.vector.memset(dA[:, q, :, 0:1], 0.0).then_inc(dA_free, 1)
                dve.wait_ge(w_in, 5 * 16)
                with dve.Fori(0, B) as b:
                    link.begin(b)
                    for c in range(IC):
                        dve.wait_ge(conv0, b * IC + c + 1)
                        for k in range(TAPS - 1):
                            lag = TAPS - 1 - k
                            y = conv[:, c % 2, lag:T]
                            last = nc.vector.scalar_tensor_tensor(out=y, in0=fv_bank[c % 2][:, 0:T - lag], scalar=convw[:, c, k:k + 1],
                                                                  in1=y, op0=ALU.mult, op1=ALU.add)
                            if k < TAPS - 2:
                                link(last)
                        last.then_inc(fv_done, 1)
                    dve.wait_ge(fv_full, b * FV + FV_XD + 1)
                    dve.wait_ge(b_out, b * 16)
                    nc.vector.tensor_copy(xdbl[:], fv_bank[0][0:XD, :]).then_inc(fv_done, 1)
                    dve.wait_ge(fv_full, b * FV + FV_C + 1)
                    nc.vector.tensor_copy(C[:], fv_bank[1][:, 0:TT * XD].rearrange("p (t x) -> p t x", x=XD)[:, :, RANK + N:XD]).then_inc(fv_done, 1)

                    for c in range(IC):
                        s = c % 2
                        dve.wait_ge(sp_w, b * IC + c + 1)
                        link(nc.vector.scalar_tensor_tensor(out=w1[:, s, :], in0=w1[:, s, :], scalar=1.0, in1=tmp[:, s, :],
                                                            op0=ALU.subtract, op1=ALU.subtract))
                        dve.wait_ge(sp_ln, b * IC + c + 1)
                        link(nc.vector.tensor_tensor(lnw[:, s, :], lnw[:, s, :], w1[:, s, :], ALU.subtract))
                        dve.wait_ge(fv_done, b * FV + FV_DT + c + 1)
                        link(nc.vector.tensor_tensor(delta[:, c, :], lnw[:, s, :], conv[:, s, :], ALU.add))
                        nc.vector.tensor_tensor(DU[:, c, :], delta[:, c, :], U[:, c, :], ALU.mult).then_inc(du_done, 1)

                    def scan(u, q):
                        dve.wait_ge(dA_done, u + 1)
                        dve.wait_ge(dbu_done, u + 1)
                        h = HS[:, q].rearrange("p j t -> p (j t)")
                        nc.vector.tensor_tensor_scan(h, dA[:, q].rearrange("p j t -> p (j t)"), h, 0.0,
                                                     ALU.mult, ALU.add).then_inc(dA_free, 1)

                    def add(u, n, q):
                        for t in range(TT):
                            dve.wait_ge(yt_full, u * TT + (TT + t + 1))
                            y = acc[:, t, q * QUAD * P:(q + 1) * QUAD * P]
                            nc.vector.scalar_tensor_tensor(out=y, in0=y_bank[t][:], scalar=C[:, t, bass.ds(n, 1)], in1=y,
                                                           op0=ALU.mult, op1=ALU.add).then_inc(acc_done, 1)

                    def turn(m, last):
                        for i in range(BODY):
                            u = b * UNITS + m * BODY + i
                            if not (last and i == BODY - 1):
                                scan(u + 1, (i + 1) % 2)
                            add(u, m * 2 + i // 2, i % 2)

                    dve.wait_ge(out_done, b * 16)
                    nc.vector.memset(acc[:], 0.0).then_inc(acc_zero, 1)
                    dve.wait_ge(acc_zero, b + 1)
                    scan(b * UNITS, 0)
                    with dve.Fori(0, TURNS - 1) as m:
                        turn(m, False)
                    turn(TURNS - 1, True)
                    for c in range(IC):
                        dve.wait_ge(fv_full, b * FV + FV_Y + c + 1)
                        nc.vector.scalar_tensor_tensor(out=U[:, c, :], in0=U[:, c, :], scalar=col("L1_cond_D_param", c),
                                                       in1=fv_bank[c % 2][:], op0=ALU.mult, op1=ALU.add).then_inc(fv_done, 1)
                        dve.wait_ge(fv_done, b * FV + FV_Y + c + 1)
                        dve.wait_ge(fa_done, b * FA + FA_Z + c + 1)
                        nc.vector.tensor_tensor(U[:, c, :], U[:, c, :], tmp[:, c % 2, :], ALU.mult).then_inc(g_done, 1)
                    dve.wait_ge(attn_in, b * 16 + 16)
                    for t in range(TT):
                        dve.wait_ge(fv_full, b * FV + FV_O + t + 1)
                        nc.vector.tensor_copy(comb[:, t, 0:D], fv_bank[t % 2][:]).then_inc(fv_done, 1)
                    dve.wait_ge(fv_done, b * FV + FV_O + TT)
                    for t in range(TT):
                        for s in range(2):
                            last = nc.vector.bn_stats(stats[:, t, s, :], comb[:, t, s * D:(s + 1) * D])
                    link(last)
                    nc.vector.memset(spare[:], 0.0)
                    for t in range(TT):
                        last = nc.vector.bn_aggr(mv[:, t, :], stats[:, t].rearrange("p s k -> p (s k)"))
                    link(last)
                    nc.vector.tensor_scalar(veps[:], mv[:, :, 1], EPS, None, ALU.add).then_inc(ln_var, 1)
                    dve.wait_ge(ln_r0, b + 1)
                    link(nc.vector.tensor_tensor(rt[:], rs[:], rs[:], ALU.mult))
                    link(nc.vector.scalar_tensor_tensor(out=rt[:], in0=rt[:], scalar=-0.5, in1=veps[:], op0=ALU.mult, op1=ALU.mult))
                    link(nc.vector.scalar_tensor_tensor(out=rs[:], in0=rt[:], scalar=1.5, in1=rs[:], op0=ALU.add, op1=ALU.mult))
                    for t in range(TT):
                        nc.vector.tensor_scalar(comb[:, t, :], comb[:, t, :], mv[:, t, 0:1], rs[:, t:t + 1],
                                                ALU.subtract, ALU.mult).then_inc(chat, 1)
                    for t in range(TT):
                        dve.wait_ge(fv_full, b * FV + FV_F + t + 1)
                        nc.vector.tensor_tensor(acc[:, t, 0:D], fv_bank[t % 2][:], bias_full[:], ALU.add).then_inc(fv_done, 1)
                    dve.wait_ge(gate_in, b * 16 + 16)
                    dve.wait_ge(x1_in, b * 16 + 16)
                    for t in range(TT):
                        dve.wait_ge(silu_done, b * TT + t + 1)
                        link(nc.vector.tensor_tensor(acc[:, t, 0:D], acc[:, t, 0:D], gate[:], ALU.mult))
                        nc.vector.tensor_tensor(acc[:, t, 0:D], acc[:, t, 0:D], x1[:, t, :], ALU.add).then_inc(out_ready, 1)
                    link.end()

            @block.tensor
            def _(pe):
                pe.sem_inc(yt_full, TT)
                pe.wait_ge(win_in, 16)
                pe.wait_ge(w_in, 5 * 16)
                with pe.Fori(0, B) as b:
                    def fv_free(i):
                        pe.wait_ge(fv_done, b * FV + max(i - 1, 0))

                    def fa_free(i):
                        pe.wait_ge(fa_done, b * FA + max(i - 1, 0))

                    def product(dst, lhs, rhs, chunks):
                        for c in range(chunks):
                            last = nc.tensor.matmul(dst, lhs(c), rhs(c), start=(c == 0), stop=(c == chunks - 1))
                        return last

                    pe.wait_ge(xm_in, b * 16 + 16)
                    for c in range(IC):
                        fv_free(FV_XR + c)
                        product(fv_bank[c % 2][:], lambda k: w_io[:, k, c * P:(c + 1) * P], lambda k: xm[:, k, :], DC).then_inc(fv_full, 1)
                    pe.wait_ge(u_done, (b + 1) * IC)
                    fv_free(FV_XD)
                    product(fv_bank[0][0:XD, :], lambda k: w_x[:, k, :], lambda k: U[:, k, :], IC).then_inc(fv_full, 1)
                    pe.wait_ge(fv_done, b * FV + FV_XD + 1)
                    for t in range(TT):
                        last = nc.tensor.transpose(fv_bank[1][:, t * XD:(t + 1) * XD], xdbl[:, t * P:(t + 1) * P], ident[0:XD, 0:XD])
                    last.then_inc(fv_full, 1)
                    for c in range(IC):
                        pe.wait_ge(fv_done, b * FV + (FV_DT if c == 0 else FV_DT + c - 1))
                        nc.tensor.matmul(fv_bank[c % 2][:], w_dt[:, c * P:(c + 1) * P], xdbl[0:RANK, :], start=True, stop=True).then_inc(fv_full, 1)
                    with pe.Fori(0, TURNS) as m:
                        for i in range(BODY):
                            q, u = i % 2, b * UNITS + m * BODY + i
                            pe.wait_ge(dA_free, u + 3)
                            pe.wait_ge(acc_done, u * TT)
                            for t in range(TT):
                                for j in range(QUAD):
                                    last = nc.tensor.transpose(y_bank[t][:, j * P:(j + 1) * P], HS[:, q, j, t * P:(t + 1) * P], ident[:])
                                last.then_inc(yt_full, 1)
                    for c in range(IC):
                        fa_free(FA_Z + c)
                        product(fa_bank[c % 2][:], lambda k: w_io[:, k, DI + c * P:DI + (c + 1) * P], lambda k: xm[:, k, :], DC).then_inc(fa_full, 1)
                        pe.wait_ge(acc_done, (b + 1) * UNITS * TT)
                        fv_free(FV_Y + c)
                        for t in range(TT):
                            last = nc.tensor.transpose(fv_bank[c % 2][:, t * P:(t + 1) * P], acc[:, t, c * P:(c + 1) * P], ident[:])
                        last.then_inc(fv_full, 1)
                    pe.wait_ge(g_done, (b + 1) * IC)
                    for t in range(TT):
                        fv_free(FV_O + t)
                        product(fv_bank[t % 2][:], lambda k: U[:, k, t * P:(t + 1) * P], lambda k: w_out[:, k, :], IC).then_inc(fv_full, 1)
                    pe.wait_ge(chat, (b + 1) * TT)
                    for c in range(2 * DC):
                        fa_free(FA_C + c)
                        for t in range(TT):
                            last = nc.tensor.transpose(fa_bank[c % 2][:, t * P:(t + 1) * P], comb[:, t, c * P:(c + 1) * P], ident[:])
                        last.then_inc(fa_full, 1)
                    pe.wait_ge(fa_done, (b + 1) * FA)
                    for t in range(TT):
                        fv_free(FV_F + t)
                        product(fv_bank[t % 2][:], lambda k: DU[:, k, t * P:(t + 1) * P], lambda k: w_full[:, k, :], 2 * DC).then_inc(fv_full, 1)


_INS = ["x", "cond_2048", "mask_BxS_ik0"] + ["L0_cond_" + k for k in (
    "norm_scale norm_bias Wq bq Wk bk Wv bv film_emb_W film_emb_b film_norm_scale film_norm_bias film_out_W film_out_b").split()] + [
    "L1_cond_" + k for k in ("ln1_g ln1_b Wqkv bqkv Wproj bproj W_ada b_ada W_in W_conv b_conv W_x W_dt b_dt A_log D_param W_out "
                             "ln2_g ln2_b W_full b_full").split()]


def kernel(**inputs):
    import numpy as _np
    import concourse.bacc as _bacc
    from concourse import mybir as _mybir
    from concourse.bass_utils import run_bass_kernel_spmd as _run

    nc = _bacc.Bacc("TRN2", target_bir_lowering=False, num_devices=1)
    arrays, aps = {}, {}
    for name in _INS:
        v = _np.ascontiguousarray(inputs[name])
        arrays[f"in_{name}"] = v
        aps[name] = nc.dram_tensor(f"in_{name}", v.shape, _mybir.dt.from_np(v.dtype), kind="ExternalInput").ap()
    out = nc.dram_tensor("out", (B, T, D), F32, kind="ExternalOutput").ap()
    build(nc, aps, out)
    r = _run(nc, [arrays], core_ids=[0])
    return r.results[0]["out"]
```

```python
from contextlib import ExitStack

import numpy as np

import concourse.bass as bass
from concourse import mybir

ALU = mybir.AluOpType
ACT = mybir.ActivationFunctionType
F32 = mybir.dt.float32
I32 = mybir.dt.int32
AX = mybir.AxisListType.X

P = 128
B, T, D, E = 8, 512, 512, 1024
TT, DC, EC = T // P, D // P, E // P
H0, DH0 = 16, 32
H1, DH1 = 8, 64
DI, N, RANK, TAPS = 1024, 16, 64, 4
IC = DI // P
XD = RANK + 2 * N
EPS = 1e-5
MASKED = -float(2 ** 100)

VECTORS = [
    ("L0_cond_norm_scale", 0, DC), ("L0_cond_norm_bias", 0, DC), ("L0_cond_bk", 0, DC),
    ("L0_cond_film_norm_scale", 0, DC), ("L0_cond_film_norm_bias", 0, DC),
    ("L1_cond_ln1_g", 0, DC), ("L1_cond_ln1_b", 0, DC), ("L1_cond_bqkv", 0, 2 * DC),
    ("L1_cond_b_conv", 0, IC), ("L1_cond_b_dt", 0, IC), ("L1_cond_D_param", 0, IC),
    ("L1_cond_ln2_g", 0, 2 * DC), ("L1_cond_ln2_b", 0, 2 * DC),
]
COL, NCOL = {}, 0
for _name, _, _n in VECTORS:
    COL[_name] = NCOL
    NCOL += _n
FILM_A, FILM_B, LN1_A, LN1_B, VALID = (DC * i for i in range(5))
NCUR = VALID + TT


class Link:

    def __init__(self, eng, sem, per):
        self.eng, self.sem, self.per = eng, sem, per

    def begin(self, b, n=0):
        self.base, self.n = b * self.per, n

    def __call__(self, ins):
        ins.then_inc(self.sem, 1)
        self.n += 1
        self.eng.wait_ge(self.sem, self.base + self.n)

    def end(self):
        assert self.n == self.per, (self.n, self.per)


class Ring:

    def __init__(self, banks, full, emptied, uses):
        assert len(uses) % 2 == 0
        self.banks, self.full, self.emptied, self.uses = banks, full, emptied, uses
        self.names = [name for name, _ in uses]

    def bank(self, use):
        return self.banks[self.names.index(use) % 2]

    def at(self, b, use):
        return b * len(self.uses) + self.names.index(use) + 1

    def done(self, b, use):
        i = self.names.index(use)
        mine = [k for k, (_, e) in enumerate(self.uses) if e == self.uses[i][1]]
        return self.emptied[self.uses[i][1]], b * len(mine) + (mine.index(i) + 1)

    def wait_free(self, pe, b, use):
        i = self.names.index(use) - 2
        if i >= 0:
            pe.wait_ge(*self.done(b, self.names[i]))
        elif not (isinstance(b, int) and b == 0):
            mine = [k for k, (_, e) in enumerate(self.uses) if e == self.uses[i][1]]
            pe.wait_ge(self.emptied[self.uses[i][1]], b * len(mine) - (len(mine) - 1 - mine.index(len(self.uses) + i)))


def build(nc, a, out):
    ctx = ExitStack()
    with ctx:
        def sem(name, c=ctx):
            return c.enter_context(nc.semaphore(name))

        def sb(name, shape, dt=F32, c=ctx):
            return c.enter_context(nc.sbuf_tensor(name, shape, dt))

        x1_d = nc.dram_tensor("x1_d", (B, T, D), F32, kind="Internal").ap()
        xm_d = nc.dram_tensor("xm_d", (B, P, DC, T), F32, kind="Internal").ap()
        attn_d = nc.dram_tensor("attn_d", (B, T, D), F32, kind="Internal").ap()
        gate_d = nc.dram_tensor("gate_d", (B, D), F32, kind="Internal").ap()
        b_d = nc.dram_tensor("b_d", (B, N, T), F32, kind="Internal").ap()

        bank = [ctx.enter_context(nc.psum_tensor(f"bank{i}", [P, 512], F32)) for i in range(8)]

        ident = sb("ident", [P, P])
        cols = sb("cols", [P, NCOL])
        bq8 = sb("bq8", [P, DC])
        aneg = sb("aneg", [P, IC, N])
        convw = sb("convw", [P, IC, TAPS])
        per_batch = sb("per_batch", [P, B, NCUR])

        def col(name, c):
            return cols[:, COL[name] + c:COL[name] + c + 1]

        setup(nc, a, bank, ident, cols, bq8, aneg, convw, per_batch, gate_d)
        attend(nc, a, bank, ident, cols, col, bq8, per_batch, x1_d, xm_d, attn_d)
        mix(nc, a, out, bank, ident, col, aneg, convw, x1_d, xm_d, attn_d, gate_d, b_d)


def setup(nc, a, bank, ident, cols, bq8, aneg, convw, per_batch, gate_d):
    ctx = ExitStack()
    with ctx:
        def sem(name):
            return ctx.enter_context(nc.semaphore(name))

        def sb(name, shape, dt=F32):
            return ctx.enter_context(nc.sbuf_tensor(name, shape, dt))

        vecrows = sb("vecrows", [P, P])
        maskrows = sb("maskrows", [B * TT, P], I32)
        validrows = sb("validrows", [B * TT, P])
        cond = sb("cond", [B, E])
        scond = sb("scond", [B, E])
        condT = sb("condT", [P, EC, B])
        wfilm = sb("wfilm", [P, EC, 2 * D])
        wada = sb("wada", [P, EC, 3 * D])
        film_bias = sb("film_bias", [B, 2 * D])
        ada_bias = sb("ada_bias", [B, 3 * D])
        film = sb("film", [B, 2 * D])
        ada = sb("ada", [B, 3 * D])
        scale1 = sb("scale1", [P, 2, DC, B])
        zeros = sb("zeros", [P, P])

        vec_in, mask_in, cond_in = sem("vec_in"), sem("mask_in"), sem("cond_in")
        par_in, film_in, ada_in = sem("par_in"), sem("film_in"), sem("ada_in")
        zeroed, ident_done, silu_done = sem("zeroed"), sem("ident_done"), sem("silu_done")
        a_exp, valid_done = sem("a_exp"), sem("valid_done")
        turned, condT_done, cond_mm, rows_done = sem("turned"), sem("condT_done"), sem("cond_mm"), sem("rows_done")
        rows_turned, own = sem("rows_turned"), sem("setup_dve")
        gate_out = sem("gate_out")

        with nc.Block() as block:

            @block.sync
            def _(sp):
                sp.dma_start(cond[:], a["cond_2048"]).then_inc(cond_in, 16)
                for name, first, n in VECTORS:
                    src = a[name][first:first + n * P].rearrange("(c p) -> c p", p=P)
                    sp.dma_start(vecrows[COL[name]:COL[name] + n, :], src).then_inc(vec_in, 16)
                sp.dma_start(maskrows[:], a["mask_BxS_ik0"].rearrange("b (t p) -> (b t) p", p=P)).then_inc(mask_in, 16)
                sp.dma_start(wfilm[:], a["L0_cond_film_emb_W"].rearrange("(c p) n -> p c n", p=P)).then_inc(film_in, 16)
                sp.dma_start(film_bias[:], a["L0_cond_film_emb_b"].rearrange("(o n) -> o n", o=1).to_broadcast([B, 2 * D])).then_inc(film_in, 16)
                sp.wait_ge(rows_done, 5)
                sp.dma_start(gate_d, ada[:, 2 * D:3 * D]).then_inc(gate_out, 16)
                sp.wait_ge(gate_out, 16)

            @block.gpsimd
            def _(pool):
                nc.gpsimd.memset(zeros[:], 0.0).then_inc(zeroed, 1)
                pool.wait_ge(zeroed, 1)
                nc.gpsimd.affine_select(out=ident[:], in_=zeros[:], compare_op=ALU.not_equal, fill=1.0, base=0,
                                        pattern=[[-1, P]], channel_multiplier=1).then_inc(ident_done, 1)

            @block.scalar
            def _(act):
                act.dma_start(aneg[:], a["L1_cond_A_log"].rearrange("(c p) n -> p c n", p=P)).then_inc(par_in, 16)
                act.dma_start(convw[:], a["L1_cond_W_conv"].rearrange("(c p) o k -> p c (o k)", p=P)).then_inc(par_in, 16)
                act.dma_start(wada[:], a["L1_cond_W_ada"].rearrange("(c p) n -> p c n", p=P)).then_inc(ada_in, 16)
                act.dma_start(ada_bias[:], a["L1_cond_b_ada"].rearrange("(o n) -> o n", o=1).to_broadcast([B, 3 * D])).then_inc(ada_in, 16)
                act.wait_ge(cond_in, 16)
                nc.scalar.activation(scond[:], cond[:], ACT.Silu).then_inc(silu_done, 1)
                act.wait_ge(par_in, 32)
                nc.scalar.activation(aneg[:], aneg[:], ACT.Exp).then_inc(a_exp, 1)

            @block.tensor
            def _(pe):
                pe.wait_ge(ident_done, 1)
                pe.wait_ge(vec_in, 16 * len(VECTORS))
                nc.tensor.transpose(bank[0][:, 0:NCOL], vecrows[0:NCOL, :], ident[0:NCOL, 0:NCOL]).then_inc(turned, 1)
                pe.wait_ge(valid_done, 1)
                nc.tensor.transpose(bank[1][:, 0:B * TT], validrows[:], ident[0:B * TT, 0:B * TT]).then_inc(turned, 1)
                pe.wait_ge(silu_done, 1)
                for c in range(EC):
                    last = nc.tensor.transpose(bank[2][:, c * B:(c + 1) * B], scond[:, c * P:(c + 1) * P], ident[0:B, 0:B])
                last.then_inc(turned, 1)
                pe.wait_ge(condT_done, 1)
                for w, arrived, first, n in ((wfilm, film_in, 3, 2), (wada, ada_in, 5, 3)):
                    pe.wait_ge(arrived, 32)
                    for j in range(n):
                        for c in range(EC):
                            last = nc.tensor.matmul(bank[first + j][0:B, :], condT[:, c, :], w[:, c, j * D:(j + 1) * D],
                                                    start=(c == 0), stop=(c == EC - 1))
                        last.then_inc(cond_mm, 1)
                pe.wait_ge(rows_done, 5)
                for i in range(4 * DC):
                    src = film if i < 2 * DC else ada
                    j = i % (2 * DC)
                    last = nc.tensor.transpose(bank[0][:, i * B:(i + 1) * B], src[:, j * P:(j + 1) * P], ident[0:B, 0:B])
                last.then_inc(rows_turned, 1)

            @block.vector
            def _(dve):
                link = Link(dve, own, 100)
                link.begin(0)
                dve.wait_ge(mask_in, 16)
                nc.vector.tensor_scalar(validrows[:], maskrows[:], 1.0, None, ALU.not_equal).then_inc(valid_done, 1)
                dve.wait_ge(turned, 1)
                link(nc.vector.tensor_copy(cols[:], bank[0][:, 0:NCOL]))
                i = COL["L1_cond_bqkv"]
                nc.vector.tensor_scalar(bq8[:], cols[:, i:i + DC], DH1 ** -0.5, None, ALU.mult)
                dve.wait_ge(turned, 2)
                nc.vector.tensor_copy(per_batch[:, :, VALID:VALID + TT], bank[1][:, 0:B * TT].rearrange("p (b t) -> p b t", t=TT))
                dve.wait_ge(turned, 3)
                nc.vector.tensor_copy(condT[:], bank[2][:, 0:EC * B].rearrange("p (c b) -> p c b", b=B)).then_inc(condT_done, 1)
                dve.wait_ge(a_exp, 1)
                nc.vector.tensor_scalar(aneg[:], aneg[:], -1.0, None, ALU.mult)
                for j in range(5):
                    rows, bias, k = (film, film_bias, j) if j < 2 else (ada, ada_bias, j - 2)
                    dve.wait_ge(film_in if j < 2 else ada_in, 32)
                    dve.wait_ge(cond_mm, j + 1)
                    nc.vector.tensor_tensor(rows[:, k * D:(k + 1) * D], bank[3 + j][0:B, :], bias[:, k * D:(k + 1) * D],
                                            ALU.add).then_inc(rows_done, 1)
                dve.wait_ge(rows_turned, 1)
                t = bank[0][:, 0:4 * DC * B].rearrange("p (k c b) -> p k c b", k=4, b=B)
                for i, (g, bb, sc, sh, at_a, at_b) in enumerate((
                        ("L0_cond_film_norm_scale", "L0_cond_film_norm_bias", 0, 1, FILM_A, FILM_B),
                        ("L1_cond_ln1_g", "L1_cond_ln1_b", 3, 2, LN1_A, LN1_B))):
                    link(nc.vector.tensor_scalar(scale1[:, i], t[:, sc], 1.0, None, ALU.add))
                    for at, v in ((at_a, g), (at_b, bb)):
                        for c in range(DC):
                            last = nc.vector.tensor_scalar(per_batch[:, :, at + c], scale1[:, i, c, :],
                                                           cols[:, COL[v] + c:COL[v] + c + 1], None, ALU.mult)
                    link(last)
                    dst = per_batch[:, :, at_b:at_b + DC].rearrange("p b c -> p c b")
                    link(nc.vector.tensor_tensor(dst, dst, t[:, sh], ALU.add))


def attend(nc, a, bank, ident, cols, col, bq8, per_batch, x1_d, xm_d, attn_d):
    ctx = ExitStack()
    with ctx:
        def sem(name):
            return ctx.enter_context(nc.semaphore(name))

        def sb(name, shape, dt=F32):
            return ctx.enter_context(nc.sbuf_tensor(name, shape, dt))

        W = {}
        for name in ("Wk", "Wq", "Wv", "film_out_W"):
            W[name] = sb(name, [P, DC, D])
        wqkv = sb("wqkv", [P, DC, 3 * D])
        wproj = sb("wproj", [P, DC, D])
        bias = {k: sb(f"bias_{k}", [P, D]) for k in ("q", "v", "film", "v1", "proj")}
        X = sb("X", [P, TT, D])
        H = sb("H", [P, TT, D])
        NT = sb("NT", [P, DC, T])
        KT = sb("KT", [P, DC, T])
        Q = sb("Q", [P, TT, D])
        QT = sb("QT", [P, DC, T])
        V = sb("V", [P, TT, D])
        ATT = sb("ATT", [P, DC, P])
        blocks = sb("blocks", [P, DC, P])
        mask = sb("mask", [P, T], I32)
        mbias = sb("mbias", [P, T])
        nkmax, kden, kr = sb("nkmax", [P, DC]), sb("kden", [P, DC]), sb("kr", [P, DC])
        qmax, qr = sb("qmax", [P, TT, H0]), sb("qr", [P, TT, H0])
        cur = sb("cur", [P, NCUR])
        H2 = sb("H2", [P, TT, D])
        XM = sb("XM", [P, DC, T])
        Q2, K2 = sb("Q2", [P, DC, T]), sb("K2", [P, DC, T])
        V2 = sb("V2", [P, TT, D])
        PR = sb("PR", [P, 2, TT, T])
        PT = sb("PT", [P, TT, T])
        nsmax, rsum = sb("nsmax", [P, 2, TT]), sb("rsum", [P, H1, TT])
        rrec = sb("rrec", [P, H1, TT])
        stats = sb("stats", [P, TT, 6])
        mv, rs, rt = sb("mv", [P, TT, 2]), sb("rs", [P, TT]), sb("rt", [P, TT])
        veps, spare = sb("veps", [P, TT]), sb("spare", [P, 1])

        w_in = sem("w_in"); bias_in = sem("bias_in")
        x_in, mask_in = sem("x_in"), sem("mk_in")
        blocks_zero, blocks_done = sem("blocks_zero"), sem("blocks_done")
        cur_done, xb_done = sem("cur_done"), sem("xb_done")
        ln_var, ln_ln, ln_r0 = sem("ln_var"), sem("ln_ln"), sem("ln_r0")
        xhat, yhat, x1hat = sem("xhat"), sem("yhat"), sem("x1hat")
        t1_full, t1_done = sem("t1_full"), sem("t1_done")
        m1_full, m1_done = sem("m1_full"), sem("m1_done")
        kmax, kexp, knorm = sem("kmax"), sem("kexp"), sem("knorm")
        mbias_done, qsub = sem("mbias_done"), sem("qsub")
        t2_full, t2_done = sem("t2_full"), sem("t2_done")
        sc_full, smax, pexp = sem("sc_full"), sem("smax"), sem("pexp")
        pt_full, pt_done = sem("pt_full"), sem("pt_done")
        o_full, o_done = sem("o_full"), sem("o_done")
        x1_out, xm_out, attn_out = sem("x1_out"), sem("xm_out"), sem("attn_out")
        own0, own1 = sem("l0_dve"), sem("l1_dve")
        T1, M1, T2, SC, PTN, O = 20, 22, 12, H1 * TT, H1 * TT, 16
        T1_X, T1_E, T1_Q, T1_Y, T1_X1 = 0, 4, 8, 12, 16
        M1_K, M1_Q, M1_V, M1_ATT, M1_SUM, M1_Y, M1_F = 0, 4, 8, 12, 13, 14, 18
        T2_QK, T2_O = 0, 8
        O_V, O_PV, O_P = 0, 4, 12
        t1_bank, m1_bank, t2_bank, sc_bank, pt_bank, o_bank = bank[0], bank[1:3], bank[3], bank[4:6], bank[6], bank[7]
        qk_bank, vp_bank = (t2_bank, pt_bank), (o_bank, pt_bank)

        S_TURN_X, S_K, S_E, S_Q, S_V, S_TURN_Q, S_ATT, S_Y, S_NORM_Y, S_TURN_Y, S_F, S_NORM_X1, S_TURN_X1 = (
            0, 4, 9, 8, 12, 12, 16, 17, 19, 22, 23, 27, 29)
        SLOTS = H1 * TT

        def l0_alone(l0, n):
            for g in range(SLOTS):
                l0(n, g)

        with nc.Block() as block:

            @block.sync
            def _(sp):
                for name in ("Wk", "Wq", "Wv", "film_out_W"):
                    sp.dma_start(W[name][:], a["L0_cond_" + name].rearrange("(c p) n -> p c n", p=P)).then_inc(w_in, 16)
                sp.dma_start(wqkv[:], a["L1_cond_Wqkv"].rearrange("(c p) n -> p c n", p=P)).then_inc(w_in, 16)
                sp.dma_start(wproj[:], a["L1_cond_Wproj"].rearrange("(c p) n -> p c n", p=P)).then_inc(w_in, 16)
                def load(n, x1_stored, x1_normed, masked):
                    sp.wait_ge(x1_out, x1_stored)
                    sp.wait_ge(x1hat, x1_normed)
                    sp.dma_start(X[:], a["x"][n].rearrange("(t p) d -> p t d", p=P)).then_inc(x_in, 16)
                    sp.wait_ge(mbias_done, masked)
                    sp.dma_start(mask[:], a["mask_BxS_ik0"][bass.ds(n, 1), :].to_broadcast([P, T])).then_inc(mask_in, 16)

                def store_l0(n):
                    sp.wait_ge(m1_done, n * M1 + M1)
                    sp.dma_start(x1_d[n].rearrange("(t p) d -> p t d", p=P), X[:]).then_inc(x1_out, 16)
                    sp.wait_ge(t1_done, n * T1 + T1)
                    sp.dma_start(xm_d[n], XM[:]).then_inc(xm_out, 16)

                def store_l1(b):
                    sp.wait_ge(o_done, b * O + O)
                    sp.dma_start(attn_d[b].rearrange("(t p) d -> p t d", p=P), H2[:]).then_inc(attn_out, 16)

                load(0, 0, 0, 0)
                store_l0(0)
                with sp.Fori(0, B - 1) as b:
                    load(b + 1, sp.to_reg((b + 1) * 16), sp.to_reg((b + 1) * TT), b + 1)
                    store_l0(b + 1)
                    store_l1(b)
                store_l1(B - 1)
                sp.wait_ge(x1_out, B * 16)
                sp.wait_ge(xm_out, B * 16)
                sp.wait_ge(attn_out, B * 16)

            @block.gpsimd
            def _(pool):
                nc.gpsimd.memset(blocks[:], 0.0).then_inc(blocks_zero, 1)
                pool.wait_ge(blocks_zero, 1)
                for g in range(P // DH0):
                    s = slice(g * DH0, (g + 1) * DH0)
                    nc.gpsimd.memset(blocks[s, :, s], 1.0).then_inc(blocks_done, 1)
                pool.wait_ge(blocks_done, P // DH0)
                pool.wait_ge(bias_in, 5 * 16)
                with pool.Fori(0, B) as n:
                    pool.wait_ge(t1_done, n * T1)
                    nc.gpsimd.tensor_copy(cur[:], per_batch[:, n, :]).then_inc(cur_done, 1)
                    for t in range(TT):
                        pool.wait_ge(xhat, n * TT + t + 1)
                        nc.gpsimd.tensor_tensor(X[:, t, :], X[:, t, :], bias["film"][:], ALU.add).then_inc(xb_done, 1)

            @block.scalar
            def _(act):
                for k, (name, first) in {"q": ("L0_cond_bq", 0), "v": ("L0_cond_bv", 0), "film": ("L0_cond_film_out_b", 0),
                                         "v1": ("L1_cond_bqkv", 2 * D), "proj": ("L1_cond_bproj", 0)}.items():
                    src = a[name][first:first + D].rearrange("(o n) -> o n", o=1).to_broadcast([P, D])
                    act.dma_start(bias[k][:], src).then_inc(bias_in, 16)

                def inv_std(n, i):
                    act.wait_ge(ln_var, n * 3 + i + 1)
                    nc.scalar.activation(rt[:], veps[:], ACT.Ln).then_inc(ln_ln, 1)
                    act.wait_ge(ln_ln, n * 3 + i + 1)
                    nc.scalar.activation(rs[:], rt[:], ACT.Exp, scale=-0.5).then_inc(ln_r0, 1)

                def l0(n, g):
                    if S_TURN_X <= g < S_TURN_X + DC:
                        c = g - S_TURN_X
                        act.wait_ge(t1_full, n * T1 + T1_X + c + 1)
                        nc.scalar.activation(NT[:, c, :], t1_bank[:], ACT.Identity, scale=col("L0_cond_norm_scale", c),
                                             bias=col("L0_cond_norm_bias", c)).then_inc(t1_done, 1)
                    if S_K + 1 <= g < S_K + 1 + DC:
                        c = g - (S_K + 1)
                        act.wait_ge(kmax, n * DC + c + 1)
                        nc.scalar.activation(KT[:, c, :], KT[:, c, :], ACT.Exp, bias=nkmax[:, c:c + 1],
                                             accum_out=kden[:, c:c + 1]).then_inc(kexp, 1)
                    if S_E <= g < S_E + TT:
                        t = g - S_E
                        if t == 0:
                            act.wait_ge(cur_done, n + 1)
                        act.wait_ge(t1_full, n * T1 + T1_E + t + 1)
                        nc.scalar.activation(H[:, t, :], t1_bank[:], ACT.Identity,
                                             scale=cur[:, VALID + t:VALID + t + 1]).then_inc(t1_done, 1)
                    if S_TURN_Q <= g < S_TURN_Q + DC:
                        c = g - S_TURN_Q
                        act.wait_ge(t1_full, n * T1 + T1_Q + c + 1)
                        nc.scalar.activation(QT[:, c, :], t1_bank[:], ACT.Exp).then_inc(t1_done, 1)
                    if g == S_NORM_Y + 1:
                        inv_std(n, 1)
                    if g == S_TURN_Y:
                        for c in range(DC):
                            act.wait_ge(t1_full, n * T1 + T1_Y + c + 1)
                            nc.scalar.activation(NT[:, c, :], t1_bank[:], ACT.Silu, scale=cur[:, FILM_A + c:FILM_A + c + 1],
                                                 bias=cur[:, FILM_B + c:FILM_B + c + 1]).then_inc(t1_done, 1)
                    if g == S_NORM_X1 + 1:
                        inv_std(n, 2)
                    if S_TURN_X1 <= g < S_TURN_X1 + DC // 2:
                        if g == S_TURN_X1:
                            act.wait_ge(xm_out, n * 16)
                        for c in range(2 * (g - S_TURN_X1), 2 * (g - S_TURN_X1) + 2):
                            act.wait_ge(t1_full, n * T1 + T1_X1 + c + 1)
                            nc.scalar.activation(XM[:, c, :], t1_bank[:], ACT.Identity, scale=cur[:, LN1_A + c:LN1_A + c + 1],
                                                 bias=cur[:, LN1_B + c:LN1_B + c + 1]).then_inc(t1_done, 1)

                def l1(b, n):
                    for i in range(2 * DC):
                        if i == DC and n is not None:
                            inv_std(n, 0)
                        act.wait_ge(t2_full, b * T2 + T2_QK + i + 1)
                        if i < DC:
                            nc.scalar.activation(Q2[:, i, :], qk_bank[i % 2][:], ACT.Identity, scale=DH1 ** -0.5,
                                                 bias=bq8[:, i:i + 1]).then_inc(t2_done, 1)
                        else:
                            nc.scalar.activation(K2[:, i - DC, :], qk_bank[i % 2][:], ACT.Identity,
                                                 bias=col("L1_cond_bqkv", i)).then_inc(t2_done, 1)

                    def probabilities(h, t):
                        act.wait_ge(smax, b * SC + h * TT + t + 1)
                        if h >= 2 and t == 0:
                            act.wait_ge(pt_full, b * PTN + (h - 1) * TT)
                        nc.scalar.activation(PR[:, h % 2, t, :], sc_bank[t % 2][:], ACT.Exp, bias=nsmax[:, h % 2, t:t + 1],
                                             accum_out=rsum[:, h, t:t + 1]).then_inc(pexp, 1)

                    for t in range(TT):
                        probabilities(0, t)
                    for h in range(H1):
                        for k in range(TT):
                            if h + 1 < H1:
                                probabilities(h + 1, k)
                            if n is not None:
                                l0(n, h * TT + k)
                    for c in range(DC):
                        act.wait_ge(t2_full, b * T2 + T2_O + c + 1)
                        nc.scalar.activation(Q2[:, c, :], t2_bank[:], ACT.Identity).then_inc(t2_done, 1)

                inv_std(0, 0)
                l0_alone(l0, 0)
                with act.Fori(0, B - 1) as b:
                    l1(b, b + 1)
                l1(B - 1, None)

            @block.vector
            def _(dve):
                link0, link1 = Link(dve, own0, 3 * 5 + TT + 2), Link(dve, own1, H1)

                def variance(src):
                    for t in range(TT):
                        last = nc.vector.bn_stats(stats[:, t, :], src[:, t, :])
                    link0(last)
                    nc.vector.memset(spare[:], 0.0)
                    for t in range(TT):
                        last = nc.vector.bn_aggr(mv[:, t, :], stats[:, t, :])
                    link0(last)
                    nc.vector.tensor_scalar(veps[:], mv[:, :, 1], EPS, None, ALU.add).then_inc(ln_var, 1)

                def norm(n, i, src, dst, ready):
                    dve.wait_ge(ln_r0, n * 3 + i + 1)
                    link0(nc.vector.tensor_tensor(rt[:], rs[:], rs[:], ALU.mult))
                    link0(nc.vector.scalar_tensor_tensor(out=rt[:], in0=rt[:], scalar=-0.5, in1=veps[:], op0=ALU.mult, op1=ALU.mult))
                    link0(nc.vector.scalar_tensor_tensor(out=rs[:], in0=rt[:], scalar=1.5, in1=rs[:], op0=ALU.add, op1=ALU.mult))
                    for t in range(TT):
                        nc.vector.tensor_scalar(dst[:, t, :], src[:, t, :], mv[:, t, 0:1], rs[:, t:t + 1],
                                                ALU.subtract, ALU.mult).then_inc(ready, 1)

                def l0_begin(n):
                    link0.begin(n)
                    dve.wait_ge(x_in, n * 16 + 16)
                    variance(X)
                    dve.wait_ge(t1_full, n * T1)
                    norm(n, 0, X, H, xhat)

                def l0(n, g):
                    if g == S_TURN_X:
                        dve.wait_ge(mask_in, n * 16 + 16)
                        nc.vector.tensor_scalar(mbias[:], mask[:], 1.0, MASKED, ALU.is_equal, ALU.mult).then_inc(mbias_done, 1)
                    if S_K <= g < S_K + DC:
                        c = g - S_K
                        if c == 0:
                            dve.wait_ge(mbias_done, n + 1)
                        dve.wait_ge(m1_full, n * M1 + M1_K + c + 1)
                        nc.vector.scalar_tensor_tensor(out=KT[:, c, :], in0=m1_bank[c % 2][:], scalar=col("L0_cond_bk", c),
                                                       in1=mbias[:], op0=ALU.add, op1=ALU.add).then_inc(m1_done, 1)
                        dve.wait_ge(m1_done, n * M1 + M1_K + c + 1)
                        nc.vector.tensor_reduce(nkmax[:, c:c + 1], KT[:, c, :], AX, ALU.max, negate=True).then_inc(kmax, 1)
                    if S_Q <= g < S_Q + TT:
                        t = g - S_Q
                        dve.wait_ge(m1_full, n * M1 + M1_Q + t + 1)
                        nc.vector.tensor_tensor(Q[:, t, :], m1_bank[t % 2][:], bias["q"][:], ALU.add).then_inc(m1_done, 1)
                        dve.wait_ge(m1_done, n * M1 + M1_Q + t + 1)
                        heads = Q[:, t, :].rearrange("p (h d) -> p h d", d=DH0)
                        link0(nc.vector.tensor_reduce(qmax[:, t, :], heads, AX, ALU.max))
                        nc.vector.tensor_tensor(heads, heads, qmax[:, t, :].unsqueeze(2).to_broadcast([P, H0, DH0]),
                                                ALU.subtract).then_inc(qsub, 1)
                    if g == S_E - 1:
                        dve.wait_ge(kexp, n * DC + DC)
                        link0(nc.vector.scalar_tensor_tensor(out=kden[:], in0=nkmax[:], scalar=-MASKED / 2, in1=kden[:],
                                                             op0=ALU.is_lt, op1=ALU.mult))
                        link0(nc.vector.reciprocal(kr[:], kden[:]))
                        for c in range(DC):
                            nc.vector.tensor_scalar(KT[:, c, :], KT[:, c, :], kr[:, c:c + 1], None, ALU.mult).then_inc(knorm, 1)
                    if S_V <= g < S_V + TT:
                        t = g - S_V
                        dve.wait_ge(m1_full, n * M1 + M1_V + t + 1)
                        nc.vector.tensor_tensor(V[:, t, :], m1_bank[t % 2][:], bias["v"][:], ALU.add).then_inc(m1_done, 1)
                    if g == S_ATT:
                        dve.wait_ge(m1_full, n * M1 + M1_ATT + 1)
                        nc.vector.tensor_tensor(ATT[:], m1_bank[0][:].rearrange("p (c e) -> p c e", e=P), blocks[:],
                                                ALU.mult).then_inc(m1_done, 1)
                        dve.wait_ge(m1_full, n * M1 + M1_SUM + 1)
                        nc.vector.reciprocal(qr[:].rearrange("p t h -> p (t h)"), m1_bank[1][:, 0:TT * H0]).then_inc(m1_done, 1)
                    if S_Y <= g < S_Y + TT // 2:
                        if g == S_Y:
                            dve.wait_ge(m1_done, n * M1 + M1_SUM + 1)
                        for t in range(2 * (g - S_Y), 2 * (g - S_Y) + 2):
                            dve.wait_ge(m1_full, n * M1 + M1_Y + t + 1)
                            nc.vector.tensor_tensor(Q[:, t, :].rearrange("p (h d) -> p h d", d=DH0),
                                                    m1_bank[t % 2][:].rearrange("p (h d) -> p h d", d=DH0),
                                                    qr[:, t, :].unsqueeze(2).to_broadcast([P, H0, DH0]), ALU.mult).then_inc(m1_done, 1)
                    if g == S_NORM_Y:
                        dve.wait_ge(m1_done, n * M1 + M1_Y + TT)
                        variance(Q)
                    if g == S_NORM_Y + 1:
                        norm(n, 1, Q, H, yhat)
                    if S_F <= g < S_F + TT:
                        t = g - S_F
                        if t == 0:
                            dve.wait_ge(xb_done, n * TT + TT)
                        dve.wait_ge(m1_full, n * M1 + M1_F + t + 1)
                        nc.vector.tensor_tensor(X[:, t, :], m1_bank[t % 2][:], X[:, t, :], ALU.add).then_inc(m1_done, 1)
                    if g == S_NORM_X1:
                        dve.wait_ge(m1_done, n * M1 + M1)
                        variance(X)
                    if g == S_NORM_X1 + 1:
                        norm(n, 2, X, H, x1hat)
                        link0.end()

                def l1(b, n):
                    link1.begin(b)
                    if n is not None:
                        l0_begin(n)
                    for t in range(TT):
                        dve.wait_ge(o_full, b * O + O_V + t + 1)
                        nc.vector.tensor_tensor(V2[:, t, :], vp_bank[t % 2][:], bias["v1"][:], ALU.add).then_inc(o_done, 1)

                    def score_max(h, t):
                        dve.wait_ge(sc_full, b * SC + h * TT + t + 1)
                        nc.vector.tensor_reduce(nsmax[:, h % 2, t:t + 1], sc_bank[t % 2][:], AX, ALU.max, negate=True).then_inc(smax, 1)

                    def head_out(h):
                        dve.wait_ge(pexp, b * SC + (h + 1) * TT)
                        link1(nc.vector.reciprocal(rrec[:, h, :], rsum[:, h, :]))
                        dve.wait_ge(o_full, b * O + O_PV + h + 1)
                        nc.vector.tensor_tensor(H2[:, :, h * DH1:(h + 1) * DH1],
                                                o_bank[:, 0:TT * DH1].rearrange("p (t d) -> p t d", d=DH1),
                                                rrec[:, h, :].unsqueeze(2).to_broadcast([P, TT, DH1]), ALU.mult).then_inc(o_done, 1)

                    for t in range(TT):
                        score_max(0, t)
                    dve.wait_ge(attn_out, b * 16)
                    for h in range(H1):
                        for k in range(TT):
                            if h + 1 < H1:
                                score_max(h + 1, k)
                            if h >= 1 and k == 0:
                                dve.wait_ge(o_full, b * O + O_PV + h)
                            dve.wait_ge(pt_full, b * PTN + h * TT + k + 1)
                            nc.vector.tensor_copy(PT[:, k, :], pt_bank[:]).then_inc(pt_done, 1)
                            if h >= 1 and k == 0:
                                head_out(h - 1)
                            if n is not None:
                                l0(n, h * TT + k)
                    head_out(H1 - 1)
                    dve.wait_ge(t2_full, b * T2 + T2)
                    for t in range(TT):
                        dve.wait_ge(o_full, b * O + O_P + t + 1)
                        nc.vector.tensor_tensor(H2[:, t, :], vp_bank[t % 2][:], bias["proj"][:], ALU.add).then_inc(o_done, 1)
                    link1.end()

                dve.wait_ge(bias_in, 5 * 16)
                dve.wait_ge(blocks_done, P // DH0)
                l0_begin(0)
                l0_alone(l0, 0)
                with dve.Fori(0, B - 1) as b:
                    l1(b, b + 1)
                l1(B - 1, None)

            @block.tensor
            def _(pe):
                def turn(dst, src, c):
                    for t in range(TT):
                        last = nc.tensor.transpose(dst[:, t * P:(t + 1) * P], src[:, t, c * P:(c + 1) * P], ident[:])
                    return last

                def product(dst, lhs, rhs):
                    for c in range(DC):
                        last = nc.tensor.matmul(dst[:], lhs(c), rhs(c), start=(c == 0), stop=(c == DC - 1))
                    return last

                def l0(n, g):
                    def m1_free(i):
                        pe.wait_ge(m1_done, n * M1 + max(i - 1, 0))

                    def t1_free(i):
                        pe.wait_ge(t1_done, n * T1 + i)

                    if S_TURN_X <= g < S_TURN_X + DC:
                        if g == S_TURN_X:
                            pe.wait_ge(xhat, n * TT + TT)
                        t1_free(T1_X + g - S_TURN_X)
                        turn(t1_bank, H, g - S_TURN_X).then_inc(t1_full, 1)
                    if S_E <= g < S_E + TT:
                        t = g - S_E
                        if t == 0:
                            pe.wait_ge(knorm, n * DC + DC)
                        t1_free(T1_E + t)
                        for c in range(DC):
                            last = nc.tensor.transpose(t1_bank[:, c * P:(c + 1) * P], KT[:, c, t * P:(t + 1) * P], ident[:])
                        last.then_inc(t1_full, 1)
                    if S_K <= g < S_K + DC:
                        c = g - S_K
                        if c == 0:
                            t1_free(T1_X + DC)
                        m1_free(M1_K + c)
                        product(m1_bank[c % 2], lambda k: W["Wk"][:, k, c * P:(c + 1) * P], lambda k: NT[:, k, :]).then_inc(m1_full, 1)
                    for s, i, w in ((S_Q, M1_Q, "Wq"), (S_V, M1_V, "Wv")):
                        if s <= g < s + TT:
                            t = g - s
                            m1_free(i + t)
                            product(m1_bank[t % 2], lambda k: NT[:, k, t * P:(t + 1) * P], lambda k: W[w][:, k, :]).then_inc(m1_full, 1)
                    if S_TURN_Q <= g < S_TURN_Q + DC:
                        c = g - S_TURN_Q
                        if c == 0:
                            pe.wait_ge(qsub, n * TT + TT)
                        t1_free(T1_Q + c)
                        turn(t1_bank, Q, c).then_inc(t1_full, 1)
                    if g == S_ATT:
                        t1_free(T1_Q + DC)
                        pe.wait_ge(m1_done, n * M1 + M1_ATT)
                        for c in range(DC):
                            f = slice(c * P, (c + 1) * P)
                            for s in range(TT):
                                last = nc.tensor.matmul(m1_bank[0][:, f], V[:, s, f], H[:, s, f], start=(s == 0), stop=(s == TT - 1))
                        last.then_inc(m1_full, 1)
                        m1_free(M1_SUM)
                        for t in range(TT):
                            for c in range(DC):
                                i = t * H0 + c * (H0 // DC)
                                last = nc.tensor.matmul(m1_bank[1][:, i:i + H0 // DC], QT[:, c, t * P:(t + 1) * P],
                                                        blocks[:, 0, 0:P:DH0], start=True, stop=True)
                        last.then_inc(m1_full, 1)
                    if S_Y <= g < S_Y + TT // 2:
                        if g == S_Y:
                            pe.wait_ge(m1_done, n * M1 + M1_ATT + 1)
                        for t in range(2 * (g - S_Y), 2 * (g - S_Y) + 2):
                            m1_free(M1_Y + t)
                            for c in range(DC):
                                last = nc.tensor.matmul(m1_bank[t % 2][:, c * P:(c + 1) * P], QT[:, c, t * P:(t + 1) * P],
                                                        ATT[:, c, :], start=True, stop=True)
                            last.then_inc(m1_full, 1)
                    if g == S_TURN_Y:
                        pe.wait_ge(yhat, n * TT + TT)
                        for c in range(DC):
                            t1_free(T1_Y + c)
                            turn(t1_bank, H, c).then_inc(t1_full, 1)
                    if S_F <= g < S_F + TT:
                        t = g - S_F
                        if t == 0:
                            t1_free(T1_Y + DC)
                        m1_free(M1_F + t)
                        product(m1_bank[t % 2], lambda k: NT[:, k, t * P:(t + 1) * P], lambda k: W["film_out_W"][:, k, :]).then_inc(m1_full, 1)
                    if S_TURN_X1 <= g < S_TURN_X1 + DC // 2:
                        if g == S_TURN_X1:
                            pe.wait_ge(x1hat, n * TT + TT)
                        for c in range(2 * (g - S_TURN_X1), 2 * (g - S_TURN_X1) + 2):
                            t1_free(T1_X1 + c)
                            turn(t1_bank, H, c).then_inc(t1_full, 1)

                def l1(b, n):
                    pe.wait_ge(t1_done, (b + 1) * T1)
                    pe.wait_ge(o_done, b * O)
                    for i in range(2 * DC):
                        pe.wait_ge(t2_done, b * T2 + T2_QK + max(i - 1, 0))
                        product(qk_bank[i % 2], lambda k: wqkv[:, k, i * P:(i + 1) * P], lambda k: XM[:, k, :]).then_inc(t2_full, 1)
                    for t in range(TT):
                        if t == 1:
                            pe.wait_ge(t2_done, b * T2 + T2_QK + 2 * DC)
                        pe.wait_ge(o_done, b * O + O_V + max(t - 1, 0))
                        product(vp_bank[t % 2], lambda k: XM[:, k, t * P:(t + 1) * P], lambda k: wqkv[:, k, 2 * D:3 * D]).then_inc(o_full, 1)

                    def scores(h, t):
                        pe.wait_ge(pexp, b * SC + max(h * TT + t - 1, 0))
                        s = slice(h % 2 * DH1, h % 2 * DH1 + DH1)
                        nc.tensor.matmul(sc_bank[t % 2][:], Q2[s, h // 2, t * P:(t + 1) * P], K2[s, h // 2, :],
                                         start=True, stop=True).then_inc(sc_full, 1)

                    for t in range(TT):
                        scores(0, t)
                    pe.wait_ge(o_done, b * O + O_V + TT)
                    for h in range(H1):
                        for k in range(TT):
                            if h + 1 < H1:
                                scores(h + 1, k)
                            pe.wait_ge(pexp, b * SC + (h + 1) * TT)
                            pe.wait_ge(pt_done, b * PTN + h * TT + k)
                            for t in range(TT):
                                last = nc.tensor.transpose(pt_bank[:, t * P:(t + 1) * P], PR[:, h % 2, t, k * P:(k + 1) * P], ident[:])
                            last.then_inc(pt_full, 1)
                            if n is not None:
                                l0(n, h * TT + k)
                        pe.wait_ge(pt_done, b * PTN + (h + 1) * TT)
                        pe.wait_ge(o_done, b * O + O_PV + h)
                        for t in range(TT):
                            for k in range(TT):
                                last = nc.tensor.matmul(o_bank[:, t * DH1:(t + 1) * DH1], PT[:, k, t * P:(t + 1) * P],
                                                        V2[:, k, h * DH1:(h + 1) * DH1], start=(k == 0), stop=(k == TT - 1))
                        last.then_inc(o_full, 1)
                    pe.wait_ge(o_done, b * O + O_PV + H1)
                    for c in range(DC):
                        pe.wait_ge(t2_done, b * T2 + T2_O + c)
                        turn(t2_bank, H2, c).then_inc(t2_full, 1)
                    pe.wait_ge(t2_done, b * T2 + T2)
                    for t in range(TT):
                        pe.wait_ge(o_done, b * O + O_P + max(t - 1, 0))
                        product(vp_bank[t % 2], lambda k: Q2[:, k, t * P:(t + 1) * P], lambda k: wproj[:, k, :]).then_inc(o_full, 1)

                pe.wait_ge(w_in, 6 * 16)
                pe.wait_ge(blocks_done, P // DH0)
                l0_alone(l0, 0)
                with pe.Fori(0, B - 1) as b:
                    l1(b, b + 1)
                l1(B - 1, None)


def mix(nc, a, out, bank, ident, col, aneg, convw, x1_d, xm_d, attn_d, gate_d, b_d):
    ctx = ExitStack()
    with ctx:
        def sem(name):
            return ctx.enter_context(nc.semaphore(name))

        def sb(name, shape, dt=F32):
            return ctx.enter_context(nc.sbuf_tensor(name, shape, dt))

        HC, UC = IC // 2, IC // 4
        UNITS = 2 * N
        TURNED = (N + 1) * TT

        w_io = sb("w_io", [P, DC, 2 * DI])
        w_x = sb("w_x", [P, IC, XD])
        w_dt = sb("w_dt", [RANK, DI])
        w_out = sb("w_out", [P, IC, D])
        w_full = sb("w_full", [P, 2 * DC, D])
        bias_full = sb("bias_full", [P, D])
        gate = sb("gate", [P, D])
        XM = sb("XM2", [P, DC, T])
        U = sb("U", [P, IC, T])
        G = sb("G", [P, IC, T])
        ZS = sb("ZS", [P, HC, T])
        delta = sb("delta", [P, IC, T])
        DU = sb("DU", [P, IC, T])
        brep = sb("brep", [P, 2, T])
        dA = sb("dA", [P, 2, UC, T])
        HS = sb("HS", [P, 2, UC, T])
        acc = sb("acc", [P, TT, HC * P])
        comb = sb("comb", [P, 2, 2 * D])
        e_abs, relu = sb("e_abs", [P, T]), sb("relu", [P, T])
        w1, lnw = sb("w1", [P, T]), sb("lnw", [P, T])
        xdbl = sb("xdbl", [XD, T])
        C = sb("C", [P, TT, N])
        stats = sb("stats2", [P, TT, 2, 6])
        mv, rs, rt, veps = sb("mv2", [P, TT, 2]), sb("rs2", [P, TT]), sb("rt2", [P, TT]), sb("veps2", [P, TT])
        spare = sb("spare2", [P, 1])

        win_in, w_in, gate_in, xm_in = sem("win_in"), sem("w2_in"), sem("gate_in"), sem("xm_in")
        attn_in, x1_in, out_done, brep_in = ([sem(f"{k}{i}") for i in range(2)] for k in ("attn_in", "x1_in", "out_done", "brep_in"))
        b_out = sem("b_out")
        conv0, u_done = sem("conv0"), sem("u_done")
        sp_abs, sp_exp, sp_w, sp_ln, du_done = sem("sp_abs"), sem("sp_exp"), sem("sp_w"), sem("sp_ln"), sem("du_done")
        zeroed, ud_done, g_done = sem("zeroed"), sem("ud_done"), sem("g_done")
        dA_done, scanned, dbu_done = sem("dA_done"), sem("scanned"), sem("dbu_done")
        turned0 = sem("turned0")
        yt_full, acc_done = sem("yt_full"), sem("acc_done")
        ln_var, ln_ln, ln_r0, chat = sem("ln2_var"), sem("ln2_ln"), sem("ln2_r0"), sem("chat")
        silu_done, out_ready = sem("silu2_done"), sem("out_ready")
        own_front, own_delta, own_tail = sem("front_dve"), sem("delta_dve"), sem("tail_dve")

        y_bank = bank[0:4]
        S_O, S_NORM, S_CT, S_F, S_OUT, EVERY = 1, 3, 4, 5, 7, 3
        S_DELTA1 = {3: 4, 6: 5, 9: 6, 12: 7}
        S_Z0, S_Z1 = {3: (0, 1), 13: (2, 3)}, {1: (4, 5), 2: (6, 7)}
        S_XR, S_XD = {4: (0, 1), 5: (2, 3), 6: (4, 5), 7: (6, 7)}, 9
        S_DELTA0 = {10: 0, 11: 1, 12: 2, 13: 3}
        FRONT = range(min(S_XR), max(S_DELTA0) + 2)

        def s_out(t):
            return min(S_OUT + EVERY * t, N - 1)

        fv = Ring(bank[4:6], sem("fv_full"), {"act": sem("fv_act"), "dve": sem("fv_dve")},
                  [(f"xr{c}", "dve") for c in range(IC)] + [("xd", "dve")] + [(f"dt{c}", "act") for c in range(4)] + [("C", "dve")]
                  + [(k, "act") for k in ("dt4", "z0", "z1", "dt5", "dt6", "dt7", "z2", "z3", "z4", "z5", "z6", "z7")])
        ta = Ring(bank[6:8], sem("ta_full"), {"act": sem("ta_act"), "dve": sem("ta_dve")},
                  [("o0", "dve"), ("c0a", "act"), ("c0b", "act"), ("o1", "dve"), ("f0", "dve"), ("c1a", "act"), ("c1b", "act"),
                   ("o2", "dve"), ("f1", "dve"), ("c2a", "act"), ("c2b", "act"), ("o3", "dve"), ("f2", "dve"), ("c3a", "act"),
                   ("c3b", "act"), ("f3", "dve")])

        def first(j):
            return isinstance(j, int) and j == 0

        with nc.Block() as block:

            @block.sync
            def _(sp):
                def load_xm(n):
                    sp.dma_start(XM[:], xm_d[n]).then_inc(xm_in, 16)

                def store_b(n):
                    sp.wait_ge(*fv.done(n, "xd"))
                    sp.dma_start(b_d[n], xdbl[RANK:RANK + N, :]).then_inc(b_out, 16)

                def load_row(j, b, n, new_batch):
                    used = None if first(j) and n < 2 else sp.to_reg(j * UNITS + 2 * n - 2)
                    if new_batch:
                        stored = sp.to_reg((b + 1) * 16)
                        sp.wait_ge(b_out, stored)
                    if used is not None:
                        sp.wait_ge(dbu_done, used)
                    sp.dma_start(brep[:, n % 2, :], b_d[b, n:n + 1, :].to_broadcast([P, T])).then_inc(brep_in[n % 2], 16)

                def load_attn(p, t):
                    sp.dma_start(comb[:, t % 2, D:2 * D], attn_d[p, t * P:(t + 1) * P, :]).then_inc(attn_in[t % 2], 16)

                def tail(p, g):
                    if g == 0:
                        sp.wait_ge(out_ready, p * TT)
                        sp.dma_start(gate[:], gate_d[bass.ds(p, 1), :].to_broadcast([P, D])).then_inc(gate_in, 16)
                        for t in range(2):
                            load_attn(p, t)
                    for t in range(TT):
                        if g == S_CT + EVERY * t:
                            sp.wait_ge(ta.full, ta.at(p, f"c{t}b"))
                            sp.dma_start(comb[:, t % 2, D:2 * D], x1_d[p, t * P:(t + 1) * P, :]).then_inc(x1_in[t % 2], 16)
                    for t in range(TT):
                        if g == s_out(t):
                            sp.wait_ge(out_ready, p * TT + t + 1)
                            sp.dma_start(out[p, t * P:(t + 1) * P, :], comb[:, t % 2, 0:D]).then_inc(out_done[t % 2], 16)
                            if t + 2 < TT:
                                load_attn(p, t + 2)

                def half0(b, p):
                    for g in range(N):
                        load_row(b * 2 + (g + 2) // N, b, (g + 2) % N, False)
                        if p is not None:
                            tail(p, g)

                def half1(b, n):
                    for g in range(N):
                        if g + 2 < N:
                            load_row(b * 2 + 1, b, g + 2, False)
                        elif n is not None:
                            load_row(n * 2, n, g + 2 - N, True)
                        if n is not None and g == max(S_Z1):
                            sp.wait_ge(fv.full, fv.at(b, "z7"))
                            load_xm(n)
                        if n is not None and g == S_XD:
                            store_b(n)

                sp.dma_start(w_io[:], a["L1_cond_W_in"].rearrange("(c p) n -> p c n", p=P)).then_inc(win_in, 16)
                load_xm(0)
                sp.dma_start(w_x[:], a["L1_cond_W_x"].rearrange("(c p) n -> p c n", p=P)).then_inc(w_in, 16)
                sp.dma_start(w_dt[:], a["L1_cond_W_dt"]).then_inc(w_in, 16)
                store_b(0)
                for r in range(2):
                    load_row(0, 0, r, True)
                half0(0, None)
                with sp.Fori(0, B - 1) as b:
                    half1(b, b + 1)
                    half0(b + 1, b)
                half1(B - 1, None)
                for g in range(N):
                    tail(B - 1, g)
                for t in range(2):
                    sp.wait_ge(out_done[t], B * TT // 2 * 16)

            @block.gpsimd
            def _(pool):
                def half(j):
                    for n in range(N):
                        for s in range(2):
                            if s == 0 and not (first(j) and n == 0):
                                pool.wait_ge(turned0, j * N + n)
                            if s == 1 and not (first(j) and n == 0):
                                pool.wait_ge(yt_full, j * TURNED + n * TT if n else j * TURNED - TT)
                            if n == 0:
                                pool.wait_ge(du_done, j * HC + HC)
                            if s == 0:
                                pool.wait_ge(brep_in[n % 2], (j * (N // 2) + n // 2) * 16 + 16)
                            c = chunk(j, s)
                            nc.gpsimd.tensor_tensor(HS[:, s], DU[:, c:c + UC, :], brep[:, n % 2, :].unsqueeze(1).to_broadcast([P, UC, T]),
                                                    ALU.mult).then_inc(dbu_done, 1)

                def chunk(j, s):
                    return q * HC + s * UC

                q = 0
                half(0)
                with pool.Fori(0, B - 1) as b:
                    q = 1
                    half(b * 2 + 1)
                    q = 0
                    half(b * 2 + 2)
                q = 1
                half(2 * B - 1)

            @block.scalar
            def _(act):
                def decay(j, q, n):
                    if n == 0:
                        act.wait_ge(du_done, j * HC + HC)
                    for s in range(2):
                        if not (first(j) and n == 0):
                            act.wait_ge(scanned, j * UNITS + 2 * n + s - 1)
                        for i in range(UC):
                            c = q * HC + s * UC + i
                            last = nc.scalar.activation(dA[:, s, i, 1:T], delta[:, c, 1:T], ACT.Exp, scale=aneg[:, c, n:n + 1])
                        last.then_inc(dA_done, 1)

                def softplus(n, c):
                    act.wait_ge(fv.full, fv.at(n, f"dt{c}"))
                    act.wait_ge(du_done, n * IC + c)
                    x, b_dt = fv.bank(f"dt{c}"), col("L1_cond_b_dt", c)
                    nc.scalar.activation(e_abs[:], x[:], ACT.Abs, bias=b_dt).then_inc(sp_abs, 1)
                    nc.scalar.activation(relu[:], x[:], ACT.Relu, bias=b_dt).then_inc(fv.emptied["act"], 1)
                    act.wait_ge(sp_abs, n * IC + c + 1)
                    nc.scalar.activation(e_abs[:], e_abs[:], ACT.Exp, scale=-1.0).then_inc(sp_exp, 1)
                    act.wait_ge(sp_exp, n * IC + c + 1)
                    nc.scalar.activation(w1[:], e_abs[:], ACT.Identity, bias=1.0).then_inc(sp_w, 1)
                    nc.scalar.activation(lnw[:], e_abs[:], ACT.Ln, bias=1.0).then_inc(sp_ln, 1)

                def silu_z(b, c):
                    if c < HC:
                        act.wait_ge(g_done, b * IC)
                    else:
                        act.wait_ge(g_done, b * IC + (c - HC + 1))
                    act.wait_ge(fv.full, fv.at(b, f"z{c}"))
                    nc.scalar.activation(ZS[:, c % HC, :], fv.bank(f"z{c}")[:], ACT.Silu).then_inc(fv.emptied["act"], 1)

                def front(n, g):
                    if g - 1 in S_XR:
                        for c in S_XR[g - 1]:
                            act.wait_ge(*fv.done(n, f"xr{c}"))
                            nc.scalar.activation(U[:, c, :], U[:, c, :], ACT.Silu).then_inc(u_done, 1)
                    if g in S_XR:
                        for c in S_XR[g]:
                            if c == 0 and not first(n):
                                act.wait_ge(du_done, n * IC)
                                act.wait_ge(acc_done, (n * 2 - 1) * TURNED)
                            if c == HC and not first(n):
                                act.wait_ge(ud_done, n * HC)
                            act.wait_ge(fv.full, fv.at(n, f"xr{c}"))
                            nc.scalar.activation(U[:, c, :], fv.bank(f"xr{c}")[:], ACT.Identity, scale=convw[:, c, TAPS - 1:TAPS],
                                                 bias=col("L1_cond_b_conv", c)).then_inc(conv0, 1)
                    if g in S_DELTA0:
                        softplus(n, S_DELTA0[g])

                def tail(p, g):
                    for t in range(TT):
                        if g == S_NORM + EVERY * t:
                            act.wait_ge(ln_var, p * TT + t + 1)
                            nc.scalar.activation(rt[:, t:t + 1], veps[:, t:t + 1], ACT.Ln).then_inc(ln_ln, 1)
                            act.wait_ge(ln_ln, p * TT + t + 1)
                            nc.scalar.activation(rs[:, t:t + 1], rt[:, t:t + 1], ACT.Exp, scale=-0.5).then_inc(ln_r0, 1)
                        if g == S_CT + EVERY * t:
                            for k in range(2):
                                use = f"c{t}{'ab'[k]}"
                                act.wait_ge(ta.full, ta.at(p, use))
                                for i in range(DC):
                                    c = k * DC + i
                                    last = nc.scalar.activation(G[:, c, t * P:(t + 1) * P], ta.bank(use)[:, i * P:(i + 1) * P], ACT.Identity,
                                                                scale=col("L1_cond_ln2_g", c), bias=col("L1_cond_ln2_b", c))
                                last.then_inc(ta.emptied["act"], 1)
                    for t in range(TT):
                        if g == s_out(t):
                            act.wait_ge(*ta.done(p, f"f{t}"))
                            nc.scalar.activation(comb[:, t % 2, 0:D], comb[:, t % 2, 0:D], ACT.Silu).then_inc(silu_done, 1)

                def half0(b, p):
                    for g in range(N):
                        if g + 1 < N:
                            decay(b * 2, 0, g + 1)
                        else:
                            decay(b * 2 + 1, 1, 0)
                        if p is not None:
                            tail(p, g)
                        if g in S_DELTA1:
                            softplus(b, S_DELTA1[g])
                        for c in S_Z0.get(g, ()):
                            silu_z(b, c)

                def half1(b, n):
                    for g in range(N):
                        if g + 1 < N:
                            decay(b * 2 + 1, 1, g + 1)
                        elif n is not None:
                            decay(n * 2, 0, 0)
                        if g == 0:
                            act.wait_ge(ta.full, b * len(ta.uses))
                            for c in range(HC, IC):
                                nc.scalar.activation(G[:, c, :], U[:, c, :], ACT.Identity, scale=col("L1_cond_D_param", c)).then_inc(ud_done, 1)
                        for c in S_Z1.get(g, ()):
                            silu_z(b, c)
                        if n is not None:
                            front(n, g)

                act.dma_start(w_out[:], a["L1_cond_W_out"].rearrange("(c p) n -> p c n", p=P)).then_inc(w_in, 16)
                act.dma_start(w_full[:], a["L1_cond_W_full"].rearrange("(c p) n -> p c n", p=P)).then_inc(w_in, 16)
                act.dma_start(bias_full[:], a["L1_cond_b_full"].rearrange("(o n) -> o n", o=1).to_broadcast([P, D])).then_inc(w_in, 16)
                for g in FRONT:
                    front(0, g)
                decay(0, 0, 0)
                half0(0, None)
                with act.Fori(0, B - 1) as b:
                    half1(b, b + 1)
                    half0(b + 1, b)
                half1(B - 1, None)
                for g in range(N):
                    tail(B - 1, g)

            @block.vector
            def _(dve):
                link_front = Link(dve, own_front, IC * (TAPS - 2))
                link_delta = Link(dve, own_delta, 3 * IC)
                link_tail = Link(dve, own_tail, 6 * TT)

                def scan(j, n, s):
                    u = j * UNITS + 2 * n + s
                    dve.wait_ge(dA_done, u + 1)
                    dve.wait_ge(dbu_done, u + 1)
                    h = HS[:, s].rearrange("p i t -> p (i t)")
                    nc.vector.tensor_tensor_scan(h, dA[:, s].rearrange("p i t -> p (i t)"), h, 0.0, ALU.mult, ALU.add).then_inc(scanned, 1)

                def add(j, n):
                    for t in range(TT):
                        dve.wait_ge(yt_full, j * TURNED + n * TT + t + 1)
                        if n == 0:
                            nc.vector.tensor_scalar(acc[:, t, :], y_bank[t][:], C[:, t, n:n + 1], None, ALU.mult).then_inc(acc_done, 1)
                        else:
                            nc.vector.scalar_tensor_tensor(out=acc[:, t, :], in0=y_bank[t][:], scalar=C[:, t, n:n + 1], in1=acc[:, t, :],
                                                           op0=ALU.mult, op1=ALU.add).then_inc(acc_done, 1)

                def total(j, b, q):
                    for i in range(HC):
                        dve.wait_ge(yt_full, j * TURNED + N * TT + i + 1)
                        if q == 0:
                            nc.vector.scalar_tensor_tensor(out=G[:, i, :], in0=U[:, i, :], scalar=col("L1_cond_D_param", i),
                                                           in1=y_bank[i][:], op0=ALU.mult, op1=ALU.add).then_inc(acc_done, 1)
                        else:
                            dve.wait_ge(ud_done, b * HC + i + 1)
                            nc.vector.tensor_tensor(G[:, HC + i, :], y_bank[i][:], G[:, HC + i, :], ALU.add).then_inc(acc_done, 1)

                def gated(j, b, q):
                    for i in range(HC):
                        c = q * HC + i
                        dve.wait_ge(acc_done, j * TURNED + N * TT + i + 1)
                        dve.wait_ge(*fv.done(b, f"z{c}"))
                        nc.vector.tensor_tensor(G[:, c, :], G[:, c, :], ZS[:, i, :], ALU.mult).then_inc(g_done, 1)

                def finish_delta(n, c):
                    dve.wait_ge(sp_w, n * IC + c + 1)
                    link_delta(nc.vector.scalar_tensor_tensor(out=w1[:], in0=w1[:], scalar=1.0, in1=e_abs[:],
                                                              op0=ALU.subtract, op1=ALU.subtract))
                    dve.wait_ge(sp_ln, n * IC + c + 1)
                    link_delta(nc.vector.tensor_tensor(lnw[:], lnw[:], w1[:], ALU.subtract))
                    dve.wait_ge(*fv.done(n, f"dt{c}"))
                    link_delta(nc.vector.tensor_tensor(delta[:, c, :], lnw[:], relu[:], ALU.add))
                    nc.vector.tensor_tensor(DU[:, c, :], delta[:, c, :], U[:, c, :], ALU.mult).then_inc(du_done, 1)

                def front(n, g):
                    if g == min(S_XR):
                        link_front.begin(n)
                        link_delta.begin(n)
                    for c in S_XR.get(g, ()):
                        dve.wait_ge(conv0, n * IC + c + 1)
                        for k in range(TAPS - 1):
                            lag = TAPS - 1 - k
                            y = U[:, c, lag:T]
                            last = nc.vector.scalar_tensor_tensor(out=y, in0=fv.bank(f"xr{c}")[:, 0:T - lag], scalar=convw[:, c, k:k + 1],
                                                                  in1=y, op0=ALU.mult, op1=ALU.add)
                            if k < TAPS - 2:
                                link_front(last)
                        last.then_inc(fv.emptied["dve"], 1)
                    if g == S_XD:
                        dve.wait_ge(fv.full, fv.at(n, "xd"))
                        dve.wait_ge(b_out, n * 16)
                        nc.vector.tensor_copy(xdbl[:], fv.bank("xd")[0:XD, :]).then_inc(fv.emptied["dve"], 1)
                    if g - 1 in S_DELTA0:
                        finish_delta(n, S_DELTA0[g - 1])

                def copy_C(b):
                    dve.wait_ge(fv.full, fv.at(b, "C"))
                    nc.vector.tensor_copy(C[:], fv.bank("C")[:, 0:TT * XD].rearrange("p (t x) -> p t x", x=XD)[:, :, RANK + N:XD]).then_inc(
                        fv.emptied["dve"], 1)
                    dve.wait_ge(*fv.done(b, "C"))

                def tail(p, g):
                    if g == 0:
                        link_tail.begin(p)
                        dve.wait_ge(gate_in, p * 16 + 16)
                    for t in range(TT):
                        tile = comb[:, t % 2, :]
                        if g == S_O + 1 + EVERY * t:
                            dve.wait_ge(ta.full, ta.at(p, f"o{t}"))
                            dve.wait_ge(out_done[t % 2], (p * (TT // 2) + t // 2) * 16)
                            nc.vector.tensor_copy(tile[:, 0:D], ta.bank(f"o{t}")[:]).then_inc(ta.emptied["dve"], 1)
                            dve.wait_ge(attn_in[t % 2], (p * (TT // 2) + t // 2) * 16 + 16)
                            nc.vector.bn_stats(stats[:, t, 1, :], tile[:, D:2 * D])
                            dve.wait_ge(*ta.done(p, f"o{t}"))
                            link_tail(nc.vector.bn_stats(stats[:, t, 0, :], tile[:, 0:D]))
                            nc.vector.memset(spare[:], 0.0)
                            link_tail(nc.vector.bn_aggr(mv[:, t, :], stats[:, t].rearrange("p s k -> p (s k)")))
                            nc.vector.tensor_scalar(veps[:, t:t + 1], mv[:, t, 1:2], EPS, None, ALU.add).then_inc(ln_var, 1)
                        if g == S_NORM + EVERY * t:
                            r, x, v = rs[:, t:t + 1], rt[:, t:t + 1], veps[:, t:t + 1]
                            dve.wait_ge(ln_r0, p * TT + t + 1)
                            link_tail(nc.vector.tensor_tensor(x, r, r, ALU.mult))
                            link_tail(nc.vector.scalar_tensor_tensor(out=x, in0=x, scalar=-0.5, in1=v, op0=ALU.mult, op1=ALU.mult))
                            link_tail(nc.vector.scalar_tensor_tensor(out=r, in0=x, scalar=1.5, in1=r, op0=ALU.add, op1=ALU.mult))
                            nc.vector.tensor_scalar(tile, tile, mv[:, t, 0:1], r, ALU.subtract, ALU.mult).then_inc(chat, 1)
                        if g == S_F + 1 + EVERY * t:
                            dve.wait_ge(ta.full, ta.at(p, f"f{t}"))
                            nc.vector.tensor_tensor(tile[:, 0:D], ta.bank(f"f{t}")[:], bias_full[:], ALU.add).then_inc(ta.emptied["dve"], 1)
                    for t in range(TT):
                        if g == s_out(t):
                            tile = comb[:, t % 2, :]
                            dve.wait_ge(silu_done, p * TT + t + 1)
                            link_tail(nc.vector.tensor_tensor(tile[:, 0:D], tile[:, 0:D], gate[:], ALU.mult))
                            dve.wait_ge(x1_in[t % 2], (p * (TT // 2) + t // 2) * 16 + 16)
                            nc.vector.tensor_tensor(tile[:, 0:D], tile[:, 0:D], tile[:, D:2 * D], ALU.add).then_inc(out_ready, 1)
                            if t == TT - 1:
                                link_tail.end()

                def half0(b, p):
                    if p is not None:
                        total(b * 2 - 1, p, 1)
                    copy_C(b)
                    for g in range(N):
                        add(b * 2, g)
                        for s in range(2):
                            if g + 1 < N:
                                scan(b * 2, g + 1, s)
                            else:
                                scan(b * 2 + 1, 0, s)
                        if p is not None:
                            if g == 0:
                                gated(b * 2 - 1, p, 1)
                            tail(p, g)
                        if g == min(S_DELTA1):
                            link_delta.begin(b, 3 * HC)
                        if g - 1 in S_DELTA1:
                            finish_delta(b, S_DELTA1[g - 1])
                    link_delta.end()

                def half1(b, n):
                    total(b * 2, b, 0)
                    for g in range(N):
                        add(b * 2 + 1, g)
                        for s in range(2):
                            if g + 1 < N:
                                scan(b * 2 + 1, g + 1, s)
                            elif n is not None:
                                scan(n * 2, 0, s)
                        if g == 0:
                            gated(b * 2, b, 0)
                        if n is not None:
                            front(n, g)

                for s in range(2):
                    nc.vector.memset(dA[:, s, :, 0:1], 0.0).then_inc(zeroed, 1)
                dve.wait_ge(zeroed, 2)
                dve.wait_ge(w_in, 5 * 16)
                for g in FRONT:
                    front(0, g)
                for s in range(2):
                    scan(0, 0, s)
                half0(0, None)
                with dve.Fori(0, B - 1) as b:
                    half1(b, b + 1)
                    half0(b + 1, b)
                half1(B - 1, None)
                total(2 * B - 1, B - 1, 1)
                gated(2 * B - 1, B - 1, 1)
                for g in range(N):
                    tail(B - 1, g)

            @block.tensor
            def _(pe):
                def product(dst, lhs, rhs, chunks, of):
                    for c in chunks:
                        last = nc.tensor.matmul(dst, lhs(c), rhs(c), start=(c == 0), stop=(c == of - 1))
                    return last

                def turn(j, n):
                    for s in range(2):
                        pe.wait_ge(scanned, j * UNITS + 2 * n + s + 1)
                        if s == 0 and not (first(j) and n == 0):
                            pe.wait_ge(acc_done, j * TURNED + n * TT)
                        for t in range(TT):
                            for i in range(UC):
                                k = s * UC + i
                                last = nc.tensor.transpose(y_bank[t][:, k * P:(k + 1) * P], HS[:, s, i, t * P:(t + 1) * P], ident[:])
                            if s == 1:
                                last.then_inc(yt_full, 1)
                            elif t == TT - 1:
                                last.then_inc(turned0, 1)

                def total(j):
                    pe.wait_ge(acc_done, j * TURNED + N * TT)
                    for i in range(HC):
                        for t in range(TT):
                            last = nc.tensor.transpose(y_bank[i][:, t * P:(t + 1) * P], acc[:, t, i * P:(i + 1) * P], ident[:])
                        last.then_inc(yt_full, 1)

                def z(b, c):
                    fv.wait_free(pe, b, f"z{c}")
                    product(fv.bank(f"z{c}")[:], lambda k: w_io[:, k, DI + c * P:DI + (c + 1) * P], lambda k: XM[:, k, :],
                            range(DC), DC).then_inc(fv.full, 1)

                def dt(n, c):
                    fv.wait_free(pe, n, f"dt{c}")
                    nc.tensor.matmul(fv.bank(f"dt{c}")[:], w_dt[:, c * P:(c + 1) * P], xdbl[0:RANK, :], start=True, stop=True).then_inc(fv.full, 1)

                def turn_C(b):
                    fv.wait_free(pe, b, "C")
                    for t in range(TT):
                        last = nc.tensor.transpose(fv.bank("C")[:, t * XD:(t + 1) * XD], xdbl[:, t * P:(t + 1) * P], ident[0:XD, 0:XD])
                    last.then_inc(fv.full, 1)

                def front(n, g):
                    for c in S_XR.get(g, ()):
                        if c == 0:
                            pe.wait_ge(xm_in, n * 16 + 16)
                        fv.wait_free(pe, n, f"xr{c}")
                        product(fv.bank(f"xr{c}")[:], lambda k: w_io[:, k, c * P:(c + 1) * P], lambda k: XM[:, k, :],
                                range(DC), DC).then_inc(fv.full, 1)
                    if g == S_XD:
                        pe.wait_ge(u_done, (n + 1) * IC)
                        fv.wait_free(pe, n, "xd")
                        product(fv.bank("xd")[0:XD, :], lambda k: w_x[:, k, :], lambda k: U[:, k, :], range(IC), IC).then_inc(fv.full, 1)
                    if g in S_DELTA0:
                        if S_DELTA0[g] == 0:
                            pe.wait_ge(*fv.done(n, "xd"))
                        dt(n, S_DELTA0[g])

                def tail(p, g):
                    for t in range(TT):
                        if g == S_CT + EVERY * t:
                            pe.wait_ge(chat, p * TT + t + 1)
                            for k in range(2):
                                use = f"c{t}{'ab'[k]}"
                                ta.wait_free(pe, p, use)
                                for i in range(DC):
                                    c = k * DC + i
                                    last = nc.tensor.transpose(ta.bank(use)[:, i * P:(i + 1) * P], comb[:, t % 2, c * P:(c + 1) * P], ident[:])
                                last.then_inc(ta.full, 1)
                    for t in range(TT):
                        for s, use, w in ((S_O, f"o{t}", w_out), (S_F, f"f{t}", w_full)):
                            for k in range(2):
                                if g == s + EVERY * t + k:
                                    if k == 0:
                                        if use == "o0":
                                            pe.wait_ge(g_done, (p + 1) * IC)
                                        if use[0] == "f":
                                            pe.wait_ge(*ta.done(p, f"c{t}b"))
                                        ta.wait_free(pe, p, use)
                                    last = product(ta.bank(use)[:], lambda c: G[:, c, t * P:(t + 1) * P], lambda c: w[:, c, :],
                                                   range(k * IC // 2, (k + 1) * IC // 2), IC)
                                    if k == 1:
                                        last.then_inc(ta.full, 1)

                def half0(b, p):
                    turn_C(b)
                    if p is not None:
                        total(b * 2 - 1)
                    for g in range(N):
                        turn(b * 2, g)
                        if p is not None:
                            tail(p, g)
                        if g in S_DELTA1:
                            dt(b, S_DELTA1[g])
                        for c in S_Z0.get(g, ()):
                            z(b, c)

                def half1(b, n):
                    total(b * 2)
                    for g in range(N):
                        turn(b * 2 + 1, g)
                        for c in S_Z1.get(g, ()):
                            z(b, c)
                        if n is not None:
                            front(n, g)

                pe.wait_ge(win_in, 16)
                pe.wait_ge(w_in, 5 * 16)
                for g in FRONT:
                    front(0, g)
                half0(0, None)
                with pe.Fori(0, B - 1) as b:
                    half1(b, b + 1)
                    half0(b + 1, b)
                half1(B - 1, None)
                total(2 * B - 1)
                for g in range(N):
                    tail(B - 1, g)


_INS = ["x", "cond_2048", "mask_BxS_ik0"] + ["L0_cond_" + k for k in (
    "norm_scale norm_bias Wq bq Wk bk Wv bv film_emb_W film_emb_b film_norm_scale film_norm_bias film_out_W film_out_b").split()] + [
    "L1_cond_" + k for k in ("ln1_g ln1_b Wqkv bqkv Wproj bproj W_ada b_ada W_in W_conv b_conv W_x W_dt b_dt A_log D_param W_out "
                             "ln2_g ln2_b W_full b_full").split()]


def kernel(**inputs):
    import numpy as _np
    import concourse.bacc as _bacc
    from concourse import mybir as _mybir
    from concourse.bass_utils import run_bass_kernel_spmd as _run

    nc = _bacc.Bacc("TRN2", target_bir_lowering=False, num_devices=1)
    arrays, aps = {}, {}
    for name in _INS:
        v = _np.ascontiguousarray(inputs[name])
        arrays[f"in_{name}"] = v
        aps[name] = nc.dram_tensor(f"in_{name}", v.shape, _mybir.dt.from_np(v.dtype), kind="ExternalInput").ap()
    out = nc.dram_tensor("out", (B, T, D), F32, kind="ExternalOutput").ap()
    build(nc, aps, out)
    r = _run(nc, [arrays], core_ids=[0])
    return r.results[0]["out"]
```

```python
from contextlib import ExitStack

import numpy as np

import concourse.bass as bass
from concourse import mybir

ALU = mybir.AluOpType
ACT = mybir.ActivationFunctionType
F32 = mybir.dt.float32
I32 = mybir.dt.int32
AX = mybir.AxisListType.X

P = 128
B, T, D, E = 8, 512, 512, 1024
TT, DC, EC = T // P, D // P, E // P
H0, DH0 = 16, 32
H1, DH1 = 8, 64
DI, N, RANK, TAPS = 1024, 16, 64, 4
IC = DI // P
XD = RANK + 2 * N
EPS = 1e-5
EXP_AND_LN = "natural_log_exp_and_others"
LN_NEAR_1 = "natural_log"
MASKED = -float(2 ** 100)

VECTORS = [
    ("L0_cond_norm_scale", 0, DC), ("L0_cond_norm_bias", 0, DC), ("L0_cond_bk", 0, DC),
    ("L0_cond_film_norm_scale", 0, DC), ("L0_cond_film_norm_bias", 0, DC),
    ("L1_cond_ln1_g", 0, DC), ("L1_cond_ln1_b", 0, DC), ("L1_cond_bqkv", 0, 2 * DC),
    ("L1_cond_b_conv", 0, IC), ("L1_cond_b_dt", 0, IC), ("L1_cond_D_param", 0, IC),
    ("L1_cond_ln2_g", 0, 2 * DC), ("L1_cond_ln2_b", 0, 2 * DC),
]
COL, NCOL = {}, 0
for _name, _, _n in VECTORS:
    COL[_name] = NCOL
    NCOL += _n
FILM_A, FILM_B, LN1_A, LN1_B, VALID = (DC * i for i in range(5))
NCUR = VALID + TT


class Link:

    def __init__(self, eng, sem, per):
        self.eng, self.sem, self.per = eng, sem, per

    def begin(self, b, n=0):
        self.base, self.n = b * self.per, n

    def __call__(self, ins):
        ins.then_inc(self.sem, 1)
        self.n += 1
        self.eng.wait_ge(self.sem, self.base + self.n)

    def end(self):
        assert self.n == self.per, (self.n, self.per)


class Ring:

    def __init__(self, banks, full, emptied, uses):
        assert len(uses) % 2 == 0
        self.banks, self.full, self.emptied, self.uses = banks, full, emptied, uses
        self.names = [name for name, _ in uses]

    def bank(self, use):
        return self.banks[self.names.index(use) % 2]

    def at(self, b, use):
        return b * len(self.uses) + self.names.index(use) + 1

    def done(self, b, use):
        i = self.names.index(use)
        mine = [k for k, (_, e) in enumerate(self.uses) if e == self.uses[i][1]]
        return self.emptied[self.uses[i][1]], b * len(mine) + (mine.index(i) + 1)

    def wait_free(self, pe, b, use):
        i = self.names.index(use) - 2
        if i >= 0:
            pe.wait_ge(*self.done(b, self.names[i]))
        elif not (isinstance(b, int) and b == 0):
            mine = [k for k, (_, e) in enumerate(self.uses) if e == self.uses[i][1]]
            pe.wait_ge(self.emptied[self.uses[i][1]], b * len(mine) - (len(mine) - 1 - mine.index(len(self.uses) + i)))


def build(nc, a, out):
    ctx = ExitStack()
    with ctx:
        def sem(name, c=ctx):
            return c.enter_context(nc.semaphore(name))

        def sb(name, shape, dt=F32, c=ctx):
            return c.enter_context(nc.sbuf_tensor(name, shape, dt))

        x1_d = nc.dram_tensor("x1_d", (B, T, D), F32, kind="Internal").ap()
        xm_d = nc.dram_tensor("xm_d", (B, P, DC, T), F32, kind="Internal").ap()
        attn_d = nc.dram_tensor("attn_d", (B, T, D), F32, kind="Internal").ap()
        gate_d = nc.dram_tensor("gate_d", (B, D), F32, kind="Internal").ap()
        b_d = nc.dram_tensor("b_d", (B, N, T), F32, kind="Internal").ap()

        bank = [ctx.enter_context(nc.psum_tensor(f"bank{i}", [P, 512], F32)) for i in range(8)]

        ident = sb("ident", [P, P])
        cols = sb("cols", [P, NCOL])
        bq8 = sb("bq8", [P, DC])
        aneg = sb("aneg", [P, IC, N])
        convw = sb("convw", [P, IC, TAPS])
        per_batch = sb("per_batch", [P, B, NCUR])

        def col(name, c):
            return cols[:, COL[name] + c:COL[name] + c + 1]

        w_l0, w_l1 = sb("w_l0", [P, 4 * DC * D]), sb("w_l1", [P, 4 * DC * D])
        W, at = {}, 0
        for name, place, n in [(k, w_l0, D) for k in ("L0_cond_Wk", "L0_cond_Wq", "L0_cond_Wv", "L0_cond_film_out_W")] + [
                ("L1_cond_Wqkv", w_l1, 3 * D), ("L1_cond_Wproj", w_l1, D)]:
            at = at if place is w_l0 or name.endswith("Wproj") else 0
            W[name] = place[:, at:at + DC * n].rearrange("p (c n) -> p c n", n=n)
            at += DC * n
        W["L1_cond_W_in"] = w_l0[:].rearrange("p (c n) -> p c n", n=2 * DI)
        W["L1_cond_W_out"] = w_l1[:, 0:IC * D].rearrange("p (c n) -> p c n", n=D)
        W["L1_cond_W_full"] = w_l1[:, IC * D:2 * IC * D].rearrange("p (c n) -> p c n", n=D)
        arrived = {name: sem("arrived_" + name) for name in W}
        arrived["x"] = sem("x_in")

        def load(eng, name):
            return eng.dma_start(W[name], a[name].rearrange("(c p) n -> p c n", p=P))

        with ExitStack() as early:
            X = sb("X", [P, TT, D], c=early)
            setup(nc, a, bank, ident, cols, bq8, aneg, convw, per_batch, gate_d, X, load, arrived)
            attend(nc, a, bank, ident, cols, col, bq8, per_batch, x1_d, xm_d, attn_d, X, W, load, arrived)
        mix(nc, a, out, bank, ident, col, aneg, convw, x1_d, xm_d, attn_d, gate_d, b_d, W, load, arrived)


def setup(nc, a, bank, ident, cols, bq8, aneg, convw, per_batch, gate_d, X, load, arrived):
    ctx = ExitStack()
    with ctx:
        def sem(name):
            return ctx.enter_context(nc.semaphore(name))

        def sb(name, shape, dt=F32):
            return ctx.enter_context(nc.sbuf_tensor(name, shape, dt))

        vecrows = sb("vecrows", [P, P])
        maskrows = sb("maskrows", [B * TT, P], I32)
        validrows = sb("validrows", [B * TT, P])
        cond = sb("cond", [B, E])
        scond = sb("scond", [B, E])
        condT = sb("condT", [P, EC, B])
        wfilm = sb("wfilm", [P, EC, 2 * D])
        wada = sb("wada", [P, EC, 3 * D])
        film_bias = sb("film_bias", [B, 2 * D])
        ada_bias = sb("ada_bias", [B, 3 * D])
        film = sb("film", [B, 2 * D])
        ada = sb("ada", [B, 3 * D])
        scale1 = sb("scale1", [P, 2, DC, B])
        zeros = sb("zeros", [P, P])

        vec_in, mask_in, cond_in = sem("vec_in"), sem("mask_in"), sem("cond_in")
        par_in, film_in, ada_in = sem("par_in"), sem("film_in"), sem("ada_in")
        zeroed, ident_done, silu_done = sem("zeroed"), sem("ident_done"), sem("silu_done")
        a_exp, valid_done = sem("a_exp"), sem("valid_done")
        turned, condT_done, cond_mm, rows_done = sem("turned"), sem("condT_done"), sem("cond_mm"), sem("rows_done")
        rows_turned, own = sem("rows_turned"), sem("setup_dve")
        gate_out = sem("gate_out")

        with nc.Block() as block:

            @block.sync
            def _(sp):
                sp.dma_start(cond[:], a["cond_2048"]).then_inc(cond_in, 16)
                for name, first, n in VECTORS:
                    src = a[name][first:first + n * P].rearrange("(c p) -> c p", p=P)
                    sp.dma_start(vecrows[COL[name]:COL[name] + n, :], src).then_inc(vec_in, 16)
                sp.dma_start(maskrows[:], a["mask_BxS_ik0"].rearrange("b (t p) -> (b t) p", p=P)).then_inc(mask_in, 16)
                sp.dma_start(wfilm[:], a["L0_cond_film_emb_W"].rearrange("(c p) n -> p c n", p=P)).then_inc(film_in, 16)
                sp.dma_start(film_bias[:], a["L0_cond_film_emb_b"].rearrange("(o n) -> o n", o=1).to_broadcast([B, 2 * D])).then_inc(film_in, 16)
                sp.dma_start(X[:], a["x"][0].rearrange("(t p) d -> p t d", p=P)).then_inc(arrived["x"], 16)
                for name in ("L0_cond_Wk", "L0_cond_Wq", "L0_cond_Wv", "L0_cond_film_out_W", "L1_cond_Wqkv", "L1_cond_Wproj"):
                    load(sp, name).then_inc(arrived[name], 16)
                sp.wait_ge(rows_done, 5)
                sp.dma_start(gate_d, ada[:, 2 * D:3 * D]).then_inc(gate_out, 16)
                sp.wait_ge(gate_out, 16)

            @block.gpsimd
            def _(pool):
                nc.gpsimd.memset(zeros[:], 0.0).then_inc(zeroed, 1)
                pool.wait_ge(zeroed, 1)
                nc.gpsimd.affine_select(out=ident[:], in_=zeros[:], compare_op=ALU.not_equal, fill=1.0, base=0,
                                        pattern=[[-1, P]], channel_multiplier=1).then_inc(ident_done, 1)

            @block.scalar
            def _(act):
                act.dma_start(aneg[:], a["L1_cond_A_log"].rearrange("(c p) n -> p c n", p=P)).then_inc(par_in, 16)
                act.dma_start(convw[:], a["L1_cond_W_conv"].rearrange("(c p) o k -> p c (o k)", p=P)).then_inc(par_in, 16)
                act.dma_start(wada[:], a["L1_cond_W_ada"].rearrange("(c p) n -> p c n", p=P)).then_inc(ada_in, 16)
                act.dma_start(ada_bias[:], a["L1_cond_b_ada"].rearrange("(o n) -> o n", o=1).to_broadcast([B, 3 * D])).then_inc(ada_in, 16)
                act.wait_ge(cond_in, 16)
                nc.scalar.activation(scond[:], cond[:], ACT.Silu).then_inc(silu_done, 1)
                act.wait_ge(par_in, 32)
                nc.scalar.activation(aneg[:], aneg[:], ACT.Exp).then_inc(a_exp, 1)

            @block.tensor
            def _(pe):
                pe.wait_ge(ident_done, 1)
                pe.wait_ge(vec_in, 16 * len(VECTORS))
                nc.tensor.transpose(bank[0][:, 0:NCOL], vecrows[0:NCOL, :], ident[0:NCOL, 0:NCOL]).then_inc(turned, 1)
                pe.wait_ge(valid_done, 1)
                nc.tensor.transpose(bank[1][:, 0:B * TT], validrows[:], ident[0:B * TT, 0:B * TT]).then_inc(turned, 1)
                pe.wait_ge(silu_done, 1)
                for c in range(EC):
                    last = nc.tensor.transpose(bank[2][:, c * B:(c + 1) * B], scond[:, c * P:(c + 1) * P], ident[0:B, 0:B])
                last.then_inc(turned, 1)
                pe.wait_ge(condT_done, 1)
                for w, arrived, first, n in ((wfilm, film_in, 3, 2), (wada, ada_in, 5, 3)):
                    pe.wait_ge(arrived, 32)
                    for j in range(n):
                        for c in range(EC):
                            last = nc.tensor.matmul(bank[first + j][0:B, :], condT[:, c, :], w[:, c, j * D:(j + 1) * D],
                                                    start=(c == 0), stop=(c == EC - 1))
                        last.then_inc(cond_mm, 1)
                pe.wait_ge(rows_done, 5)
                for i in range(4 * DC):
                    src = film if i < 2 * DC else ada
                    j = i % (2 * DC)
                    last = nc.tensor.transpose(bank[0][:, i * B:(i + 1) * B], src[:, j * P:(j + 1) * P], ident[0:B, 0:B])
                last.then_inc(rows_turned, 1)

            @block.vector
            def _(dve):
                link = Link(dve, own, 100)
                link.begin(0)
                dve.wait_ge(mask_in, 16)
                nc.vector.tensor_scalar(validrows[:], maskrows[:], 1.0, None, ALU.not_equal).then_inc(valid_done, 1)
                dve.wait_ge(turned, 1)
                link(nc.vector.tensor_copy(cols[:], bank[0][:, 0:NCOL]))
                i = COL["L1_cond_bqkv"]
                nc.vector.tensor_scalar(bq8[:], cols[:, i:i + DC], DH1 ** -0.5, None, ALU.mult)
                dve.wait_ge(turned, 2)
                nc.vector.tensor_copy(per_batch[:, :, VALID:VALID + TT], bank[1][:, 0:B * TT].rearrange("p (b t) -> p b t", t=TT))
                dve.wait_ge(turned, 3)
                nc.vector.tensor_copy(condT[:], bank[2][:, 0:EC * B].rearrange("p (c b) -> p c b", b=B)).then_inc(condT_done, 1)
                dve.wait_ge(a_exp, 1)
                nc.vector.tensor_scalar(aneg[:], aneg[:], -1.0, None, ALU.mult)
                for j in range(5):
                    rows, bias, k = (film, film_bias, j) if j < 2 else (ada, ada_bias, j - 2)
                    dve.wait_ge(film_in if j < 2 else ada_in, 32)
                    dve.wait_ge(cond_mm, j + 1)
                    nc.vector.tensor_tensor(rows[:, k * D:(k + 1) * D], bank[3 + j][0:B, :], bias[:, k * D:(k + 1) * D],
                                            ALU.add).then_inc(rows_done, 1)
                dve.wait_ge(rows_turned, 1)
                t = bank[0][:, 0:4 * DC * B].rearrange("p (k c b) -> p k c b", k=4, b=B)
                for i, (g, bb, sc, sh, at_a, at_b) in enumerate((
                        ("L0_cond_film_norm_scale", "L0_cond_film_norm_bias", 0, 1, FILM_A, FILM_B),
                        ("L1_cond_ln1_g", "L1_cond_ln1_b", 3, 2, LN1_A, LN1_B))):
                    link(nc.vector.tensor_scalar(scale1[:, i], t[:, sc], 1.0, None, ALU.add))
                    for at, v in ((at_a, g), (at_b, bb)):
                        for c in range(DC):
                            last = nc.vector.tensor_scalar(per_batch[:, :, at + c], scale1[:, i, c, :],
                                                           cols[:, COL[v] + c:COL[v] + c + 1], None, ALU.mult)
                    link(last)
                    dst = per_batch[:, :, at_b:at_b + DC].rearrange("p b c -> p c b")
                    link(nc.vector.tensor_tensor(dst, dst, t[:, sh], ALU.add))


def attend(nc, a, bank, ident, cols, col, bq8, per_batch, x1_d, xm_d, attn_d, X, W, load, arrived):
    ctx = ExitStack()
    with ctx:
        def sem(name):
            return ctx.enter_context(nc.semaphore(name))

        def sb(name, shape, dt=F32):
            return ctx.enter_context(nc.sbuf_tensor(name, shape, dt))

        wqkv, wproj = W["L1_cond_Wqkv"], W["L1_cond_Wproj"]
        bias = {k: sb(f"bias_{k}", [P, D]) for k in ("q", "v", "film", "v1", "proj")}
        H = sb("H", [P, TT, D])
        NT = sb("NT", [P, DC, T])
        KT = sb("KT", [P, DC, T])
        Q = sb("Q", [P, TT, D])
        QT = sb("QT", [P, DC, T])
        V = sb("V", [P, TT, D])
        ATT = sb("ATT", [P, DC, P])
        blocks = sb("blocks", [P, DC, P])
        mask = sb("mask", [P, T], I32)
        mbias = sb("mbias", [P, T])
        nkmax, kden, kr = sb("nkmax", [P, DC]), sb("kden", [P, DC]), sb("kr", [P, DC])
        qmax, qr = sb("qmax", [P, TT, H0]), sb("qr", [P, TT, H0])
        cur = sb("cur", [P, NCUR])
        H2 = sb("H2", [P, TT, D])
        XM = sb("XM", [P, DC, T])
        Q2, K2 = sb("Q2", [P, DC, T]), sb("K2", [P, DC, T])
        V2 = sb("V2", [P, TT, D])
        PR = sb("PR", [P, 2, TT, T])
        PT = sb("PT", [P, TT, T])
        nsmax, rsum = sb("nsmax", [P, 2, TT]), sb("rsum", [P, H1, TT])
        rrec = sb("rrec", [P, H1, TT])
        stats = sb("stats", [P, TT, 6])
        mv, rs, rt = sb("mv", [P, TT, 2]), sb("rs", [P, TT]), sb("rt", [P, TT])
        veps, spare = sb("veps", [P, TT]), sb("spare", [P, 1])

        bias_in = sem("bias_in")
        x_in, mask_in = arrived["x"], sem("mk_in")
        blocks_zero, blocks_done = sem("blocks_zero"), sem("blocks_done")
        cur_done, xb_done = sem("cur_done"), sem("xb_done")
        ln_var, ln_ln, ln_r0 = sem("ln_var"), sem("ln_ln"), sem("ln_r0")
        xhat, yhat, x1hat = sem("xhat"), sem("yhat"), sem("x1hat")
        t1_full, t1_done = sem("t1_full"), sem("t1_done")
        m1_full, m1_done = sem("m1_full"), sem("m1_done")
        kmax, kexp, knorm = sem("kmax"), sem("kexp"), sem("knorm")
        mbias_done, qsub = sem("mbias_done"), sem("qsub")
        t2_full, t2_done = sem("t2_full"), sem("t2_done")
        sc_full, smax, pexp = sem("sc_full"), sem("smax"), sem("pexp")
        pt_full, pt_done = sem("pt_full"), sem("pt_done")
        o_full, o_done = sem("o_full"), sem("o_done")
        x1_out, xm_out, attn_out = sem("x1_out"), sem("xm_out"), sem("attn_out")
        own0, own1 = sem("l0_dve"), sem("l1_dve")
        T1, M1, T2, SC, PTN, O = 20, 22, 12, H1 * TT, H1 * TT, 16
        T1_X, T1_E, T1_Q, T1_Y, T1_X1 = 0, 4, 8, 12, 16
        M1_K, M1_Q, M1_V, M1_ATT, M1_SUM, M1_Y, M1_F = 0, 4, 8, 12, 13, 14, 18
        T2_QK, T2_O = 0, 8
        O_V, O_PV, O_P = 0, 4, 12
        t1_bank, m1_bank, t2_bank, sc_bank, pt_bank, o_bank = bank[0], bank[1:3], bank[3], bank[4:6], bank[6], bank[7]
        turn_bank = (t1_bank, t2_bank)
        qk_bank, vp_bank = (t2_bank, pt_bank), (o_bank, pt_bank)

        S_TURN_X, S_K, S_E, S_Q, S_V, S_TURN_Q, S_ATT, S_Y, S_NORM_Y, S_TURN_Y, S_F, S_NORM_X1, S_TURN_X1 = (
            0, 4, 10, 8, 12, 14, 16, 17, 19, 22, 23, 27, 30)
        SLOTS = 1 + H1 * TT

        def l0_alone(l0, n):
            for g in range(SLOTS):
                l0(n, g)

        with nc.Block() as block:

            @block.sync
            def _(sp):
                def load_mask(n):
                    sp.wait_ge(mbias_done, n)
                    sp.dma_start(mask[:], a["mask_BxS_ik0"][bass.ds(n, 1), :].to_broadcast([P, T])).then_inc(mask_in, 16)

                def load_x(n):
                    stored, normed = sp.to_reg(n * 16), sp.to_reg(n * TT)
                    sp.wait_ge(x1_out, stored)
                    sp.wait_ge(x1hat, normed)
                    sp.dma_start(X[:], a["x"][n].rearrange("(t p) d -> p t d", p=P)).then_inc(x_in, 16)

                def store_l0(n):
                    sp.wait_ge(m1_done, n * M1 + M1)
                    sp.dma_start(x1_d[n].rearrange("(t p) d -> p t d", p=P), X[:]).then_inc(x1_out, 16)
                    sp.wait_ge(t1_done, n * T1 + T1)
                    sp.dma_start(xm_d[n], XM[:]).then_inc(xm_out, 16)

                def store_l1(b):
                    sp.wait_ge(o_done, b * O + O)
                    sp.dma_start(attn_d[b].rearrange("(t p) d -> p t d", p=P), H2[:]).then_inc(attn_out, 16)

                load_mask(0)
                store_l0(0)
                with sp.Fori(0, B - 1) as b:
                    load_x(b + 1)
                    load_mask(b + 1)
                    store_l0(b + 1)
                    store_l1(b)
                sp.wait_ge(m1_full, B * M1)
                load(sp, "L1_cond_W_in").then_inc(arrived["L1_cond_W_in"], 16)
                sp.wait_ge(o_full, (B - 1) * O + O_V + TT)
                load(sp, "L1_cond_W_out").then_inc(arrived["L1_cond_W_out"], 16)
                store_l1(B - 1)
                sp.wait_ge(x1_out, B * 16)
                sp.wait_ge(xm_out, B * 16)
                sp.wait_ge(attn_out, B * 16)

            @block.gpsimd
            def _(pool):
                nc.gpsimd.memset(blocks[:], 0.0).then_inc(blocks_zero, 1)
                pool.wait_ge(blocks_zero, 1)
                for g in range(P // DH0):
                    s = slice(g * DH0, (g + 1) * DH0)
                    nc.gpsimd.memset(blocks[s, :, s], 1.0).then_inc(blocks_done, 1)
                pool.wait_ge(blocks_done, P // DH0)
                pool.wait_ge(bias_in, 5 * 16)
                with pool.Fori(0, B) as n:
                    pool.wait_ge(t1_done, n * T1)
                    nc.gpsimd.tensor_copy(cur[:], per_batch[:, n, :]).then_inc(cur_done, 1)
                    for t in range(TT):
                        pool.wait_ge(xhat, n * TT + t + 1)
                        nc.gpsimd.tensor_tensor(X[:, t, :], X[:, t, :], bias["film"][:], ALU.add).then_inc(xb_done, 1)

            @block.scalar
            def _(act):
                for k, (name, first) in {"q": ("L0_cond_bq", 0), "v": ("L0_cond_bv", 0), "film": ("L0_cond_film_out_b", 0),
                                         "v1": ("L1_cond_bqkv", 2 * D), "proj": ("L1_cond_bproj", 0)}.items():
                    src = a[name][first:first + D].rearrange("(o n) -> o n", o=1).to_broadcast([P, D])
                    act.dma_start(bias[k][:], src).then_inc(bias_in, 16)

                def inv_std(n, i):
                    act.wait_ge(ln_var, n * 3 + i + 1)
                    nc.scalar.activation(rt[:], veps[:], ACT.Ln).then_inc(ln_ln, 1)
                    act.wait_ge(ln_ln, n * 3 + i + 1)
                    nc.scalar.activation(rs[:], rt[:], ACT.Exp, scale=-0.5).then_inc(ln_r0, 1)

                def l0(n, g):
                    if S_TURN_X <= g < S_TURN_X + DC:
                        c = g - S_TURN_X
                        act.wait_ge(t1_full, n * T1 + T1_X + c + 1)
                        nc.scalar.activation(NT[:, c, :], turn_bank[c % 2][:], ACT.Identity, scale=col("L0_cond_norm_scale", c),
                                             bias=col("L0_cond_norm_bias", c)).then_inc(t1_done, 1)
                    if S_K + 1 <= g < S_K + 1 + DC:
                        c = g - (S_K + 1)
                        act.wait_ge(kmax, n * DC + c + 1)
                        nc.scalar.activation(KT[:, c, :], KT[:, c, :], ACT.Exp, bias=nkmax[:, c:c + 1],
                                             accum_out=kden[:, c:c + 1]).then_inc(kexp, 1)
                    if S_E <= g < S_E + TT:
                        t = g - S_E
                        if t == 0:
                            act.wait_ge(cur_done, n + 1)
                        act.wait_ge(t1_full, n * T1 + T1_E + t + 1)
                        nc.scalar.activation(H[:, t, :], turn_bank[t % 2][:], ACT.Identity,
                                             scale=cur[:, VALID + t:VALID + t + 1]).then_inc(t1_done, 1)
                    if S_TURN_Q <= g < S_TURN_Q + DC // 2:
                        for c in range(2 * (g - S_TURN_Q), 2 * (g - S_TURN_Q) + 2):
                            act.wait_ge(t1_full, n * T1 + T1_Q + c + 1)
                            nc.scalar.activation(QT[:, c, :], turn_bank[c % 2][:], ACT.Exp).then_inc(t1_done, 1)
                    if g == S_NORM_Y + 1:
                        inv_std(n, 1)
                    if g == S_TURN_Y:
                        for c in range(DC):
                            act.wait_ge(t1_full, n * T1 + T1_Y + c + 1)
                            nc.scalar.activation(NT[:, c, :], turn_bank[c % 2][:], ACT.Silu, scale=cur[:, FILM_A + c:FILM_A + c + 1],
                                                 bias=cur[:, FILM_B + c:FILM_B + c + 1]).then_inc(t1_done, 1)
                        act.preload_act_table_set(EXP_AND_LN)
                    if g == S_NORM_X1 + 1:
                        inv_std(n, 2)
                    if S_TURN_X1 <= g < S_TURN_X1 + DC // 2:
                        if g == S_TURN_X1:
                            act.wait_ge(xm_out, n * 16)
                        for c in range(2 * (g - S_TURN_X1), 2 * (g - S_TURN_X1) + 2):
                            act.wait_ge(t1_full, n * T1 + T1_X1 + c + 1)
                            nc.scalar.activation(XM[:, c, :], turn_bank[c % 2][:], ACT.Identity, scale=cur[:, LN1_A + c:LN1_A + c + 1],
                                                 bias=cur[:, LN1_B + c:LN1_B + c + 1]).then_inc(t1_done, 1)

                def l1(b, n):
                    act.preload_act_table_set(EXP_AND_LN)
                    for i in range(2 * DC):
                        if i == DC and n is not None:
                            inv_std(n, 0)
                        act.wait_ge(t2_full, b * T2 + T2_QK + i + 1)
                        if i < DC:
                            nc.scalar.activation(Q2[:, i, :], qk_bank[i % 2][:], ACT.Identity, scale=DH1 ** -0.5,
                                                 bias=bq8[:, i:i + 1]).then_inc(t2_done, 1)
                        else:
                            nc.scalar.activation(K2[:, i - DC, :], qk_bank[i % 2][:], ACT.Identity,
                                                 bias=col("L1_cond_bqkv", i)).then_inc(t2_done, 1)

                    def probabilities(h, t):
                        act.wait_ge(smax, b * SC + h * TT + t + 1)
                        if h >= 2 and t == 0:
                            act.wait_ge(pt_full, b * PTN + (h - 1) * TT)
                        nc.scalar.activation(PR[:, h % 2, t, :], sc_bank[t % 2][:], ACT.Exp, bias=nsmax[:, h % 2, t:t + 1],
                                             accum_out=rsum[:, h, t:t + 1]).then_inc(pexp, 1)

                    for t in range(TT):
                        probabilities(0, t)
                    if n is not None:
                        l0(n, 0)
                    for h in range(H1):
                        for k in range(TT):
                            if h + 1 < H1:
                                probabilities(h + 1, k)
                            if n is not None:
                                l0(n, 1 + h * TT + k)
                    for c in range(DC):
                        act.wait_ge(t2_full, b * T2 + T2_O + c + 1)
                        nc.scalar.activation(Q2[:, c, :], qk_bank[c % 2][:], ACT.Identity).then_inc(t2_done, 1)

                act.preload_act_table_set(EXP_AND_LN)
                inv_std(0, 0)
                l0_alone(l0, 0)
                with act.Fori(0, B - 1) as b:
                    l1(b, b + 1)
                l1(B - 1, None)

            @block.vector
            def _(dve):
                link0, link1 = Link(dve, own0, 3 * 5 + TT + 2), Link(dve, own1, H1)

                def variance(src):
                    for t in range(TT):
                        last = nc.vector.bn_stats(stats[:, t, :], src[:, t, :])
                    link0(last)
                    nc.vector.memset(spare[:], 0.0)
                    for t in range(TT):
                        last = nc.vector.bn_aggr(mv[:, t, :], stats[:, t, :])
                    link0(last)
                    nc.vector.tensor_scalar(veps[:], mv[:, :, 1], EPS, None, ALU.add).then_inc(ln_var, 1)

                def norm(n, i, src, dst, ready):
                    dve.wait_ge(ln_r0, n * 3 + i + 1)
                    link0(nc.vector.tensor_tensor(rt[:], rs[:], rs[:], ALU.mult))
                    link0(nc.vector.scalar_tensor_tensor(out=rt[:], in0=rt[:], scalar=-0.5, in1=veps[:], op0=ALU.mult, op1=ALU.mult))
                    link0(nc.vector.scalar_tensor_tensor(out=rs[:], in0=rt[:], scalar=1.5, in1=rs[:], op0=ALU.add, op1=ALU.mult))
                    for t in range(TT):
                        nc.vector.tensor_scalar(dst[:, t, :], src[:, t, :], mv[:, t, 0:1], rs[:, t:t + 1],
                                                ALU.subtract, ALU.mult).then_inc(ready, 1)

                def l0_begin(n):
                    link0.begin(n)
                    dve.wait_ge(x_in, n * 16 + 16)
                    variance(X)
                    dve.wait_ge(t1_full, n * T1)
                    norm(n, 0, X, H, xhat)

                def l0(n, g):
                    if g == S_TURN_X:
                        dve.wait_ge(mask_in, n * 16 + 16)
                        nc.vector.tensor_scalar(mbias[:], mask[:], 1.0, MASKED, ALU.is_equal, ALU.mult).then_inc(mbias_done, 1)
                    if S_K <= g < S_K + DC:
                        c = g - S_K
                        if c == 0:
                            dve.wait_ge(mbias_done, n + 1)
                        dve.wait_ge(m1_full, n * M1 + M1_K + c + 1)
                        nc.vector.scalar_tensor_tensor(out=KT[:, c, :], in0=m1_bank[c % 2][:], scalar=col("L0_cond_bk", c),
                                                       in1=mbias[:], op0=ALU.add, op1=ALU.add).then_inc(m1_done, 1)
                        dve.wait_ge(m1_done, n * M1 + M1_K + c + 1)
                        nc.vector.tensor_reduce(nkmax[:, c:c + 1], KT[:, c, :], AX, ALU.max, negate=True).then_inc(kmax, 1)
                    if S_Q <= g < S_Q + TT:
                        t = g - S_Q
                        dve.wait_ge(m1_full, n * M1 + M1_Q + t + 1)
                        nc.vector.tensor_tensor(Q[:, t, :], m1_bank[t % 2][:], bias["q"][:], ALU.add).then_inc(m1_done, 1)
                        dve.wait_ge(m1_done, n * M1 + M1_Q + t + 1)
                        heads = Q[:, t, :].rearrange("p (h d) -> p h d", d=DH0)
                        link0(nc.vector.tensor_reduce(qmax[:, t, :], heads, AX, ALU.max))
                        nc.vector.tensor_tensor(heads, heads, qmax[:, t, :].unsqueeze(2).to_broadcast([P, H0, DH0]),
                                                ALU.subtract).then_inc(qsub, 1)
                    if g == S_E - 1:
                        dve.wait_ge(kexp, n * DC + DC)
                        link0(nc.vector.scalar_tensor_tensor(out=kden[:], in0=nkmax[:], scalar=-MASKED / 2, in1=kden[:],
                                                             op0=ALU.is_lt, op1=ALU.mult))
                        link0(nc.vector.reciprocal(kr[:], kden[:]))
                        for c in range(DC):
                            nc.vector.tensor_scalar(KT[:, c, :], KT[:, c, :], kr[:, c:c + 1], None, ALU.mult).then_inc(knorm, 1)
                    if S_V <= g < S_V + TT:
                        t = g - S_V
                        dve.wait_ge(m1_full, n * M1 + M1_V + t + 1)
                        nc.vector.tensor_tensor(V[:, t, :], m1_bank[t % 2][:], bias["v"][:], ALU.add).then_inc(m1_done, 1)
                    if g == S_ATT:
                        dve.wait_ge(m1_full, n * M1 + M1_ATT + 1)
                        nc.vector.tensor_tensor(ATT[:], m1_bank[0][:].rearrange("p (c e) -> p c e", e=P), blocks[:],
                                                ALU.mult).then_inc(m1_done, 1)
                        dve.wait_ge(m1_full, n * M1 + M1_SUM + 1)
                        nc.vector.reciprocal(qr[:].rearrange("p t h -> p (t h)"), m1_bank[1][:, 0:TT * H0]).then_inc(m1_done, 1)
                    if S_Y <= g < S_Y + TT // 2:
                        if g == S_Y:
                            dve.wait_ge(m1_done, n * M1 + M1_SUM + 1)
                        for t in range(2 * (g - S_Y), 2 * (g - S_Y) + 2):
                            dve.wait_ge(m1_full, n * M1 + M1_Y + t + 1)
                            nc.vector.tensor_tensor(Q[:, t, :].rearrange("p (h d) -> p h d", d=DH0),
                                                    m1_bank[t % 2][:].rearrange("p (h d) -> p h d", d=DH0),
                                                    qr[:, t, :].unsqueeze(2).to_broadcast([P, H0, DH0]), ALU.mult).then_inc(m1_done, 1)
                    if g == S_NORM_Y:
                        dve.wait_ge(m1_done, n * M1 + M1_Y + TT)
                        variance(Q)
                    if g == S_NORM_Y + 1:
                        norm(n, 1, Q, H, yhat)
                    if S_F <= g < S_F + TT:
                        t = g - S_F
                        if t == 0:
                            dve.wait_ge(xb_done, n * TT + TT)
                        dve.wait_ge(m1_full, n * M1 + M1_F + t + 1)
                        nc.vector.tensor_tensor(X[:, t, :], m1_bank[t % 2][:], X[:, t, :], ALU.add).then_inc(m1_done, 1)
                    if g == S_NORM_X1:
                        dve.wait_ge(m1_done, n * M1 + M1)
                        variance(X)
                    if g == S_NORM_X1 + 1:
                        norm(n, 2, X, H, x1hat)
                        link0.end()

                def l1(b, n):
                    link1.begin(b)
                    if n is not None:
                        l0_begin(n)
                    for t in range(TT):
                        dve.wait_ge(o_full, b * O + O_V + t + 1)
                        nc.vector.tensor_tensor(V2[:, t, :], vp_bank[t % 2][:], bias["v1"][:], ALU.add).then_inc(o_done, 1)

                    def score_max(h, t):
                        dve.wait_ge(sc_full, b * SC + h * TT + t + 1)
                        nc.vector.tensor_reduce(nsmax[:, h % 2, t:t + 1], sc_bank[t % 2][:], AX, ALU.max, negate=True).then_inc(smax, 1)

                    def head_out(h):
                        dve.wait_ge(pexp, b * SC + (h + 1) * TT)
                        link1(nc.vector.reciprocal(rrec[:, h, :], rsum[:, h, :]))
                        dve.wait_ge(o_full, b * O + O_PV + h + 1)
                        nc.vector.tensor_tensor(H2[:, :, h * DH1:(h + 1) * DH1],
                                                o_bank[:, 0:TT * DH1].rearrange("p (t d) -> p t d", d=DH1),
                                                rrec[:, h, :].unsqueeze(2).to_broadcast([P, TT, DH1]), ALU.mult).then_inc(o_done, 1)

                    for t in range(TT):
                        score_max(0, t)
                    if n is not None:
                        l0(n, 0)
                    dve.wait_ge(attn_out, b * 16)
                    for h in range(H1):
                        for k in range(TT):
                            if h + 1 < H1:
                                score_max(h + 1, k)
                            if h >= 1 and k == 0:
                                dve.wait_ge(o_full, b * O + O_PV + h)
                            dve.wait_ge(pt_full, b * PTN + h * TT + k + 1)
                            nc.vector.tensor_copy(PT[:, k, :], pt_bank[:]).then_inc(pt_done, 1)
                            if h >= 1 and k == 0:
                                head_out(h - 1)
                            if n is not None:
                                l0(n, 1 + h * TT + k)
                    head_out(H1 - 1)
                    dve.wait_ge(t2_full, b * T2 + T2)
                    for t in range(TT):
                        dve.wait_ge(o_full, b * O + O_P + t + 1)
                        nc.vector.tensor_tensor(H2[:, t, :], vp_bank[t % 2][:], bias["proj"][:], ALU.add).then_inc(o_done, 1)
                    link1.end()

                dve.wait_ge(bias_in, 5 * 16)
                dve.wait_ge(blocks_done, P // DH0)
                l0_begin(0)
                l0_alone(l0, 0)
                with dve.Fori(0, B - 1) as b:
                    l1(b, b + 1)
                l1(B - 1, None)

            @block.tensor
            def _(pe):
                def turn(dst, src, c):
                    for t in range(TT):
                        last = nc.tensor.transpose(dst[:, t * P:(t + 1) * P], src[:, t, c * P:(c + 1) * P], ident[:])
                    return last

                def product(dst, lhs, rhs):
                    for c in range(DC):
                        last = nc.tensor.matmul(dst[:], lhs(c), rhs(c), start=(c == 0), stop=(c == DC - 1))
                    return last

                def l0(n, g):
                    def m1_free(i):
                        pe.wait_ge(m1_done, n * M1 + max(i - 1, 0))

                    def turns(i):
                        pe.wait_ge(t1_done, n * T1 + i)

                    def t1_free(i):
                        pe.wait_ge(t1_done, n * T1 + max(i - 1, 0))

                    if S_TURN_X <= g < S_TURN_X + DC:
                        if g == S_TURN_X:
                            pe.wait_ge(xhat, n * TT + TT)
                        t1_free(T1_X + g - S_TURN_X)
                        turn(turn_bank[(g - S_TURN_X) % 2], H, g - S_TURN_X).then_inc(t1_full, 1)
                    if S_E <= g < S_E + TT:
                        t = g - S_E
                        if t == 0:
                            pe.wait_ge(knorm, n * DC + DC)
                        t1_free(T1_E + t)
                        for c in range(DC):
                            last = nc.tensor.transpose(turn_bank[t % 2][:, c * P:(c + 1) * P], KT[:, c, t * P:(t + 1) * P], ident[:])
                        last.then_inc(t1_full, 1)
                    if S_K <= g < S_K + DC:
                        c = g - S_K
                        if c == 0:
                            turns(T1_X + DC)
                        m1_free(M1_K + c)
                        product(m1_bank[c % 2], lambda k: W["L0_cond_Wk"][:, k, c * P:(c + 1) * P], lambda k: NT[:, k, :]).then_inc(m1_full, 1)
                    for s, i, w in ((S_Q, M1_Q, "L0_cond_Wq"), (S_V, M1_V, "L0_cond_Wv")):
                        if s <= g < s + TT:
                            t = g - s
                            m1_free(i + t)
                            product(m1_bank[t % 2], lambda k: NT[:, k, t * P:(t + 1) * P], lambda k: W[w][:, k, :]).then_inc(m1_full, 1)
                    if S_TURN_Q <= g < S_TURN_Q + DC // 2:
                        for c in range(2 * (g - S_TURN_Q), 2 * (g - S_TURN_Q) + 2):
                            if c == 0:
                                pe.wait_ge(qsub, n * TT + TT)
                            t1_free(T1_Q + c)
                            turn(turn_bank[c % 2], Q, c).then_inc(t1_full, 1)
                    if g == S_ATT:
                        turns(T1_Q + DC)
                        pe.wait_ge(m1_done, n * M1 + M1_ATT)
                        for c in range(DC):
                            f = slice(c * P, (c + 1) * P)
                            for s in range(TT):
                                last = nc.tensor.matmul(m1_bank[0][:, f], V[:, s, f], H[:, s, f], start=(s == 0), stop=(s == TT - 1))
                        last.then_inc(m1_full, 1)
                        m1_free(M1_SUM)
                        for t in range(TT):
                            for c in range(DC):
                                i = t * H0 + c * (H0 // DC)
                                last = nc.tensor.matmul(m1_bank[1][:, i:i + H0 // DC], QT[:, c, t * P:(t + 1) * P],
                                                        blocks[:, 0, 0:P:DH0], start=True, stop=True)
                        last.then_inc(m1_full, 1)
                    if S_Y <= g < S_Y + TT // 2:
                        if g == S_Y:
                            pe.wait_ge(m1_done, n * M1 + M1_ATT + 1)
                        for t in range(2 * (g - S_Y), 2 * (g - S_Y) + 2):
                            m1_free(M1_Y + t)
                            for c in range(DC):
                                last = nc.tensor.matmul(m1_bank[t % 2][:, c * P:(c + 1) * P], QT[:, c, t * P:(t + 1) * P],
                                                        ATT[:, c, :], start=True, stop=True)
                            last.then_inc(m1_full, 1)
                    if g == S_TURN_Y:
                        pe.wait_ge(yhat, n * TT + TT)
                        for c in range(DC):
                            t1_free(T1_Y + c)
                            turn(turn_bank[c % 2], H, c).then_inc(t1_full, 1)
                    if S_F <= g < S_F + TT:
                        t = g - S_F
                        if t == 0:
                            turns(T1_Y + DC)
                        m1_free(M1_F + t)
                        product(m1_bank[t % 2], lambda k: NT[:, k, t * P:(t + 1) * P], lambda k: W["L0_cond_film_out_W"][:, k, :]).then_inc(m1_full, 1)
                    if S_TURN_X1 <= g < S_TURN_X1 + DC // 2:
                        if g == S_TURN_X1:
                            pe.wait_ge(x1hat, n * TT + TT)
                        for c in range(2 * (g - S_TURN_X1), 2 * (g - S_TURN_X1) + 2):
                            t1_free(T1_X1 + c)
                            turn(turn_bank[c % 2], H, c).then_inc(t1_full, 1)

                def l1(b, n):
                    pe.wait_ge(t1_done, (b + 1) * T1)
                    pe.wait_ge(o_done, b * O)
                    for i in range(2 * DC):
                        pe.wait_ge(t2_done, b * T2 + T2_QK + max(i - 1, 0))
                        product(qk_bank[i % 2], lambda k: wqkv[:, k, i * P:(i + 1) * P], lambda k: XM[:, k, :]).then_inc(t2_full, 1)
                    for t in range(TT):
                        if t == 1:
                            pe.wait_ge(t2_done, b * T2 + T2_QK + 2 * DC)
                        pe.wait_ge(o_done, b * O + O_V + max(t - 1, 0))
                        product(vp_bank[t % 2], lambda k: XM[:, k, t * P:(t + 1) * P], lambda k: wqkv[:, k, 2 * D:3 * D]).then_inc(o_full, 1)

                    def scores(h, t):
                        pe.wait_ge(pexp, b * SC + max(h * TT + t - 1, 0))
                        s = slice(h % 2 * DH1, h % 2 * DH1 + DH1)
                        nc.tensor.matmul(sc_bank[t % 2][:], Q2[s, h // 2, t * P:(t + 1) * P], K2[s, h // 2, :],
                                         start=True, stop=True).then_inc(sc_full, 1)

                    for t in range(TT):
                        scores(0, t)
                    if n is not None:
                        l0(n, 0)
                    pe.wait_ge(o_done, b * O + O_V + TT)
                    for h in range(H1):
                        for k in range(TT):
                            if h + 1 < H1:
                                scores(h + 1, k)
                            pe.wait_ge(pexp, b * SC + (h + 1) * TT)
                            pe.wait_ge(pt_done, b * PTN + h * TT + k)
                            for t in range(TT):
                                last = nc.tensor.transpose(pt_bank[:, t * P:(t + 1) * P], PR[:, h % 2, t, k * P:(k + 1) * P], ident[:])
                            last.then_inc(pt_full, 1)
                            if n is not None:
                                l0(n, 1 + h * TT + k)
                        pe.wait_ge(pt_done, b * PTN + (h + 1) * TT)
                        pe.wait_ge(o_done, b * O + O_PV + h)
                        for t in range(TT):
                            for k in range(TT):
                                last = nc.tensor.matmul(o_bank[:, t * DH1:(t + 1) * DH1], PT[:, k, t * P:(t + 1) * P],
                                                        V2[:, k, h * DH1:(h + 1) * DH1], start=(k == 0), stop=(k == TT - 1))
                        last.then_inc(o_full, 1)
                    pe.wait_ge(o_done, b * O + O_PV + H1)
                    if n is not None:
                        pe.wait_ge(t1_done, (n + 1) * T1)
                    for c in range(DC):
                        pe.wait_ge(t2_done, b * T2 + T2_O + max(c - 1, 0))
                        turn(qk_bank[c % 2], H2, c).then_inc(t2_full, 1)
                    pe.wait_ge(t2_done, b * T2 + T2)
                    for t in range(TT):
                        pe.wait_ge(o_done, b * O + O_P + max(t - 1, 0))
                        product(vp_bank[t % 2], lambda k: Q2[:, k, t * P:(t + 1) * P], lambda k: wproj[:, k, :]).then_inc(o_full, 1)

                pe.wait_ge(blocks_done, P // DH0)
                for name in ("L0_cond_Wk", "L0_cond_Wq", "L0_cond_Wv", "L0_cond_film_out_W"):
                    pe.wait_ge(arrived[name], 16)
                l0_alone(l0, 0)
                for name in ("L1_cond_Wqkv", "L1_cond_Wproj"):
                    pe.wait_ge(arrived[name], 16)
                with pe.Fori(0, B - 1) as b:
                    l1(b, b + 1)
                l1(B - 1, None)


def mix(nc, a, out, bank, ident, col, aneg, convw, x1_d, xm_d, attn_d, gate_d, b_d, W, load, arrived):
    ctx = ExitStack()
    with ctx:
        def sem(name):
            return ctx.enter_context(nc.semaphore(name))

        def sb(name, shape, dt=F32):
            return ctx.enter_context(nc.sbuf_tensor(name, shape, dt))

        HC, UC = IC // 2, IC // 4
        UNITS = 2 * N
        TURNED = (N + 1) * TT
        ADDED = (N - 1) * TT + HC

        w_io, w_out, w_full = W["L1_cond_W_in"], W["L1_cond_W_out"], W["L1_cond_W_full"]
        w_x = sb("w_x", [P, IC, XD])
        w_dt = sb("w_dt", [RANK, DI])
        bias_full = sb("bias_full", [P, D])
        gate = sb("gate", [P, D])
        XM = sb("XM2", [P, DC, T])
        U = sb("U", [P, IC, T])
        G = sb("G", [P, IC, T])
        ZS = sb("ZS", [P, HC, T])
        delta = sb("delta", [P, IC, T])
        DU = sb("DU", [P, IC, T])
        brep = sb("brep", [P, 2, T])
        dA = sb("dA", [P, 2, UC, T])
        HS = sb("HS", [P, 2, HC, T])
        acc = sb("acc", [P, TT, HC * P])
        comb = sb("comb", [P, 2, 2 * D])
        e_abs, lnw = sb("e_abs", [P, T]), sb("lnw", [P, T])
        xdbl = sb("xdbl", [XD, T])
        C = sb("C", [P, TT, N])
        stats = sb("stats2", [P, TT, 2, 6])
        mv, rs, rt, veps = sb("mv2", [P, TT, 2]), sb("rs2", [P, TT]), sb("rt2", [P, TT]), sb("veps2", [P, TT])
        spare = sb("spare2", [P, 1])

        small_in, bias_in, gate_in, xm_in = sem("small_in"), sem("b_full_in"), sem("gate_in"), sem("xm_in")
        attn_in, x1_in, out_done, brep_in = ([sem(f"{k}{i}") for i in range(2)] for k in ("attn_in", "x1_in", "out_done", "brep_in"))
        b_out = sem("b_out")
        conv0, conv_done, u_done = sem("conv0"), sem("conv_done"), sem("u_done")
        sp_abs, sp_exp, sp_w, sp_ln, du_done = sem("sp_abs"), sem("sp_exp"), sem("sp_w"), sem("sp_ln"), sem("du_done")
        zeroed, ud_done, g_done = sem("zeroed"), sem("ud_done"), sem("g_done")
        dA_done, scanned, dbu_done = sem("dA_done"), sem("scanned"), sem("dbu_done")
        yt_full, sum_begun, acc_done = sem("yt_full"), sem("sum_begun"), sem("acc_done")
        ln_var, ln_ln, ln_r0, chat = sem("ln2_var"), sem("ln2_ln"), sem("ln2_r0"), sem("chat")
        silu_done, out_ready = sem("silu2_done"), sem("out_ready")
        own_front, own_delta, own_tail = sem("front_dve"), sem("delta_dve"), sem("tail_dve")

        y_bank = bank[0:4]
        S_O, S_NORM, S_CT, S_F, S_OUT, EVERY = 2, 3, 4, 6, 7, 3
        S_DELTA1 = {1: 4, 4: 5, 7: 6, 10: 7}
        S_Z0, S_Z1 = {3: (0, 1), 13: (2, 3)}, {0: (4,), 1: (5, 6), 2: (7,)}
        S_XR, S_XD = {3: (0,), 4: (1, 2), 5: (3, 4), 6: (5, 6), 7: (7,)}, 9
        S_SILU_U = {7: (0, 1, 2, 3), 9: (4, 5, 6, 7)}
        S_DELTA0 = {10: 0, 11: 1, 12: 2, 13: 3}
        FRONT = range(min(S_XR), max(S_DELTA0) + 2)

        def s_out(t):
            return min(S_OUT + EVERY * t, N - 1)

        fv = Ring(bank[4:6], sem("fv_full"), {"act": sem("fv_act"), "dve": sem("fv_dve")},
                  [(f"xr{c}", "act") for c in range(IC)] + [("xd", "dve")] + [(f"dt{c}", "act") for c in range(4)] + [("C", "dve")]
                  + [(k, "act") for k in ("dt4", "z0", "z1", "dt5", "dt6", "dt7", "z2", "z3", "z4", "z5", "z6", "z7")])
        ta = Ring(bank[6:8], sem("ta_full"), {"act": sem("ta_act"), "dve": sem("ta_dve")},
                  [("o0", "dve"), ("c0a", "act"), ("c0b", "act"), ("o1", "dve"), ("f0", "dve"), ("c1a", "act"), ("c1b", "act"),
                   ("o2", "dve"), ("f1", "dve"), ("c2a", "act"), ("c2b", "act"), ("o3", "dve"), ("f2", "dve"), ("c3a", "act"),
                   ("c3b", "act"), ("f3", "dve")])

        def first(j):
            return isinstance(j, int) and j == 0

        with nc.Block() as block:

            @block.sync
            def _(sp):
                def load_xm(n):
                    sp.dma_start(XM[:], xm_d[n]).then_inc(xm_in, 16)

                def store_b(n):
                    sp.wait_ge(*fv.done(n, "xd"))
                    sp.dma_start(b_d[n], xdbl[RANK:RANK + N, :]).then_inc(b_out, 16)

                def load_row(j, b, n, new_batch):
                    used = None if first(j) and n < 2 else sp.to_reg(j * UNITS + 2 * n - 2)
                    if new_batch:
                        stored = sp.to_reg((b + 1) * 16)
                        sp.wait_ge(b_out, stored)
                    if used is not None:
                        sp.wait_ge(dbu_done, used)
                    sp.dma_start(brep[:, n % 2, :], b_d[b, n:n + 1, :].to_broadcast([P, T])).then_inc(brep_in[n % 2], 16)

                def load_attn(p, t):
                    sp.dma_start(comb[:, t % 2, D:2 * D], attn_d[p, t * P:(t + 1) * P, :]).then_inc(attn_in[t % 2], 16)

                def tail(p, g):
                    if g == 0:
                        sp.wait_ge(out_ready, p * TT)
                        sp.dma_start(gate[:], gate_d[bass.ds(p, 1), :].to_broadcast([P, D])).then_inc(gate_in, 16)
                        for t in range(2):
                            load_attn(p, t)
                    for t in range(TT):
                        if g == S_CT + EVERY * t:
                            sp.wait_ge(ta.full, ta.at(p, f"c{t}b"))
                            sp.dma_start(comb[:, t % 2, D:2 * D], x1_d[p, t * P:(t + 1) * P, :]).then_inc(x1_in[t % 2], 16)
                    for t in range(TT):
                        if g == s_out(t):
                            sp.wait_ge(out_ready, p * TT + t + 1)
                            sp.dma_start(out[p, t * P:(t + 1) * P, :], comb[:, t % 2, 0:D]).then_inc(out_done[t % 2], 16)
                            if t + 2 < TT:
                                load_attn(p, t + 2)

                def half0(b, p):
                    for g in range(N):
                        load_row(b * 2 + (g + 2) // N, b, (g + 2) % N, False)
                        if p is not None:
                            tail(p, g)

                def half1(b, n):
                    for g in range(N):
                        if g + 2 < N:
                            load_row(b * 2 + 1, b, g + 2, False)
                        elif n is not None:
                            load_row(n * 2, n, g + 2 - N, True)
                        if n is not None and g == max(S_Z1):
                            sp.wait_ge(fv.full, fv.at(b, "z7"))
                            load_xm(n)
                        if n is not None and g == S_XD:
                            store_b(n)

                load_xm(0)
                sp.dma_start(w_x[:], a["L1_cond_W_x"].rearrange("(c p) n -> p c n", p=P)).then_inc(small_in, 16)
                sp.dma_start(w_dt[:], a["L1_cond_W_dt"]).then_inc(small_in, 16)
                store_b(0)
                for r in range(2):
                    load_row(0, 0, r, True)
                half0(0, None)
                with sp.Fori(0, B - 1) as b:
                    half1(b, b + 1)
                    half0(b + 1, b)
                half1(B - 1, None)
                for g in range(N):
                    tail(B - 1, g)
                for t in range(2):
                    sp.wait_ge(out_done[t], B * TT // 2 * 16)

            @block.gpsimd
            def _(pool):
                def half(j):
                    for n in range(N):
                        for s in range(2):
                            if n >= 2:
                                pool.wait_ge(yt_full, j * TURNED + (n - 1) * TT)
                            elif not first(j):
                                pool.wait_ge(yt_full, j * TURNED - HC - (1 - n) * TT)
                            if n == 0:
                                pool.wait_ge(du_done, j * HC + HC)
                            if s == 0:
                                pool.wait_ge(brep_in[n % 2], (j * (N // 2) + n // 2) * 16 + 16)
                            c = chunk(j, s)
                            nc.gpsimd.tensor_tensor(HS[:, n % 2, s * UC:(s + 1) * UC], DU[:, c:c + UC, :], brep[:, n % 2, :].unsqueeze(1).to_broadcast([P, UC, T]),
                                                    ALU.mult).then_inc(dbu_done, 1)

                def chunk(j, s):
                    return q * HC + s * UC

                q = 0
                half(0)
                with pool.Fori(0, B - 1) as b:
                    q = 1
                    half(b * 2 + 1)
                    q = 0
                    half(b * 2 + 2)
                q = 1
                half(2 * B - 1)

            @block.scalar
            def _(act):
                def decay(j, q, n):
                    if n == 0:
                        act.wait_ge(du_done, j * HC + HC)
                    for s in range(2):
                        if not (first(j) and n == 0):
                            act.wait_ge(scanned, j * UNITS + 2 * n + s - 1)
                        for i in range(UC):
                            c = q * HC + s * UC + i
                            last = nc.scalar.activation(dA[:, s, i, 1:T], delta[:, c, 1:T], ACT.Exp, scale=aneg[:, c, n:n + 1])
                        last.then_inc(dA_done, 1)

                def softplus(n, c):
                    act.wait_ge(fv.full, fv.at(n, f"dt{c}"))
                    act.wait_ge(du_done, n * IC + c)
                    x, b_dt = fv.bank(f"dt{c}"), col("L1_cond_b_dt", c)
                    nc.scalar.activation(e_abs[:], x[:], ACT.Abs, bias=b_dt).then_inc(sp_abs, 1)
                    halves = 2 * n - 1 if c < HC else 2 * n
                    if not first(n):
                        act.wait_ge(dA_done, halves * UNITS)
                    nc.scalar.activation(delta[:, c, :], x[:], ACT.Relu, bias=b_dt).then_inc(fv.emptied["act"], 1)
                    act.wait_ge(sp_abs, n * IC + c + 1)
                    nc.scalar.activation(e_abs[:], e_abs[:], ACT.Exp, scale=-1.0).then_inc(sp_exp, 1)
                    act.wait_ge(sp_exp, n * IC + c + 1)
                    if not first(n):
                        act.wait_ge(dbu_done, halves * UNITS)
                    nc.scalar.activation(DU[:, c, :], e_abs[:], ACT.Identity, bias=1.0).then_inc(sp_w, 1)
                    act.preload_act_table_set(LN_NEAR_1)
                    nc.scalar.activation(lnw[:], e_abs[:], ACT.Ln, bias=1.0).then_inc(sp_ln, 1)
                    act.preload_act_table_set(EXP_AND_LN)

                def set_sum(j, b):
                    act.wait_ge(*fv.done(b, "C"))
                    for t in range(TT):
                        act.wait_ge(yt_full, j * TURNED + t + 1)
                        nc.scalar.activation(acc[:, t, :], y_bank[t][:], ACT.Identity, scale=C[:, t, 0:1]).then_inc(sum_begun, 1)

                def silu_z(b, c):
                    if c < HC:
                        act.wait_ge(g_done, b * IC)
                    else:
                        act.wait_ge(g_done, b * IC + (c - HC + 1))
                    act.wait_ge(fv.full, fv.at(b, f"z{c}"))
                    nc.scalar.activation(ZS[:, c % HC, :], fv.bank(f"z{c}")[:], ACT.Silu).then_inc(fv.emptied["act"], 1)

                def front(n, g):
                    if g in S_SILU_U:
                        for c in S_SILU_U[g]:
                            act.wait_ge(conv_done, n * IC + c + 1)
                            nc.scalar.activation(U[:, c, :], U[:, c, :], ACT.Silu).then_inc(u_done, 1)
                        act.preload_act_table_set(EXP_AND_LN)
                    if g - 1 in S_XR:
                        for c in S_XR[g - 1]:
                            if c == 0 and not first(n):
                                act.wait_ge(du_done, n * IC)
                                act.wait_ge(acc_done, (n * 2 - 1) * ADDED)
                            if c == HC and not first(n):
                                act.wait_ge(ud_done, n * HC)
                            act.wait_ge(fv.full, fv.at(n, f"xr{c}"))
                            if c < HC and not first(n):
                                act.wait_ge(dbu_done, (2 * n - 1) * UNITS)
                            if c >= HC:
                                act.wait_ge(conv_done, n * IC + c - HC + 1)
                            nc.scalar.activation(U[:, c, :], fv.bank(f"xr{c}")[:], ACT.Identity, scale=convw[:, c, TAPS - 1:TAPS],
                                                 bias=col("L1_cond_b_conv", c)).then_inc(conv0, 1)
                            nc.scalar.activation(DU[:, c % HC, :], fv.bank(f"xr{c}")[:], ACT.Identity).then_inc(fv.emptied["act"], 1)
                    if g - 1 in S_DELTA0:
                        softplus(n, S_DELTA0[g - 1])

                def tail(p, g):
                    for t in range(TT):
                        if g == S_NORM + EVERY * t:
                            act.wait_ge(ln_var, p * TT + t + 1)
                            nc.scalar.activation(rt[:, t:t + 1], veps[:, t:t + 1], ACT.Ln).then_inc(ln_ln, 1)
                            act.wait_ge(ln_ln, p * TT + t + 1)
                            nc.scalar.activation(rs[:, t:t + 1], rt[:, t:t + 1], ACT.Exp, scale=-0.5).then_inc(ln_r0, 1)
                        if g == S_CT + 1 + EVERY * t:
                            for k in range(2):
                                use = f"c{t}{'ab'[k]}"
                                act.wait_ge(ta.full, ta.at(p, use))
                                for i in range(DC):
                                    c = k * DC + i
                                    last = nc.scalar.activation(G[:, c, t * P:(t + 1) * P], ta.bank(use)[:, i * P:(i + 1) * P], ACT.Identity,
                                                                scale=col("L1_cond_ln2_g", c), bias=col("L1_cond_ln2_b", c))
                                last.then_inc(ta.emptied["act"], 1)
                    for t in range(TT):
                        if g == s_out(t):
                            act.wait_ge(*ta.done(p, f"f{t}"))
                            nc.scalar.activation(comb[:, t % 2, 0:D], comb[:, t % 2, 0:D], ACT.Silu).then_inc(silu_done, 1)
                            if g - 1 not in S_Z0:
                                act.preload_act_table_set(EXP_AND_LN)

                def half0(b, p):
                    for g in range(N):
                        if g + 1 < N:
                            decay(b * 2, 0, g + 1)
                        else:
                            decay(b * 2 + 1, 1, 0)
                        if g == 0:
                            set_sum(b * 2, b)
                        if p is not None:
                            tail(p, g)
                        if g - 1 in S_DELTA1:
                            softplus(b, S_DELTA1[g - 1])
                        for c in S_Z0.get(g - 1, ()):
                            silu_z(b, c)
                        if g - 1 in S_Z0:
                            act.preload_act_table_set(EXP_AND_LN)

                def half1(b, n):
                    act.preload_act_table_set(EXP_AND_LN)
                    for g in range(N):
                        if g + 1 < N:
                            decay(b * 2 + 1, 1, g + 1)
                        elif n is not None:
                            decay(n * 2, 0, 0)
                        if g == 0:
                            set_sum(b * 2 + 1, b)
                            act.wait_ge(ta.full, b * len(ta.uses))
                            for c in range(HC, IC):
                                nc.scalar.activation(G[:, c, :], U[:, c, :], ACT.Identity, scale=col("L1_cond_D_param", c)).then_inc(ud_done, 1)
                        for c in S_Z1.get(g - 1, ()):
                            silu_z(b, c)
                        if g - 1 in S_Z1:
                            act.preload_act_table_set(EXP_AND_LN)
                        if n is not None:
                            front(n, g)

                load(act, "L1_cond_W_full").then_inc(arrived["L1_cond_W_full"], 16)
                act.dma_start(bias_full[:], a["L1_cond_b_full"].rearrange("(o n) -> o n", o=1).to_broadcast([P, D])).then_inc(bias_in, 16)
                for g in FRONT:
                    front(0, g)
                decay(0, 0, 0)
                half0(0, None)
                with act.Fori(0, B - 1) as b:
                    half1(b, b + 1)
                    half0(b + 1, b)
                half1(B - 1, None)
                for g in range(N):
                    tail(B - 1, g)

            @block.vector
            def _(dve):
                link_front = Link(dve, own_front, IC * (TAPS - 2))
                link_delta = Link(dve, own_delta, 3 * IC)
                link_tail = Link(dve, own_tail, 6 * TT)

                def scan(j, n, s):
                    u = j * UNITS + 2 * n + s
                    dve.wait_ge(dA_done, u + 1)
                    dve.wait_ge(dbu_done, u + 1)
                    h = HS[:, n % 2, s * UC:(s + 1) * UC].rearrange("p i t -> p (i t)")
                    nc.vector.tensor_tensor_scan(h, dA[:, s].rearrange("p i t -> p (i t)"), h, 0.0, ALU.mult, ALU.add).then_inc(scanned, 1)

                def add(j, n):
                    for t in range(TT):
                        dve.wait_ge(yt_full, j * TURNED + n * TT + t + 1)
                        nc.vector.scalar_tensor_tensor(out=acc[:, t, :], in0=y_bank[t][:], scalar=C[:, t, n:n + 1], in1=acc[:, t, :],
                                                       op0=ALU.mult, op1=ALU.add).then_inc(acc_done, 1)

                def total(j, b, q):
                    for i in range(HC):
                        dve.wait_ge(yt_full, j * TURNED + N * TT + i + 1)
                        if q == 0:
                            nc.vector.scalar_tensor_tensor(out=G[:, i, :], in0=U[:, i, :], scalar=col("L1_cond_D_param", i),
                                                           in1=y_bank[i][:], op0=ALU.mult, op1=ALU.add).then_inc(acc_done, 1)
                        else:
                            dve.wait_ge(ud_done, b * HC + i + 1)
                            nc.vector.tensor_tensor(G[:, HC + i, :], y_bank[i][:], G[:, HC + i, :], ALU.add).then_inc(acc_done, 1)

                def gated(j, b, q):
                    for i in range(HC):
                        c = q * HC + i
                        dve.wait_ge(acc_done, j * ADDED + (N - 1) * TT + i + 1)
                        dve.wait_ge(*fv.done(b, f"z{c}"))
                        nc.vector.tensor_tensor(G[:, c, :], G[:, c, :], ZS[:, i, :], ALU.mult).then_inc(g_done, 1)

                def finish_delta(n, c):
                    dve.wait_ge(sp_w, n * IC + c + 1)
                    link_delta(nc.vector.scalar_tensor_tensor(out=DU[:, c, :], in0=DU[:, c, :], scalar=1.0, in1=e_abs[:],
                                                              op0=ALU.subtract, op1=ALU.subtract))
                    dve.wait_ge(sp_ln, n * IC + c + 1)
                    link_delta(nc.vector.tensor_tensor(lnw[:], lnw[:], DU[:, c, :], ALU.subtract))
                    dve.wait_ge(*fv.done(n, f"dt{c}"))
                    link_delta(nc.vector.tensor_tensor(delta[:, c, :], lnw[:], delta[:, c, :], ALU.add))
                    nc.vector.tensor_tensor(DU[:, c, :], delta[:, c, :], U[:, c, :], ALU.mult).then_inc(du_done, 1)

                def front(n, g):
                    if g == min(S_XR):
                        link_front.begin(n)
                        link_delta.begin(n)
                    for c in S_XR.get(g - 1, ()):
                        dve.wait_ge(conv0, n * IC + c + 1)
                        dve.wait_ge(*fv.done(n, f"xr{c}"))
                        for k in range(TAPS - 1):
                            lag = TAPS - 1 - k
                            y = U[:, c, lag:T]
                            last = nc.vector.scalar_tensor_tensor(out=y, in0=DU[:, c % HC, 0:T - lag], scalar=convw[:, c, k:k + 1],
                                                                  in1=y, op0=ALU.mult, op1=ALU.add)
                            if k < TAPS - 2:
                                link_front(last)
                        last.then_inc(conv_done, 1)
                    if g == S_XD:
                        dve.wait_ge(fv.full, fv.at(n, "xd"))
                        dve.wait_ge(b_out, n * 16)
                        nc.vector.tensor_copy(xdbl[:], fv.bank("xd")[0:XD, :]).then_inc(fv.emptied["dve"], 1)
                    if g - 1 in S_DELTA0:
                        finish_delta(n, S_DELTA0[g - 1])

                def copy_C(b):
                    dve.wait_ge(fv.full, fv.at(b, "C"))
                    nc.vector.tensor_copy(C[:], fv.bank("C")[:, 0:TT * XD].rearrange("p (t x) -> p t x", x=XD)[:, :, RANK + N:XD]).then_inc(
                        fv.emptied["dve"], 1)
                    dve.wait_ge(*fv.done(b, "C"))

                def tail(p, g):
                    if g == 0:
                        link_tail.begin(p)
                        dve.wait_ge(gate_in, p * 16 + 16)
                    for t in range(TT):
                        tile = comb[:, t % 2, :]
                        if g == S_O + EVERY * t:
                            dve.wait_ge(attn_in[t % 2], (p * (TT // 2) + t // 2) * 16 + 16)
                            nc.vector.bn_stats(stats[:, t, 1, :], tile[:, D:2 * D])
                            dve.wait_ge(ta.full, ta.at(p, f"o{t}"))
                            dve.wait_ge(out_done[t % 2], (p * (TT // 2) + t // 2) * 16)
                            nc.vector.tensor_copy(tile[:, 0:D], ta.bank(f"o{t}")[:]).then_inc(ta.emptied["dve"], 1)
                            dve.wait_ge(*ta.done(p, f"o{t}"))
                            link_tail(nc.vector.bn_stats(stats[:, t, 0, :], tile[:, 0:D]))
                            nc.vector.memset(spare[:], 0.0)
                            link_tail(nc.vector.bn_aggr(mv[:, t, :], stats[:, t].rearrange("p s k -> p (s k)")))
                            nc.vector.tensor_scalar(veps[:, t:t + 1], mv[:, t, 1:2], EPS, None, ALU.add).then_inc(ln_var, 1)
                        if g == S_NORM + EVERY * t:
                            r, x, v = rs[:, t:t + 1], rt[:, t:t + 1], veps[:, t:t + 1]
                            dve.wait_ge(ln_r0, p * TT + t + 1)
                            link_tail(nc.vector.tensor_tensor(x, r, r, ALU.mult))
                            link_tail(nc.vector.scalar_tensor_tensor(out=x, in0=x, scalar=-0.5, in1=v, op0=ALU.mult, op1=ALU.mult))
                            link_tail(nc.vector.scalar_tensor_tensor(out=r, in0=x, scalar=1.5, in1=r, op0=ALU.add, op1=ALU.mult))
                            nc.vector.tensor_scalar(tile, tile, mv[:, t, 0:1], r, ALU.subtract, ALU.mult).then_inc(chat, 1)
                        if g == S_F + EVERY * t:
                            dve.wait_ge(ta.full, ta.at(p, f"f{t}"))
                            nc.vector.tensor_tensor(tile[:, 0:D], ta.bank(f"f{t}")[:], bias_full[:], ALU.add).then_inc(ta.emptied["dve"], 1)
                    for t in range(TT):
                        if g == s_out(t):
                            tile = comb[:, t % 2, :]
                            dve.wait_ge(silu_done, p * TT + t + 1)
                            link_tail(nc.vector.tensor_tensor(tile[:, 0:D], tile[:, 0:D], gate[:], ALU.mult))
                            dve.wait_ge(x1_in[t % 2], (p * (TT // 2) + t // 2) * 16 + 16)
                            nc.vector.tensor_tensor(tile[:, 0:D], tile[:, 0:D], tile[:, D:2 * D], ALU.add).then_inc(out_ready, 1)
                            if t == TT - 1:
                                link_tail.end()

                def half0(b, p):
                    if p is not None:
                        total(b * 2 - 1, p, 1)
                    copy_C(b)
                    for g in range(N):
                        for s in range(2):
                            if g + 1 < N:
                                scan(b * 2, g + 1, s)
                            else:
                                scan(b * 2 + 1, 0, s)
                        if g:
                            add(b * 2, g)
                        if g == min(S_DELTA1):
                            link_delta.begin(b, 3 * HC)
                        if g - 1 in S_DELTA1:
                            finish_delta(b, S_DELTA1[g - 1])
                        if p is not None:
                            if g == 0:
                                gated(b * 2 - 1, p, 1)
                            tail(p, g)
                    link_delta.end()

                def half1(b, n):
                    total(b * 2, b, 0)
                    for g in range(N):
                        for s in range(2):
                            if g + 1 < N:
                                scan(b * 2 + 1, g + 1, s)
                            elif n is not None:
                                scan(n * 2, 0, s)
                        if g:
                            add(b * 2 + 1, g)
                        if g == 0:
                            gated(b * 2, b, 0)
                        if n is not None:
                            front(n, g)

                for s in range(2):
                    nc.vector.memset(dA[:, s, :, 0:1], 0.0).then_inc(zeroed, 1)
                dve.wait_ge(zeroed, 2)
                dve.wait_ge(bias_in, 16)
                for g in FRONT:
                    front(0, g)
                for s in range(2):
                    scan(0, 0, s)
                half0(0, None)
                with dve.Fori(0, B - 1) as b:
                    half1(b, b + 1)
                    half0(b + 1, b)
                half1(B - 1, None)
                total(2 * B - 1, B - 1, 1)
                gated(2 * B - 1, B - 1, 1)
                for g in range(N):
                    tail(B - 1, g)

            @block.tensor
            def _(pe):
                def product(dst, lhs, rhs, chunks, of):
                    for c in chunks:
                        last = nc.tensor.matmul(dst, lhs(c), rhs(c), start=(c == 0), stop=(c == of - 1))
                    return last

                def turn(j, n):
                    pe.wait_ge(scanned, j * UNITS + 2 * n + 2)
                    for t in range(TT):
                        if n == 1:
                            pe.wait_ge(sum_begun, j * TT + t + 1)
                        elif n:
                            pe.wait_ge(acc_done, j * ADDED + (n - 2) * TT + t + 1)
                        elif not first(j):
                            pe.wait_ge(acc_done, j * ADDED - HC + t + 1)
                        for i in range(HC):
                            last = nc.tensor.transpose(y_bank[t][:, i * P:(i + 1) * P], HS[:, n % 2, i, t * P:(t + 1) * P], ident[:])
                        last.then_inc(yt_full, 1)

                def total(j):
                    pe.wait_ge(acc_done, j * ADDED + (N - 1) * TT)
                    for i in range(HC):
                        for t in range(TT):
                            last = nc.tensor.transpose(y_bank[i][:, t * P:(t + 1) * P], acc[:, t, i * P:(i + 1) * P], ident[:])
                        last.then_inc(yt_full, 1)

                def z(b, c):
                    fv.wait_free(pe, b, f"z{c}")
                    product(fv.bank(f"z{c}")[:], lambda k: w_io[:, k, DI + c * P:DI + (c + 1) * P], lambda k: XM[:, k, :],
                            range(DC), DC).then_inc(fv.full, 1)

                def dt(n, c):
                    fv.wait_free(pe, n, f"dt{c}")
                    nc.tensor.matmul(fv.bank(f"dt{c}")[:], w_dt[:, c * P:(c + 1) * P], xdbl[0:RANK, :], start=True, stop=True).then_inc(fv.full, 1)

                def turn_C(b):
                    fv.wait_free(pe, b, "C")
                    for t in range(TT):
                        last = nc.tensor.transpose(fv.bank("C")[:, t * XD:(t + 1) * XD], xdbl[:, t * P:(t + 1) * P], ident[0:XD, 0:XD])
                    last.then_inc(fv.full, 1)

                def front(n, g):
                    for c in S_XR.get(g, ()):
                        if c == 0:
                            pe.wait_ge(xm_in, n * 16 + 16)
                        fv.wait_free(pe, n, f"xr{c}")
                        product(fv.bank(f"xr{c}")[:], lambda k: w_io[:, k, c * P:(c + 1) * P], lambda k: XM[:, k, :],
                                range(DC), DC).then_inc(fv.full, 1)
                    if g == S_XD:
                        pe.wait_ge(u_done, (n + 1) * IC)
                        fv.wait_free(pe, n, "xd")
                        product(fv.bank("xd")[0:XD, :], lambda k: w_x[:, k, :], lambda k: U[:, k, :], range(IC), IC).then_inc(fv.full, 1)
                    if g in S_DELTA0:
                        if S_DELTA0[g] == 0:
                            pe.wait_ge(*fv.done(n, "xd"))
                        dt(n, S_DELTA0[g])

                def tail(p, g):
                    for t in range(TT):
                        if g == S_CT + EVERY * t:
                            pe.wait_ge(chat, p * TT + t + 1)
                            for k in range(2):
                                use = f"c{t}{'ab'[k]}"
                                ta.wait_free(pe, p, use)
                                for i in range(DC):
                                    c = k * DC + i
                                    last = nc.tensor.transpose(ta.bank(use)[:, i * P:(i + 1) * P], comb[:, t % 2, c * P:(c + 1) * P], ident[:])
                                last.then_inc(ta.full, 1)
                    for t in range(TT):
                        if g == S_O + EVERY * t:
                            if t == 0:
                                pe.wait_ge(g_done, (p + 1) * IC)
                            ta.wait_free(pe, p, f"o{t}")
                            product(ta.bank(f"o{t}")[:], lambda c: G[:, c, t * P:(t + 1) * P], lambda c: w_out[:, c, :],
                                    range(IC), IC).then_inc(ta.full, 1)
                        if g == S_F + EVERY * t:
                            ta.wait_free(pe, p, f"f{t}")
                            for k in range(2):
                                pe.wait_ge(*ta.done(p, f"c{t}{'ab'[k]}"))
                                last = product(ta.bank(f"f{t}")[:], lambda c: G[:, c, t * P:(t + 1) * P], lambda c: w_full[:, c, :],
                                               range(k * DC, (k + 1) * DC), 2 * DC)
                            last.then_inc(ta.full, 1)

                def half0(b, p):
                    turn_C(b)
                    if p is not None:
                        total(b * 2 - 1)
                    for g in range(N):
                        turn(b * 2, g)
                        if p is not None:
                            tail(p, g)
                        if g in S_DELTA1:
                            dt(b, S_DELTA1[g])
                        for c in S_Z0.get(g, ()):
                            z(b, c)

                def half1(b, n):
                    total(b * 2)
                    for g in range(N):
                        turn(b * 2 + 1, g)
                        for c in S_Z1.get(g, ()):
                            z(b, c)
                        if n is not None:
                            front(n, g)

                pe.wait_ge(arrived["L1_cond_W_in"], 16)
                pe.wait_ge(small_in, 2 * 16)
                for g in FRONT:
                    front(0, g)
                half0(0, None)
                for name in ("L1_cond_W_out", "L1_cond_W_full"):
                    pe.wait_ge(arrived[name], 16)
                with pe.Fori(0, B - 1) as b:
                    half1(b, b + 1)
                    half0(b + 1, b)
                half1(B - 1, None)
                total(2 * B - 1)
                for g in range(N):
                    tail(B - 1, g)


_INS = ["x", "cond_2048", "mask_BxS_ik0"] + ["L0_cond_" + k for k in (
    "norm_scale norm_bias Wq bq Wk bk Wv bv film_emb_W film_emb_b film_norm_scale film_norm_bias film_out_W film_out_b").split()] + [
    "L1_cond_" + k for k in ("ln1_g ln1_b Wqkv bqkv Wproj bproj W_ada b_ada W_in W_conv b_conv W_x W_dt b_dt A_log D_param W_out "
                             "ln2_g ln2_b W_full b_full").split()]


def kernel(**inputs):
    import numpy as _np
    import concourse.bacc as _bacc
    from concourse import mybir as _mybir
    from concourse.bass_utils import run_bass_kernel_spmd as _run

    nc = _bacc.Bacc("TRN2", target_bir_lowering=False, num_devices=1)
    arrays, aps = {}, {}
    for name in _INS:
        v = _np.ascontiguousarray(inputs[name])
        arrays[f"in_{name}"] = v
        aps[name] = nc.dram_tensor(f"in_{name}", v.shape, _mybir.dt.from_np(v.dtype), kind="ExternalInput").ap()
    out = nc.dram_tensor("out", (B, T, D), F32, kind="ExternalOutput").ap()
    build(nc, aps, out)
    r = _run(nc, [arrays], core_ids=[0])
    return r.results[0]["out"]
```
